# Optimizing a Trainium2 kernel written in Bass

```python
import numpy as np
import jax
import jax.numpy as jnp

def _softmax(x, axis=-1):
    return jax.nn.softmax(x, axis=axis)

def _gelu(x):
    return jax.nn.gelu(x, approximate=True)

def _silu(x):
    return jax.nn.silu(x)

def _sigmoid(x):
    return jax.nn.sigmoid(x)

def _layernorm(x, axis=-1, eps=1e-05):
    m = jnp.mean(x, axis=axis, keepdims=True)
    v = jnp.var(x, axis=axis, keepdims=True)
    return (x - m) / jnp.sqrt(v + eps)

def _scatter_add(tgt, idx, src, axis=0):
    return tgt.at[idx].add(src)

def _segment_sum(src, seg, n):
    return jax.ops.segment_sum(src, seg, n)
kernel_name = 'mk_adaln_d1_jaxref_r8_570c22'

def setup_inputs(seed: int=0):
    np.random.seed(seed)
    _w = jnp.asarray

    def _L0_attn_setup():
        import jax, jax.numpy as jnp
        import numpy as np
        HEADS = 16
        EPS = 1e-08

        def _attention(x, Wq, Wkv, Wo, heads=HEADS, causal=True, eps=EPS):
            B, N, D = x.shape
            dh = D // heads
            q = x @ Wq.T
            k, v = jnp.split(x @ Wkv.T, 2, axis=-1)

            def split_heads(t):
                return t.reshape(B, N, heads, dh).transpose(0, 2, 1, 3)
            q, k, v = map(split_heads, (q, k, v))
            q = q * dh ** (-0.5)
            sim = jnp.einsum('bhid,bhjd->bhij', q, k)
            mask_value = -jnp.finfo(sim.dtype).max
            if causal:
                causal_mask = jnp.triu(jnp.ones((N, N), dtype=bool), 1)
                sim = jnp.where(causal_mask, mask_value, sim)
            m = jax.lax.stop_gradient(jnp.max(sim, axis=-1, keepdims=True))
            e = jnp.exp(sim - m)
            num = jnp.einsum('bhij,bhjd->bhid', e, v)
            den = jnp.sum(e, axis=-1, keepdims=True) + eps
            out = num / den
            out = out.transpose(0, 2, 1, 3).reshape(B, N, D)
            return out @ Wo.T
        key = jax.random.key(seed)
        k0, k1, k2, k3 = jax.random.split(key, 4)
        B, N, D = (2, 256, 128)
        x = jax.random.normal(k0, (B, N, D), jnp.float32)
        Wq = jax.random.normal(k1, (D, D), jnp.float32) * 0.02
        Wkv = jax.random.normal(k2, (2 * D, D), jnp.float32) * 0.02
        Wo = jax.random.normal(k3, (D, D), jnp.float32) * 0.02
        return {'x': x, 'Wq': Wq, 'Wkv': Wkv, 'Wo': Wo}
    _L0_attn_in = _L0_attn_setup()

    def _L0_ffn_setup():
        import jax, jax.numpy as jnp
        import numpy as np
        DIM = 128
        DEPTH = 6
        HEADS = 16
        DIM_HEAD = 64
        WINDOW = 32
        INNER = HEADS * DIM_HEAD
        DIM_INNER = int(DIM * 4 * 2 / 3)
        QK_SCALE = 8.0

        def shift_tokens(t):
            a, s = jnp.split(t, 2, -1)
            s = jnp.pad(s, ((0, 0), (1, 0), (0, 0)))[:, :-1]
            return jnp.concatenate([a, s], -1)

        def l2norm(t):
            return t / jnp.maximum(jnp.linalg.norm(t, axis=-1, keepdims=True), 1e-12)

        def rotate_half(x):
            x1, x2 = jnp.split(x, 2, -1)
            return jnp.concatenate([-x2, x1], -1)

        def rotary_tables(n):
            half = jnp.arange(0, DIM_HEAD, 2, dtype=jnp.float32)
            inv_freq = 1.0 / 10000.0 ** (half / DIM_HEAD)
            t = jnp.arange(n, dtype=jnp.float32)
            freqs = t[:, None] * inv_freq[None, :]
            freqs = jnp.concatenate([freqs, freqs], -1)
            base_scale = (half + 0.4 * DIM_HEAD) / (1.4 * DIM_HEAD)
            power = (t - n // 2) / (WINDOW // 2)
            scale = base_scale[None, :] ** power[:, None]
            scale = jnp.concatenate([scale, scale], -1)
            return (freqs, scale)

        def local_attention(q, k, v):
            b, h, n, d = q.shape
            w = WINDOW
            nw = n // w
            bq = q.reshape(b, h, nw, w, d)
            bk = k.reshape(b, h, nw, w, d)
            bv = v.reshape(b, h, nw, w, d)

            def look(t):
                p = jnp.pad(t, ((0, 0), (0, 0), (1, 0), (0, 0), (0, 0)))
                return jnp.concatenate([p[:, :, :nw], p[:, :, 1:]], axis=3)
            bk2, bv2 = (look(bk), look(bv))
            seq = jnp.arange(n).reshape(nw, w)
            seq_p = jnp.pad(seq, ((1, 0), (0, 0)), constant_values=-1)
            jt = jnp.concatenate([seq_p[:nw], seq_p[1:]], axis=1)
            it = seq[:, :, None]
            jb = jt[:, None, :]
            mask = (it < jb) | (it > jb + w) | (jb == -1)
            sim = jnp.einsum('bhwie,bhwje->bhwij', bq, bk2) * QK_SCALE
            sim = jnp.where(mask, -jnp.finfo(sim.dtype).max, sim)
            attn = jax.nn.softmax(sim, -1)
            out = jnp.einsum('bhwij,bhwje->bhwie', attn, bv2)
            return out.reshape(b, h, n, d)

        def attn_layer(x, Wqkv, qs, ksc, Wo):
            b, n, _ = x.shape
            qkv = x @ Wqkv
            q, k, v = jnp.split(qkv, 3, -1)
            sh = lambda t: t.reshape(b, n, HEADS, DIM_HEAD).transpose(0, 2, 1, 3)
            q, k, v = (sh(q), sh(k), sh(v))
            q = l2norm(q) * qs
            k = l2norm(k) * ksc
            freqs, scale = rotary_tables(n)
            cos, sin = (jnp.cos(freqs), jnp.sin(freqs))
            q = q * cos * scale + rotate_half(q) * sin * scale
            inv = 1.0 / scale
            k = k * cos * inv + rotate_half(k) * sin * inv
            out = local_attention(q, k, v)
            out = out.transpose(0, 2, 1, 3).reshape(b, n, INNER)
            return out @ Wo

        def ffn_layer(x, g, bln, W1, b1, W2, b2):
            mu = x.mean(-1, keepdims=True)
            var = ((x - mu) ** 2).mean(-1, keepdims=True)
            xn = (x - mu) / jnp.sqrt(var + 1e-05) * g + bln
            hg = xn @ W1 + b1
            a, gate = jnp.split(hg, 2, -1)
            return a * jax.nn.gelu(gate, approximate=False) @ W2 + b2
        key = jax.random.key(seed)
        ks = jax.random.split(key, 8)
        B, N = (2, 256)
        init = lambda k, shape: jax.random.normal(k, shape, jnp.float32) * 0.02
        return {'x': jax.random.normal(ks[0], (B, N, DIM), jnp.float32), 'Wqkv': init(ks[1], (DEPTH, DIM, 3 * INNER)), 'q_scale': jnp.ones((DEPTH, DIM_HEAD), jnp.float32), 'k_scale': jnp.ones((DEPTH, DIM_HEAD), jnp.float32), 'Wo': init(ks[2], (DEPTH, INNER, DIM)), 'ln_g': jnp.ones((DEPTH, DIM), jnp.float32), 'ln_b': jnp.zeros((DEPTH, DIM), jnp.float32), 'W1': init(ks[3], (DEPTH, DIM, 2 * DIM_INNER)), 'b1': jnp.zeros((DEPTH, 2 * DIM_INNER), jnp.float32), 'W2': init(ks[4], (DEPTH, DIM_INNER, DIM)), 'b2': jnp.zeros((DEPTH, DIM), jnp.float32)}
    _L0_ffn_in = _L0_ffn_setup()
    _L0_c = _w((lambda *s: np.random.randn(*s).astype(np.float32) * 0.05)(8, 128))
    _L0_wmod = _w((lambda *s: np.random.randn(*s).astype(np.float32) * 0.05)(128, 6 * 128) * 128 ** (-0.5))
    _d = {'L0_attn_x': _L0_attn_in['x'], 'L0_attn_Wq': _L0_attn_in['Wq'], 'L0_attn_Wkv': _L0_attn_in['Wkv'], 'L0_attn_Wo': _L0_attn_in['Wo'], 'L0_ffn_Wqkv': _L0_ffn_in['Wqkv'], 'L0_ffn_q_scale': _L0_ffn_in['q_scale'], 'L0_ffn_k_scale': _L0_ffn_in['k_scale'], 'L0_ffn_Wo': _L0_ffn_in['Wo'], 'L0_ffn_ln_g': _L0_ffn_in['ln_g'], 'L0_ffn_ln_b': _L0_ffn_in['ln_b'], 'L0_ffn_W1': _L0_ffn_in['W1'], 'L0_ffn_b1': _L0_ffn_in['b1'], 'L0_ffn_W2': _L0_ffn_in['W2'], 'L0_ffn_b2': _L0_ffn_in['b2'], 'L0_c': _L0_c, 'L0_wmod': _L0_wmod}
    _x0 = _d['L0_attn_x']
    _d['L0_attn_x'] = jax.random.normal(jax.random.fold_in(jax.random.key(seed), 1), (8, 512, 128), dtype=_x0.dtype)
    del _x0
    return _d

def reference(L0_attn_x, L0_attn_Wq, L0_attn_Wkv, L0_attn_Wo, L0_ffn_Wqkv, L0_ffn_q_scale, L0_ffn_k_scale, L0_ffn_Wo, L0_ffn_ln_g, L0_ffn_ln_b, L0_ffn_W1, L0_ffn_b1, L0_ffn_W2, L0_ffn_b2, L0_c, L0_wmod):

    def _L0_attn_ref(x, Wq, Wkv, Wo):
        import jax, jax.numpy as jnp
        import numpy as np
        HEADS = 16
        EPS = 1e-08

        def _attention(x, Wq, Wkv, Wo, heads=HEADS, causal=True, eps=EPS):
            B, N, D = x.shape
            dh = D // heads
            q = x @ Wq.T
            k, v = jnp.split(x @ Wkv.T, 2, axis=-1)

            def split_heads(t):
                return t.reshape(B, N, heads, dh).transpose(0, 2, 1, 3)
            q, k, v = map(split_heads, (q, k, v))
            q = q * dh ** (-0.5)
            sim = jnp.einsum('bhid,bhjd->bhij', q, k)
            mask_value = -jnp.finfo(sim.dtype).max
            if causal:
                causal_mask = jnp.triu(jnp.ones((N, N), dtype=bool), 1)
                sim = jnp.where(causal_mask, mask_value, sim)
            m = jax.lax.stop_gradient(jnp.max(sim, axis=-1, keepdims=True))
            e = jnp.exp(sim - m)
            num = jnp.einsum('bhij,bhjd->bhid', e, v)
            den = jnp.sum(e, axis=-1, keepdims=True) + eps
            out = num / den
            out = out.transpose(0, 2, 1, 3).reshape(B, N, D)
            return out @ Wo.T
        return _attention(x, Wq, Wkv, Wo)

    def _L0_ffn_ref(x, Wqkv, q_scale, k_scale, Wo, ln_g, ln_b, W1, b1, W2, b2):
        import jax, jax.numpy as jnp
        import numpy as np
        DIM = 128
        DEPTH = 6
        HEADS = 16
        DIM_HEAD = 64
        WINDOW = 32
        INNER = HEADS * DIM_HEAD
        DIM_INNER = int(DIM * 4 * 2 / 3)
        QK_SCALE = 8.0

        def shift_tokens(t):
            a, s = jnp.split(t, 2, -1)
            s = jnp.pad(s, ((0, 0), (1, 0), (0, 0)))[:, :-1]
            return jnp.concatenate([a, s], -1)

        def l2norm(t):
            return t / jnp.maximum(jnp.linalg.norm(t, axis=-1, keepdims=True), 1e-12)

        def rotate_half(x):
            x1, x2 = jnp.split(x, 2, -1)
            return jnp.concatenate([-x2, x1], -1)

        def rotary_tables(n):
            half = jnp.arange(0, DIM_HEAD, 2, dtype=jnp.float32)
            inv_freq = 1.0 / 10000.0 ** (half / DIM_HEAD)
            t = jnp.arange(n, dtype=jnp.float32)
            freqs = t[:, None] * inv_freq[None, :]
            freqs = jnp.concatenate([freqs, freqs], -1)
            base_scale = (half + 0.4 * DIM_HEAD) / (1.4 * DIM_HEAD)
            power = (t - n // 2) / (WINDOW // 2)
            scale = base_scale[None, :] ** power[:, None]
            scale = jnp.concatenate([scale, scale], -1)
            return (freqs, scale)

        def local_attention(q, k, v):
            b, h, n, d = q.shape
            w = WINDOW
            nw = n // w
            bq = q.reshape(b, h, nw, w, d)
            bk = k.reshape(b, h, nw, w, d)
            bv = v.reshape(b, h, nw, w, d)

            def look(t):
                p = jnp.pad(t, ((0, 0), (0, 0), (1, 0), (0, 0), (0, 0)))
                return jnp.concatenate([p[:, :, :nw], p[:, :, 1:]], axis=3)
            bk2, bv2 = (look(bk), look(bv))
            seq = jnp.arange(n).reshape(nw, w)
            seq_p = jnp.pad(seq, ((1, 0), (0, 0)), constant_values=-1)
            jt = jnp.concatenate([seq_p[:nw], seq_p[1:]], axis=1)
            it = seq[:, :, None]
            jb = jt[:, None, :]
            mask = (it < jb) | (it > jb + w) | (jb == -1)
            sim = jnp.einsum('bhwie,bhwje->bhwij', bq, bk2) * QK_SCALE
            sim = jnp.where(mask, -jnp.finfo(sim.dtype).max, sim)
            attn = jax.nn.softmax(sim, -1)
            out = jnp.einsum('bhwij,bhwje->bhwie', attn, bv2)
            return out.reshape(b, h, n, d)

        def attn_layer(x, Wqkv, qs, ksc, Wo):
            b, n, _ = x.shape
            qkv = x @ Wqkv
            q, k, v = jnp.split(qkv, 3, -1)
            sh = lambda t: t.reshape(b, n, HEADS, DIM_HEAD).transpose(0, 2, 1, 3)
            q, k, v = (sh(q), sh(k), sh(v))
            q = l2norm(q) * qs
            k = l2norm(k) * ksc
            freqs, scale = rotary_tables(n)
            cos, sin = (jnp.cos(freqs), jnp.sin(freqs))
            q = q * cos * scale + rotate_half(q) * sin * scale
            inv = 1.0 / scale
            k = k * cos * inv + rotate_half(k) * sin * inv
            out = local_attention(q, k, v)
            out = out.transpose(0, 2, 1, 3).reshape(b, n, INNER)
            return out @ Wo

        def ffn_layer(x, g, bln, W1, b1, W2, b2):
            mu = x.mean(-1, keepdims=True)
            var = ((x - mu) ** 2).mean(-1, keepdims=True)
            xn = (x - mu) / jnp.sqrt(var + 1e-05) * g + bln
            hg = xn @ W1 + b1
            a, gate = jnp.split(hg, 2, -1)
            return a * jax.nn.gelu(gate, approximate=False) @ W2 + b2
        for i in range(DEPTH):
            x = attn_layer(shift_tokens(x), Wqkv[i], q_scale[i], k_scale[i], Wo[i]) + x
            x = ffn_layer(shift_tokens(x), ln_g[i], ln_b[i], W1[i], b1[i], W2[i], b2[i]) + x
        return x
    x = L0_attn_x
    mod = (_silu(L0_c) @ L0_wmod).reshape(L0_c.shape[0], 6, 1, -1)
    sa, ca, ga, sb, cb, gb = (mod[:, 0], mod[:, 1], mod[:, 2], mod[:, 3], mod[:, 4], mod[:, 5])
    ga = (2 * (ga >= 0) - 1) * jnp.maximum(jnp.abs(ga), 0.25)
    gb = (2 * (gb >= 0) - 1) * jnp.maximum(jnp.abs(gb), 0.25)
    h = _layernorm(x, axis=-1) * (1 + ca) + sa
    x = x + ga * _L0_attn_ref(h, L0_attn_Wq, L0_attn_Wkv, L0_attn_Wo)
    h = _layernorm(x, axis=-1) * (1 + cb) + sb
    x = x + gb * _L0_ffn_ref(h, L0_ffn_Wqkv, L0_ffn_q_scale, L0_ffn_k_scale, L0_ffn_Wo, L0_ffn_ln_g, L0_ffn_ln_b, L0_ffn_W1, L0_ffn_b1, L0_ffn_W2, L0_ffn_b2)
    return x

_drawn_inputs = setup_inputs


def setup_inputs(seed=0):
    import zlib

    import numpy as np

    out = dict(_drawn_inputs(seed))
    spreads = {'L0_ffn_q_scale': (1.0, 0.6),
     'L0_ffn_k_scale': (1.0, 0.6),
     'L0_ffn_ln_g': (1.0, 0.6),
     'L0_ffn_ln_b': (0.0, 0.8),
     'L0_ffn_b1': (0.0, 0.8),
     'L0_ffn_b2': (0.0, 0.649)}
    factors = {'L0_attn_Wq': 8.0,
     'L0_attn_Wkv': 8.0,
     'L0_attn_Wo': 8.0,
     'L0_ffn_W1': 7.418,
     'L0_ffn_W2': 7.286}
    for name, (base, spread) in spreads.items():
        noise = np.random.default_rng([zlib.crc32(name.encode()), seed]).standard_normal(out[name].shape)
        drawn = base * np.exp(spread * noise) if base else spread * noise
        out[name] = jnp.asarray(drawn.astype(out[name].dtype))
    for name, factor in factors.items():
        out[name] = (out[name] * factor).astype(out[name].dtype)
    return out
```

```python
from contextlib import ExitStack

import numpy as np

import concourse.bass as bass
from concourse import mybir

ALU = mybir.AluOpType
ACT = mybir.ActivationFunctionType
AX = mybir.AxisListType
F32 = mybir.dt.float32

P = 128
BATCH, N, DIM = 8, 512, 128
TILES = N // P
DEPTH, HEADS, DH, WIN = 6, 16, 64, 32
INNER = HEADS * DH
IC = INNER // P
WPT = P // WIN
HID = int(DIM * 4 * 2 / 3)
HC = -(-HID // P)
LN_EPS = 1e-5
NORM_FLOOR = 1e-24
SS_SCALE = 2.0 ** 24
RN_SHIFT = 12.0 * float(np.log(2.0))
EXP_LN_SET = "natural_log_exp_and_others"
MASKED = -3.0e38

C_IDENT, C_MEAN, C_MASK, C_CAUSAL = 0, P, 2 * P, 2 * P + 4 * WIN
C_ROT = C_CAUSAL + P
C_HEAD = C_ROT + TILES * 2 * 2 * DH
C_SHIFT = C_HEAD + HEADS
C_THREE = C_SHIFT + 1
C_END = C_THREE + 2 * HEADS


def shape_constants():
    c = np.zeros((P, C_END), np.float32)
    c[:, C_IDENT:C_IDENT + P] = np.eye(P, dtype=np.float32)
    c[:, C_MEAN:C_MEAN + P] = 1.0 / DIM
    i = np.arange(P)[:, None] % WIN
    j = np.arange(2 * WIN)[None, :]
    seen = np.where(j < WIN, j >= i, j - WIN <= i)
    first = seen & ((np.arange(P)[:, None] >= WIN) | (j >= WIN))
    c[:, C_MASK:C_MASK + 2 * WIN] = np.where(first, 0.0, MASKED)
    c[:, C_MASK + 2 * WIN:C_MASK + 4 * WIN] = np.where(seen, 0.0, MASKED)
    c[:, C_CAUSAL:C_CAUSAL + P] = np.where(np.arange(P)[None, :] <= np.arange(P)[:, None], 0.0, MASKED)
    half = np.arange(0, DH, 2, dtype=np.float32)
    inv_freq = (np.float32(1.0) / np.float32(10000.0) ** (half / np.float32(DH))).astype(np.float32)
    pos = np.arange(N, dtype=np.float32)
    freqs = (pos[:, None] * inv_freq[None, :]).astype(np.float64)
    base = ((half + np.float32(0.4 * DH)) / np.float32(1.4 * DH)).astype(np.float64)
    scale = base[None, :] ** ((pos.astype(np.float64)[:, None] - N // 2) / (WIN // 2))
    cos, sin = (np.concatenate([f(freqs)] * 2, -1) for f in (np.cos, np.sin))
    sin[:, :DH // 2] *= -1.0
    scale = np.concatenate([scale, scale], -1)
    tables = 0.5 * np.stack([np.concatenate([f * scale * 8.0, f / scale], -1) for f in (cos, sin)], 1)
    c[:, C_ROT:C_HEAD] = tables.reshape(TILES, P, 2 * 2 * DH).transpose(1, 0, 2).reshape(P, -1)
    c[:, C_SHIFT] = RN_SHIFT
    c[:, C_THREE:C_END] = 3.0
    c[:, C_HEAD:C_SHIFT] = np.arange(P)[:, None] // (P // HEADS) == np.arange(HEADS)[None, :]
    return c


def constant_views(consts):
    width = 2 * 2 * DH
    return {
        "ident": consts[:, C_IDENT:C_IDENT + P],
        "ones_mean": consts[:, C_MEAN:C_MEAN + P],
        "mask": [consts[:, C_MASK + i * 2 * WIN:C_MASK + (i + 1) * 2 * WIN] for i in range(2)],
        "causal": consts[:, C_CAUSAL:C_CAUSAL + P],
        "rot_base": [[consts[:, C_ROT + t * width + i * 2 * DH:C_ROT + t * width + (i + 1) * 2 * DH] for i in range(2)]
                     for t in range(TILES)],
        "head": consts[:, C_HEAD:C_SHIFT],
        "rn_shift": consts[:, C_SHIFT:C_SHIFT + 1],
        "three": consts[:, C_THREE:C_END],
    }


def local_stack(nc, w, LAYERS, const_sb, xT, x_done):
    NU = LAYERS * BATCH
    ident, ones_mean, mask, rot_base, rn_shift, three = (
        const_sb[k] for k in ("ident", "ones_mean", "mask", "rot_base", "rn_shift", "three"))

    def alive(u, d):
        return not isinstance(u, int) or 0 <= u + d < NU

    def tiles_done(u, d, t):
        return u * TILES + (TILES * d + t + 1)

    def units_done(u, d, per=1, index=0):
        return u * per + (per * d + index + 1)

    def batch_of(u, d):
        return (u + d) % BATCH if isinstance(u, int) else (u + (d % BATCH)) % BATCH

    def layer_of(u, d):
        return (u + d) // BATCH if isinstance(u, int) else (u + d) // BATCH

    def column(tensor, rows, layer, c=None):
        if isinstance(layer, int):
            return tensor[0:rows, layer:layer + 1] if c is None else tensor[0:rows, layer, c:c + 1]
        if c is None:
            return tensor[0:rows, bass.ds(layer, 1)]
        return tensor[0:rows, bass.ds(layer, 1), c:c + 1].rearrange("p a c -> p (a c)")

    def columns_of(b, t, shift=0, rows=slice(0, P), width=P):
        if isinstance(b, int):
            start = b * N + t * P - shift
            return xT[rows, start:start + width]
        return xT[rows, bass.ds(b * N + (t * P - shift), width)]

    with ExitStack() as ctx:
        def sb(name, shape):
            return ctx.enter_context(nc.sbuf_tensor("st_" + name, shape, F32))

        def sem(name):
            return ctx.enter_context(nc.semaphore("st_" + name))

        wqkv = sb("wqkv", [P, 2, 3 * INNER])
        wo = sb("wo", [P, IC, P])
        w1 = sb("w1", [P, 2 * HID])
        w2 = sb("w2", [P, HC, P])
        ln_g = sb("ln_g", [P, LAYERS])
        ln_b = sb("ln_b", [P, LAYERS])
        b1 = sb("b1", [P, LAYERS, 2 * HC])
        b2 = sb("b2", [P, LAYERS])
        qk_scale = sb("qk_scale", [P, 2, LAYERS, 2 * DH])
        rot = sb("rot", [P, TILES, 2, 2 * DH])
        xs = sb("xs", [P, N])
        qk_sq = sb("qk_sq", [P, 2 * INNER])
        qk_rot = sb("qk_rot", [P, 2 * INNER])
        ss = sb("ss", [P, 2, 2 * HEADS])
        rn = sb("rn", [P, 2, 2 * HEADS])
        nt = sb("nt", [P, 4, 2 * HEADS])
        v_tok = sb("v_tok", [P, 2, INNER])
        v_bd = sb("v_bd", [P, 2, WPT, 2, INNER // 2])
        qT = sb("qT", [P, 2, INNER])
        k_bd = sb("k_bd", [P, IC, 2, WIN + N])
        s = sb("s", [P, 2, INNER])
        mx = sb("mx", [P, 2, HEADS])
        den = sb("den", [P, 2, 2, HEADS])
        probT = sb("probT", [P, INNER])
        o = sb("o", [P, INNER])
        oT = sb("oT", [P, INNER])
        xs2 = sb("xs2", [P, N])
        xc = sb("xc", [P, N])
        xc2 = sb("xc2", [P, N])
        var = sb("var", [P, N])
        rstd = sb("rstd", [P, N])
        hid = sb("hid", [P, HC, N])

        ps_qk = ctx.enter_context(nc.psum_tensor("st_ps_qk", [P, 2 * INNER], F32))
        ps = ctx.enter_context(nc.psum_tensor("st_ps", [P, 2, INNER], F32))

        small_in, wqkv_in, wo_in, w12_in = sem("small_in"), sem("wqkv_in"), sem("wo_in"), sem("w12_in")
        vbd_in = [sem("vbd_in0"), sem("vbd_in1")]
        zeroed = sem("zeroed")
        KINDS = ("z", "v", "tq", "tk", "pt", "sim", "o", "m1", "m2", "h", "y", "ot")
        PER_UNIT = {k: {"m1": 1, "m2": 1, "h": HC, "y": 1}.get(k, TILES) for k in KINDS}
        qk_ready = sem("qk_ready")
        ready = {k: sem(k + "_ready") for k in KINDS}
        taken = {k: sem(k + "_taken") for k in KINDS}
        squared, rot_read, rot_done = sem("squared"), sem("rot_read"), sem("rot_done")
        xs_ready, ss_ready, rn_ready, normed = sem("xs_ready"), sem("ss_ready"), sem("rn_ready"), sem("normed")
        rot_table = sem("rot_table")
        max_ready, shifted, exp_ready, den_ready = sem("max_ready"), sem("shifted"), sem("exp_ready"), sem("den_ready")
        ff_copied, ff_squared, ff_rstd, ff_xn = sem("ff_copied"), sem("ff_squared"), sem("ff_rstd"), sem("ff_xn")
        gelu_ready = sem("gelu_ready")
        dve_zero, newton, ss_sum, cos_done = sem("dve_zero"), sem("newton"), sem("ss_sum"), sem("cos_done")
        pool_own, rn_final = sem("pool_own"), sem("rn_final")

        def jobs_of(t):
            def tile(kind, back):
                d, tt = divmod(t - back, TILES)
                return (kind, d, tt)

            feed = {3: [("m1", -1, 0)], 0: [("m2", -2, 0)], 1: [("h", -2, j) for j in range(HC)], 2: [("y", -2, 0)]}[t]
            return [tile("z", 3), tile("v", 0), tile("tq", 1), tile("tk", 1), tile("pt", 2), tile("sim", 1),
                    tile("o", 2), *feed, tile("ot", 2)]

        JOBS = [job for t in range(TILES) for job in jobs_of(t)]
        STARTS = [sum(len(jobs_of(i)) for i in range(t)) for t in range(TILES)]
        assert len(JOBS) % 2 == 0
        SLOT = {job: i % 2 for i, job in enumerate(JOBS)}

        def slot_of(kind, d, index):
            return ps[:, SLOT[(kind, d, index)], :]

        def half_free(eng, u, at):
            back = at - 2
            while True:
                over, i = divmod(back, len(JOBS))
                kind, d, index = JOBS[i]
                if isinstance(u, int) and u + over < 0:
                    return
                if alive(u, d + over):
                    eng.wait_ge(taken[kind], units_done(u, d + over, PER_UNIT[kind], index))
                    return
                back -= 2

        def loop(eng, unit):
            unit(0)
            unit(1)
            with eng.Fori(2, NU - 1) as u:
                unit(u)
            unit(NU - 1)
            unit(NU)
            unit(NU + 1)

        with nc.Block() as block:
            @block.sync
            def _(sp):
                for dst, src in ((ln_g, "ln_g"), (ln_b, "ln_b"), (b1[:, :, :].rearrange("p l c -> p (l c)"), "b1"), (b2, "b2")):
                    sp.dma_start(dst[:, :], w[src]).then_inc(small_in, 16)
                sp.dma_start(qk_scale[:, :, :, :].rearrange("p a l d -> p (a l d)"),
                             w["qk_scale"].partition_broadcast(P)).then_inc(small_in, 16)

                def load_wqkv(layer):
                    half = layer % 2
                    dst = wqkv[:, half, :] if isinstance(half, int) else wqkv[:, bass.ds(half, 1), :]
                    src = w["wqkv"][layer, :, :] if isinstance(layer, int) else w["wqkv"][bass.ds(layer, 1), :, :].rearrange("l p n -> p l n")
                    sp.dma_start(dst, src).then_inc(wqkv_in, 16)

                def one(name, layer):
                    return w[name][layer, :, :] if isinstance(layer, int) else w[name][bass.ds(layer, 1), :, :]

                def load_wo(layer):
                    src = one("wo", layer)
                    src = src.rearrange("(c p) n -> p c n", p=P) if isinstance(layer, int) else src.rearrange("l (c p) n -> p (l c) n", p=P)
                    sp.dma_start(wo[:, :, :], src).then_inc(wo_in, 16)

                def load_w12(layer):
                    a = one("w1", layer)
                    sp.dma_start(w1[:, :], a if isinstance(layer, int) else a.rearrange("l p n -> p (l n)")).then_inc(w12_in, 16)
                    b = one("w2", layer)
                    b = b if isinstance(layer, int) else b.rearrange("l p n -> (l p) n")
                    full = HID // P
                    sp.dma_start(w2[:, 0:full, :], b[0:full * P, :].rearrange("(c p) n -> p c n", p=P)).then_inc(w12_in, 16)
                    sp.dma_start(w2[0:HID - full * P, full, :], b[full * P:HID, :]).then_inc(w12_in, 16)

                def spread_v(u, t):
                    par = t % 2
                    sp.wait_ge(taken["v"], tiles_done(u, 0, t))
                    sp.wait_ge(ready["o"], tiles_done(u, 0, t))
                    for a in range(2):
                        rows = slice(a * 2 * WIN, (a + 1) * 2 * WIN)
                        cols = slice(a * INNER // 2, (a + 1) * INNER // 2)
                        for g in range(1, WPT):
                            sp.dma_start(v_bd[rows, par, g, a, :], v_tok[(g - 1) * WIN:(g + 1) * WIN, par, cols])\
                              .then_inc(vbd_in[par], 16)
                        sp.dma_start(v_bd[a * 2 * WIN + WIN:(a + 1) * 2 * WIN, par, 0, a, :], v_tok[0:WIN, par, cols])\
                          .then_inc(vbd_in[par], 16)
                        if t:
                            sp.dma_start(v_bd[a * 2 * WIN:a * 2 * WIN + WIN, par, 0, a, :],
                                         v_tok[P - WIN:P, 1 - par, cols]).then_inc(vbd_in[par], 16)

                def unit(u, layer=None, what=None):
                    for t in range(TILES):
                        if what == "wo" and t == 2:
                            sp.wait_ge(ready["z"], tiles_done(u, -1, TILES - 1))
                            sp.wait_ge(small_in, 80)
                            load_wo(layer)
                        if what == "w12" and t == 3:
                            sp.wait_ge(ready["y"], units_done(u, -2))
                            sp.wait_ge(small_in, 80)
                            load_w12(layer)
                        spread_v(u, t)

                def layer_loads(layer, first):
                    u0 = layer * BATCH
                    if not isinstance(layer, int) or layer + 1 < LAYERS:
                        if not first:
                            sp.wait_ge(ready["v"], u0 * TILES)
                        sp.wait_ge(wqkv_in, 16 * layer + 16)
                        sp.wait_ge(small_in, 80)
                        load_wqkv(layer + 1)
                    unit(u0, layer, None if first else "wo")
                    unit(u0 + 1, layer, None if first else "w12")
                    with sp.Fori(2, BATCH) as b:
                        unit(u0 + b)

                load_wqkv(0)
                load_wo(0)
                load_w12(0)
                layer_loads(0, True)
                if LAYERS > 2:
                    with sp.Fori(1, LAYERS - 1) as layer:
                        layer_loads(layer, False)
                layer_loads(LAYERS - 1, False)

            @block.tensor
            def _(pe):
                pe.wait_ge(zeroed, 2)
                pe.sem_inc(ready["o"], 2)

                def unit(u):
                    for t in range(TILES):
                        at = STARTS[t]
                        if alive(u, 0):
                            pe.wait_ge(xs_ready, tiles_done(u, 0, t))
                            if t == 0:
                                pe.wait_ge(wqkv_in, layer_of(u, 0) * 16 + 16)
                            if not (isinstance(u, int) and u * TILES + t == 0):
                                pe.wait_ge(squared, tiles_done(u, 0, t) - 1)
                                pe.wait_ge(rot_read, tiles_done(u, 0, t) - 1)
                            half = layer_of(u, 0) % 2
                            for c in range(2 * INNER // 512):
                                rhs = wqkv[:, half, c * 512:(c + 1) * 512] if isinstance(u, int) \
                                    else wqkv[:, bass.ds(half, 1), c * 512:(c + 1) * 512].rearrange("p a n -> p (a n)")
                                last = pe.matmul(ps_qk[:, c * 512:(c + 1) * 512], xs[:, t * P:(t + 1) * P], rhs,
                                                 start=True, stop=True)
                            last.then_inc(qk_ready, 1)
                        for i, (kind, d, index) in enumerate(jobs_of(t)):
                            if not alive(u, d):
                                continue
                            half_free(pe, u, at + i)
                            out = slot_of(kind, d, index)
                            par = index % 2
                            if kind == "z":
                                pe.wait_ge(taken["ot"], tiles_done(u, d, index))
                                pe.wait_ge(wo_in, layer_of(u, d) * 16 + 16)
                                for c in range(IC):
                                    last = pe.matmul(out[:, 0:P], wo[:, c, :], oT[:, c * P:(c + 1) * P],
                                                     start=(c == 0), stop=(c == IC - 1))
                            elif kind == "v":
                                half = layer_of(u, 0) % 2
                                for a in range(2):
                                    cols = slice(2 * INNER, 3 * INNER)
                                    rhs = wqkv[:, half, cols] if isinstance(u, int) \
                                        else wqkv[:, bass.ds(half, 1), cols].rearrange("p a n -> p (a n)")
                                    rhs = rhs.rearrange("p (h a d) -> p a h d", a=2, d=DH)[:, a, :, :]
                                    last = pe.matmul(out[:, a * 512:(a + 1) * 512], xs[:, index * P:(index + 1) * P],
                                                     rhs, start=True, stop=True)
                            elif kind in ("tq", "tk"):
                                pe.wait_ge(normed, tiles_done(u, d, index))
                                src = qk_rot[:, (kind == "tk") * INNER:(1 + (kind == "tk")) * INNER]
                                for c in range(IC):
                                    last = pe.transpose(out[:, c * P:(c + 1) * P], src[:, c * P:(c + 1) * P], ident)
                            elif kind == "pt":
                                pe.wait_ge(exp_ready, tiles_done(u, d, index))
                                for c in range(IC):
                                    last = pe.transpose(out[:, c * P:(c + 1) * P], s[:, par, c * P:(c + 1) * P], ident)
                            elif kind == "sim":
                                pe.wait_ge(taken["tk"], tiles_done(u, d, index))
                                pe.wait_ge(taken["tq"], tiles_done(u, d, index))
                                for c in range(IC):
                                    for g in range(WPT):
                                        key = index * P + g * WIN
                                        last = pe.matmul(
                                            out[g * WIN:(g + 1) * WIN, c * P:(c + 1) * P],
                                            qT[:, par, c * P + g * WIN:c * P + (g + 1) * WIN],
                                            k_bd[:, c, :, key:key + 2 * WIN], start=True, stop=True)
                            elif kind == "o":
                                pe.wait_ge(taken["pt"], tiles_done(u, d, index))
                                pe.wait_ge(vbd_in[par], spread_count(u, d, index))
                                for c in range(IC):
                                    for g in range(WPT):
                                        last = pe.matmul(
                                            out[g * WIN:(g + 1) * WIN, c * P:(c + 1) * P],
                                            probT[:, c * P + g * WIN:c * P + (g + 1) * WIN],
                                            v_bd[:, par, g, :, c * DH:(c + 1) * DH], start=True, stop=True)
                            elif kind == "ot":
                                pe.wait_ge(taken["o"], tiles_done(u, d, index))
                                for c in range(IC):
                                    last = pe.transpose(out[:, c * P:(c + 1) * P], o[:, c * P:(c + 1) * P], ident)
                            elif kind == "m1":
                                pe.wait_ge(ff_copied, units_done(u, d))
                                last = pe.matmul(out[:, 0:N], ones_mean, xs2[:, :], start=True, stop=True)
                            elif kind == "m2":
                                pe.wait_ge(ff_squared, units_done(u, d))
                                last = pe.matmul(out[:, 0:N], ones_mean, xc2[:, :], start=True, stop=True)
                            elif kind == "h":
                                rows = min(P, HID - index * P)
                                if index == 0:
                                    pe.wait_ge(ff_xn, units_done(u, d))
                                    pe.wait_ge(w12_in, layer_of(u, d) * 48 + 48)
                                for a in range(2):
                                    last = pe.matmul(out[0:rows, a * 512:a * 512 + N],
                                                     w1[:, a * HID + index * P:a * HID + index * P + rows], xc[:, :],
                                                     start=True, stop=True)
                            elif kind == "y":
                                pe.wait_ge(taken["h"], units_done(u, d, HC, HC - 1))
                                for c in range(HC):
                                    rows = min(P, HID - c * P)
                                    last = pe.matmul(out[:, 0:N], w2[0:rows, c, :], hid[0:rows, c, :],
                                                     start=(c == 0), stop=(c == HC - 1))
                            last.then_inc(ready[kind], 1)

                def spread_count(u, d, t):
                    per = 16 * (18 if t % 2 == 0 else 20)
                    within = 16 * {0: 8, 1: 10, 2: 18, 3: 20}[t]
                    return u * per + (per * d + within)

                loop(pe, unit)

            @block.scalar
            def _(act):
                act.preload_act_table_set(EXP_LN_SET)
                act.wait_ge(small_in, 80)
                act.wait_ge(zeroed, 2)

                def unit(u):
                    for t in range(TILES):
                        n = tiles_done(u, 0, t)
                        start = isinstance(u, int)
                        if alive(u, 0):
                            par = t % 2
                            act.wait_ge(qk_ready, n)
                            if not (start and n < 2):
                                act.wait_ge(rot_done, n - 1)
                            act.activation(qk_sq[:, :], ps_qk[:, :], ACT.Square).then_inc(squared, 1)
                            act.wait_ge(ready["v"], n)
                            if not (start and n < 2):
                                d1, t1 = divmod(t - 1, TILES)
                                per = 16 * (18 if t1 % 2 == 0 else 20)
                                act.wait_ge(vbd_in[t1 % 2], u * per + (per * d1 + 16 * {0: 8, 1: 10, 2: 18, 3: 20}[t1]))
                            if not (start and n < 3):
                                per = 16 * (18 if par == 0 else 20)
                                d1, t1 = divmod(t - 2, TILES)
                                act.wait_ge(vbd_in[par], u * per + (per * d1 + 16 * {0: 8, 1: 10, 2: 18, 3: 20}[t1]))
                            act.activation(v_tok[:, par, :], slot_of("v", 0, t), ACT.Copy).then_inc(taken["v"], 1)
                        d, tt = divmod(t - 1, TILES)
                        if alive(u, d):
                            par = tt % 2
                            act.wait_ge(ready["tq"], n - 1)
                            if not (start and n < 4):
                                act.wait_ge(ready["sim"], n - 3)
                            act.activation(qT[:, par, :], slot_of("tq", d, tt), ACT.Copy).then_inc(taken["tq"], 1)
                            act.wait_ge(ready["tk"], n - 1)
                            src = slot_of("tk", d, tt).rearrange("p (c n) -> p c n", n=P)
                            for a in range(2):
                                rows = slice(a * DH, (a + 1) * DH)
                                last = act.activation(k_bd[rows, :, a, WIN + tt * P:WIN + (tt + 1) * P], src[rows, :, :], ACT.Copy)
                            last.then_inc(taken["tk"], 1)
                        d, tt = divmod(t - 2, TILES)
                        if alive(u, d):
                            act.wait_ge(ready["pt"], n - 2)
                            if not (start and n < 4):
                                act.wait_ge(ready["o"], n - 1)
                            act.activation(probT[:, :], slot_of("pt", d, tt), ACT.Copy).then_inc(taken["pt"], 1)
                        if alive(u, 0):
                            par = t % 2
                            act.wait_ge(ss_ready, n)
                            if not (start and n < 3):
                                act.wait_ge(normed, n - 2)
                            act.activation(rn[:, par, :], ss[:, par, :], ACT.Ln, scale=SS_SCALE).then_inc(rn_ready, 1)
                            act.wait_ge(rn_ready, 2 * n - 1)
                            act.activation(rn[:, par, :], rn[:, par, :], ACT.Exp, bias=rn_shift, scale=-0.5).then_inc(rn_ready, 1)
                        if t == 3 and alive(u, -1):
                            act.wait_ge(taken["m1"], units_done(u, -1))
                            if alive(u, -2):
                                act.wait_ge(ready["m2"], units_done(u, -2))
                            act.activation(xc2[:, :], xc[:, :], ACT.Square).then_inc(ff_squared, 1)
                        if t == 0 and alive(u, -2):
                            act.wait_ge(taken["m2"], units_done(u, -2))
                            if alive(u, -3):
                                act.wait_ge(ff_xn, units_done(u, -3))
                            act.activation(rstd[:, :], var[:, :], ACT.Ln).then_inc(ff_rstd, 1)
                            act.wait_ge(ff_rstd, units_done(u, -2, 2, 0))
                            act.activation(rstd[:, :], rstd[:, :], ACT.Exp, scale=-0.5).then_inc(ff_rstd, 1)
                        if t == 1 and alive(u, -2):
                            for j in range(HC):
                                rows = min(P, HID - j * P)
                                act.wait_ge(ready["h"], units_done(u, -2, HC, j))
                                if j == 0 and alive(u, -3):
                                    act.wait_ge(ready["y"], units_done(u, -3))
                                gate = slot_of("h", -2, j)[0:rows, 512:512 + N]
                                act.activation(hid[0:rows, j, :], gate, ACT.Gelu,
                                               bias=column(b1, rows, layer_of(u, -2), HC + j)).then_inc(gelu_ready, 1)
                            act.preload_act_table_set(EXP_LN_SET)
                        if alive(u, d):
                            act.wait_ge(ready["ot"], n - 2)
                            if not (start and n < 4):
                                act.wait_ge(ready["z"], n - 3)
                            act.activation(oT[:, :], slot_of("ot", d, tt), ACT.Copy).then_inc(taken["ot"], 1)
                        d, tt = divmod(t - 1, TILES)
                        if alive(u, d):
                            act.wait_ge(shifted, n - 1)
                            act.activation(s[:, tt % 2, :], s[:, tt % 2, :], ACT.Exp).then_inc(exp_ready, 1)

                loop(act, unit)

            @block.vector
            def _(dve):
                dve.memset(k_bd[:, :, :, :], 0.0).then_inc(zeroed, 1)
                dve.memset(v_bd[:, :, :, :, :], 0.0).then_inc(zeroed, 1)
                dve.memset(xs[DH:P, 0:1], 0.0).then_inc(dve_zero, 1)
                dve.memset(xs2[DH:P, 0:1], 0.0).then_inc(dve_zero, 1)
                dve.wait_ge(small_in, 80)
                dve.wait_ge(dve_zero, 2)

                def shift_tile(u, d, t):
                    if t == 0:
                        dve.wait_ge(x_done, units_done(u, d))
                    if alive(u, d - 1):
                        dve.wait_ge(ready["v"], tiles_done(u, d - 1, t))
                    b = batch_of(u, d)
                    dve.tensor_copy(xs[0:DH, t * P:(t + 1) * P], columns_of(b, t, 0, slice(0, DH)))
                    if t:
                        dve.tensor_copy(xs[DH:P, t * P:(t + 1) * P], columns_of(b, t, 1, slice(DH, P))).then_inc(xs_ready, 1)
                    else:
                        dve.tensor_copy(xs[DH:P, 1:P], columns_of(b, 0, 0, slice(DH, P), P - 1)).then_inc(xs_ready, 1)

                shift_tile(0, 0, 0)

                def unit(u):
                    start = isinstance(u, int)
                    for t in range(TILES):
                        n = tiles_done(u, 0, t)
                        d2, t2 = divmod(t - 2, TILES)
                        if alive(u, d2):
                            dve.wait_ge(exp_ready, n - 2)
                            dve.tensor_reduce(den[:, t2 % 2, 0, :], s[:, t2 % 2, :].rearrange("p (h k) -> p h k", h=HEADS),
                                              AX.X, ALU.add).then_inc(den_ready, 1)
                            dve.wait_ge(den_ready, 2 * (n - 2) - 1)
                            dve.reciprocal(den[:, t2 % 2, 1, :], den[:, t2 % 2, 0, :]).then_inc(den_ready, 1)
                        if t == 1 and alive(u, -2):
                            dve.wait_ge(ff_rstd, units_done(u, -2, 2, 1))
                            chain = units_done(u, -2, 4, 0)
                            dve.tensor_tensor(xc2[:, :], rstd[:, :], rstd[:, :], ALU.mult).then_inc(newton, 1)
                            dve.wait_ge(newton, chain)
                            dve.tensor_tensor(xc2[:, :], xc2[:, :], var[:, :], ALU.mult).then_inc(newton, 1)
                            dve.scalar_tensor_tensor(xc[:, :], xc[:, :], column(ln_g, P, layer_of(u, -2)), rstd[:, :],
                                                     ALU.mult, ALU.mult)
                            dve.wait_ge(newton, chain + 1)
                            dve.tensor_scalar(xc2[:, :], xc2[:, :], -0.5, 1.5, ALU.mult, ALU.add).then_inc(newton, 1)
                            dve.wait_ge(newton, chain + 2)
                            dve.tensor_tensor(xc[:, :], xc[:, :], xc2[:, :], ALU.mult).then_inc(newton, 1)
                            dve.wait_ge(newton, chain + 3)
                            dve.tensor_scalar(xc[:, :], xc[:, :], column(ln_b, P, layer_of(u, -2)), None,
                                              ALU.add).then_inc(ff_xn, 1)
                        dn, tn = divmod(t + 1, TILES)
                        if alive(u, dn):
                            shift_tile(u, dn, tn)
                        d3, t3 = divmod(t - 3, TILES)
                        if alive(u, d3):
                            dve.wait_ge(ready["z"], n - 3)
                            x = columns_of(batch_of(u, d3), t3)
                            dve.tensor_tensor(x, slot_of("z", d3, t3)[:, 0:P], x, ALU.add).then_inc(taken["z"], 1)
                        if t == 2 and alive(u, -1):
                            dve.wait_ge(taken["z"], tiles_done(u, -1, TILES - 1))
                            if alive(u, -2):
                                dve.wait_ge(ready["m1"], units_done(u, -2))
                            b = batch_of(u, -1)
                            dve.tensor_copy(xs2[0:DH, :], columns_of(b, 0, 0, slice(0, DH), N))
                            dve.tensor_copy(xs2[DH:P, 1:N], columns_of(b, 0, 0, slice(DH, P), N - 1)).then_inc(ff_copied, 1)
                        if alive(u, 0):
                            par = t % 2
                            dve.wait_ge(squared, n)
                            if not (start and n < 3):
                                dve.wait_ge(normed, n - 2)
                            dve.tensor_reduce(nt[:, 2 + par, :], qk_sq[:, :].rearrange("p (h d) -> p h d", d=DH),
                                              AX.X, ALU.add).then_inc(ss_sum, 1)
                            dve.wait_ge(ss_sum, n)
                            dve.tensor_scalar(ss[:, par, :], nt[:, 2 + par, :], NORM_FLOOR, None, ALU.max).then_inc(ss_ready, 1)
                            dve.wait_ge(qk_ready, n)
                            dve.wait_ge(rot_table, n)
                            if not (start and n < 2):
                                dve.wait_ge(ready["tk"], n - 1)
                            dve.tensor_tensor(
                                qk_rot[:, :].rearrange("p (a h d) -> p a h d", a=2, d=DH),
                                ps_qk[:, :].rearrange("p (a h d) -> p a h d", a=2, d=DH),
                                rot[:, t, 0, :].rearrange("p (a d) -> p a d", a=2).unsqueeze(2).to_broadcast([P, 2, HEADS, DH]),
                                ALU.mult).then_inc(cos_done, 1)
                            half_view = dict(a=2 * HEADS, g=2)
                            src = ps_qk[:, :].rearrange("p (a g d) -> p a g d", **half_view)
                            dst = qk_sq[:, :].rearrange("p (a g d) -> p a g d", **half_view)
                            for g in range(2):
                                table = rot[:, t, 1, :].rearrange("p (a g d) -> p a g d", a=2, g=2)[:, :, g, :]
                                last = dve.tensor_tensor(
                                    dst[:, :, g, :].rearrange("p (a h) d -> p a h d", a=2),
                                    src[:, :, 1 - g, :].rearrange("p (a h) d -> p a h d", a=2),
                                    table.unsqueeze(2).to_broadcast([P, 2, HEADS, DH // 2]), ALU.mult)
                            last.then_inc(rot_read, 1)
                            dve.wait_ge(cos_done, n)
                            dve.wait_ge(rot_read, n)
                            dve.tensor_tensor(qk_rot[:, :], qk_rot[:, :], qk_sq[:, :], ALU.add).then_inc(rot_done, 1)
                        d1, t1 = divmod(t - 1, TILES)
                        if alive(u, d1):
                            par = t1 % 2
                            dve.wait_ge(ready["sim"], n - 1)
                            if not (start and n < 4):
                                dve.wait_ge(ready["pt"], n - 3)
                            scores = s[:, par, :].rearrange("p (h k) -> p h k", h=HEADS)
                            dve.tensor_tensor(scores, slot_of("sim", d1, t1).rearrange("p (h k) -> p h k", h=HEADS),
                                              mask[0 if t1 == 0 else 1].unsqueeze(1).to_broadcast([P, HEADS, 2 * WIN]),
                                              ALU.add).then_inc(taken["sim"], 1)
                            dve.wait_ge(taken["sim"], n - 1)
                            dve.tensor_reduce(mx[:, par, :], scores, AX.X, ALU.max).then_inc(max_ready, 1)
                        if alive(u, d2):
                            dve.wait_ge(ready["o"], n)
                            dve.wait_ge(den_ready, 2 * (n - 2))
                            if not (start and n < 4):
                                dve.wait_ge(ready["ot"], n - 3)
                            dve.tensor_tensor(
                                o[:, :].rearrange("p (h d) -> p h d", h=HEADS),
                                slot_of("o", d2, t2).rearrange("p (h d) -> p h d", h=HEADS),
                                den[:, t2 % 2, 1, :].unsqueeze(2).to_broadcast([P, HEADS, DH]),
                                ALU.mult).then_inc(taken["o"], 1)
                        if t == 3 and alive(u, -1):
                            dve.wait_ge(ready["m1"], units_done(u, -1))
                            if alive(u, -2):
                                dve.wait_ge(ready["h"], units_done(u, -2, HC, HC - 1))
                            dve.tensor_tensor(xc[:, :], xs2[:, :], slot_of("m1", -1, 0)[:, 0:N],
                                              ALU.subtract).then_inc(taken["m1"], 1)
                        if t == 0 and alive(u, -2):
                            dve.wait_ge(ready["m2"], units_done(u, -2))
                            dve.tensor_scalar(var[:, :], slot_of("m2", -2, 0)[:, 0:N], LN_EPS, None,
                                              ALU.add).then_inc(taken["m2"], 1)
                        if t == 1 and alive(u, -2):
                            for j in range(HC):
                                rows = min(P, HID - j * P)
                                dve.wait_ge(gelu_ready, units_done(u, -2, HC, j))
                                dve.scalar_tensor_tensor(hid[0:rows, j, :], slot_of("h", -2, j)[0:rows, 0:N],
                                                         column(b1, rows, layer_of(u, -2), j), hid[0:rows, j, :],
                                                         ALU.add, ALU.mult).then_inc(taken["h"], 1)
                        if t == 2 and alive(u, -2):
                            dve.wait_ge(ready["y"], units_done(u, -2))
                            x = columns_of(batch_of(u, -2), 0, 0, slice(0, P), N)
                            dve.scalar_tensor_tensor(x, slot_of("y", -2, 0)[:, 0:N], column(b2, P, layer_of(u, -2)), x,
                                                     ALU.add, ALU.add).then_inc(taken["y"], 1)
                            dve.wait_ge(taken["y"], units_done(u, -2))
                            dve.sem_inc(x_done, 1)

                loop(dve, unit)

            @block.gpsimd
            def _(pool):
                pool.wait_ge(small_in, 80)

                def rot_tables(u, d, t):
                    layer = layer_of(u, d)
                    for part in range(2):
                        scale = qk_scale[:, part, layer, :] if isinstance(layer, int) \
                            else qk_scale[:, part, bass.ds(layer, 1), :].rearrange("p l d -> p (l d)")
                        last = pool.tensor_tensor(rot[:, t, part, :], rot_base[t][part], scale, ALU.mult)
                    last.then_inc(rot_table, 1)

                rot_tables(0, 0, 0)

                def unit(u):
                    start = isinstance(u, int)
                    for t in range(TILES):
                        n = tiles_done(u, 0, t)
                        if alive(u, 0):
                            par = t % 2
                            if not (start and n < 4):
                                pool.wait_ge(rot_read, n - 3)
                            pool.wait_ge(rn_ready, 2 * n)
                            r, q, a = rn[:, par, :], ss[:, par, :], nt[:, par, :]
                            chain = 3 * n - 3
                            pool.tensor_tensor(a, r, r, ALU.mult).then_inc(pool_own, 1)
                            pool.wait_ge(pool_own, chain + 1)
                            pool.tensor_tensor(a, a, q, ALU.mult).then_inc(pool_own, 1)
                            pool.wait_ge(pool_own, chain + 2)
                            pool.tensor_tensor(a, three, a, ALU.subtract).then_inc(pool_own, 1)
                            pool.wait_ge(pool_own, chain + 3)
                            pool.tensor_tensor(r, r, a, ALU.mult).then_inc(rn_final, 1)
                            pool.wait_ge(rn_final, n)
                            pool.wait_ge(rot_done, n)
                            view = qk_rot[:, :].rearrange("p (h d) -> p h d", d=DH)
                            pool.tensor_tensor(view, view, r.unsqueeze(2).to_broadcast([P, 2 * HEADS, DH]),
                                               ALU.mult).then_inc(normed, 1)
                        dn, tn = divmod(t + 1, TILES)
                        if alive(u, dn):
                            rot_tables(u, dn, tn)
                        d, tt = divmod(t - 1, TILES)
                        if alive(u, d):
                            pool.wait_ge(max_ready, n - 1)
                            scores = s[:, tt % 2, :].rearrange("p (h k) -> p h k", h=HEADS)
                            pool.tensor_tensor(scores, scores, mx[:, tt % 2, :].unsqueeze(2).to_broadcast([P, HEADS, 2 * WIN]),
                                               ALU.subtract).then_inc(shifted, 1)

                loop(pool, unit)
AH = 16
AD = DIM // AH
ATT_EPS = 1e-8
JOBS_HEAD = TILES
JOBS_BATCH = AH * TILES
HEADS_ROUND = 4
ROUNDS = AH // HEADS_ROUND
SCORE_BANKS = 3


def modulated_attention(nc, w, const_sb, mod, xT, x_done, x1_dram):
    ident, ones_mean, causal, head = (const_sb[k] for k in ("ident", "ones_mean", "causal", "head"))
    SA, CA, GA, SB, CB, GB = range(6)

    with ExitStack() as ctx:
        def sb(name, shape):
            return ctx.enter_context(nc.sbuf_tensor("at_" + name, shape, F32))

        def sem(name):
            return ctx.enter_context(nc.semaphore("at_" + name))

        def bank(name):
            return ctx.enter_context(nc.psum_tensor("at_" + name, [P, 512], F32))

        cT = sb("cT", [P, BATCH])
        silu = sb("silu", [P, 2, BATCH])
        sign = sb("sign", [P, BATCH])
        wmod = sb("wmod", [P, 6 * DIM])
        wq, wk, wv = sb("wq", [P, P]), sb("wk", [P, P]), sb("wv", [P, P])
        wo = sb("wo", [P, ROUNDS, P])
        x_tok = sb("x_tok", [P, TILES, P])
        xr = sb("xr", [P, N])
        x1 = sb("x1", [P, N])
        xc, sq, var, rstd, hT = (sb(k, [P, N]) for k in ("xc", "sq", "var", "rstd", "hT"))
        qT, kT = sb("qT", [P, N]), sb("kT", [P, N])
        qm = sb("qm", [P, 2, N])
        v_pad = sb("v_pad", [P, TILES, AH, 32])
        probs = sb("probs", [P, 2, TILES, N])
        probT = sb("probT", [P, 2, TILES, N])
        nmx = sb("nmx", [P, 2, TILES])
        den = sb("den", [P, 2, TILES])
        rden = sb("rden", [P, 2, 2, TILES])
        aT = sb("aT", [P, ROUNDS, N])

        ps_score = [bank(f"score{i}") for i in range(SCORE_BANKS)]
        ps_t = [bank(f"t{i}") for i in range(3)]
        ps_a = bank("a")
        ps_m = bank("m")
        PLACE = [(0, 0), (1, 0), (2, 0), (1, 384)]

        w_in, x_in, x1_out = sem("w_in"), sem("x_in"), sem("x1_out")
        exp_c, silu_ready, mod_ready, mod_taken, mod_done = (
            sem(k) for k in ("exp_c", "silu_ready", "mod_ready", "mod_taken", "mod_done"))
        zeroed, x_ready, xr_ready = sem("zeroed"), sem("x_ready"), sem("xr_ready")
        mean_ready, centred, squared, var_ready, var_taken, root, newton, h_ready = (
            sem(k) for k in ("mean_ready", "centred", "squared", "var_ready", "var_taken", "root", "newton", "h_ready"))
        proj_ready, proj_taken = sem("proj_ready"), sem("proj_taken")
        qm_ready, scores_ready, masked, max_ready, exp_ready = (
            sem(k) for k in ("qm_ready", "scores_ready", "masked", "max_ready", "exp_ready"))
        rden_own, weights_ready, t_ready, t_act, t_dve = (
            sem(k) for k in ("rden_own", "weights_ready", "t_ready", "t_act", "t_dve"))
        a_ready, a_taken, wo_ready, x1_ready = (sem(k) for k in ("a_ready", "a_taken", "wo_ready", "x1_ready"))

        with nc.Block() as block:
            @block.sync
            def _(sp):
                for dst, src in ((cT[:, :], w["cT"]), (wmod[:, :], w["wmod"]), (wq[:, :], w["wq"]), (wk[:, :], w["wk"]),
                                 (wv[:, :], w["wv"]), (wo[:, :, :], w["a_wo"])):
                    sp.dma_start(dst, src).then_inc(w_in, 16)
                sp.dma_start(x_tok[:, :, :], w["x"][0, :, :].rearrange("(t p) d -> p t d", p=P)).then_inc(x_in, 16)

                sp.sem_inc(x1_out, 16)

                def store(b):
                    sp.wait_ge(x1_ready, b + 1)
                    dst = x1_dram[:, b * N:(b + 1) * N] if isinstance(b, int) else x1_dram[:, bass.ds(b * N, N)]
                    sp.dma_start(dst, x1[:, :]).then_inc(x1_out, 16)

                with sp.Fori(0, BATCH - 1) as b:
                    sp.wait_ge(x_ready, b + 1)
                    sp.dma_start(x_tok[:, :, :], w["x"][bass.ds(b + 1, 1), :, :].rearrange("b (t p) d -> p (b t) d", p=P))\
                      .then_inc(x_in, 16)
                    store(b)
                store(BATCH - 1)
                sp.wait_ge(x1_out, 16 * BATCH + 16)

            @block.tensor
            def _(pe):
                pe.wait_ge(w_in, 96)
                pe.wait_ge(silu_ready, 1)
                for j in range(6):
                    last = pe.matmul(ps_m[:, j * BATCH:(j + 1) * BATCH], wmod[:, j * DIM:(j + 1) * DIM], silu[:, 1, :],
                                     start=True, stop=True)
                last.then_inc(mod_ready, 1)
                pe.wait_ge(mod_taken, 1)

                def layer_norm(b, k):
                    pe.matmul(ps_m[:, :], ones_mean, (xr if k == 0 else x1)[:, :], start=True, stop=True)\
                      .then_inc(mean_ready, 1)
                    pe.wait_ge(squared, 2 * b + (k + 1))
                    pe.matmul(ps_m[:, :], ones_mean, sq[:, :], start=True, stop=True).then_inc(var_ready, 1)

                def weigh(b, h):
                    pe.wait_ge(weights_ready, AH * b + (h + 1))
                    if h:
                        pe.wait_ge(t_act, AH * 2 * b + 2 * h)
                        pe.wait_ge(t_dve, AH * b + h)
                    for j in (0, 1, 3, 2):
                        at, col = PLACE[j]
                        for i in range(j, TILES):
                            last = pe.transpose(ps_t[at][:, col + (i - j) * P:col + (i - j + 1) * P],
                                                probs[:, h % 2, i, j * P:(j + 1) * P], ident)
                        if j in (0, 3, 2):
                            last.then_inc(t_ready, 1)
                    if h % HEADS_ROUND == 0 and h:
                        pe.wait_ge(a_taken, ROUNDS * b + h // HEADS_ROUND)
                    pe.wait_ge(t_act, AH * 2 * b + (2 * h + 2))
                    pe.wait_ge(t_dve, AH * b + (h + 1))
                    g = h % HEADS_ROUND
                    for j in range(TILES):
                        last = pe.matmul(ps_a[g * 32:(g + 1) * 32, j * P:N], v_pad[:, j, h, :],
                                         probT[:, h % 2, j, 0:N - j * P], start=(j == 0), stop=(j == TILES - 1))
                    last.then_inc(a_ready, 1)

                with pe.Fori(0, BATCH) as b:
                    pe.wait_ge(x_in, 16 * b + 16)
                    for t in range(TILES):
                        last = pe.transpose(ps_m[:, t * P:(t + 1) * P], x_tok[:, t, :], ident)
                    last.then_inc(x_ready, 1)
                    pe.wait_ge(xr_ready, b + 1)
                    layer_norm(b, 0)
                    pe.wait_ge(h_ready, 2 * b + 1)
                    pe.matmul(ps_score[0][:, :], wq[:, :], hT[:, :], start=True, stop=True).then_inc(proj_ready, 1)
                    pe.matmul(ps_score[1][:, :], wk[:, :], hT[:, :], start=True, stop=True).then_inc(proj_ready, 1)
                    for t in range(TILES):
                        last = pe.matmul(ps_score[2][:, t * P:(t + 1) * P], hT[:, t * P:(t + 1) * P], wv[:, :],
                                         start=True, stop=True)
                    last.then_inc(proj_ready, 1)
                    pe.wait_ge(proj_taken, 3 * b + 3)
                    for h in range(AH):
                        pe.wait_ge(qm_ready, AH * b + (h + 1))
                        for i in range(TILES):
                            k = h * TILES + i
                            if k >= SCORE_BANKS:
                                pe.wait_ge(exp_ready, JOBS_BATCH * b + (k - SCORE_BANKS + 1))
                            pe.matmul(ps_score[k % SCORE_BANKS][:, 0:(i + 1) * P], qm[:, h % 2, i * P:(i + 1) * P],
                                      kT[:, 0:(i + 1) * P], start=True, stop=True).then_inc(scores_ready, 1)
                        if h:
                            weigh(b, h - 1)
                    weigh(b, AH - 1)
                    pe.wait_ge(a_taken, ROUNDS * b + ROUNDS)
                    for r in range(ROUNDS):
                        last = pe.matmul(ps_m[:, :], wo[:, r, :], aT[:, r, :], start=(r == 0), stop=(r == ROUNDS - 1))
                    last.then_inc(wo_ready, 1)
                    pe.wait_ge(x1_ready, b + 1)
                    layer_norm(b, 1)
                    pe.wait_ge(var_taken, 2 * b + 2)

            @block.scalar
            def _(act):
                act.preload_act_table_set(EXP_LN_SET)
                act.wait_ge(w_in, 96)
                act.activation(silu[:, 0, :], cT[:, :], ACT.Exp, scale=-1.0).then_inc(exp_c, 1)

                def layer_norm(b, k):
                    act.wait_ge(centred, 2 * b + (k + 1))
                    act.activation(sq[:, :], xc[:, :], ACT.Square).then_inc(squared, 1)
                    act.wait_ge(var_taken, 2 * b + (k + 1))
                    act.activation(rstd[:, :], var[:, :], ACT.Ln).then_inc(root, 1)
                    act.wait_ge(root, 4 * b + (2 * k + 1))
                    act.activation(rstd[:, :], rstd[:, :], ACT.Exp, scale=-0.5).then_inc(root, 1)

                def take_transposed(b, h):
                    act.wait_ge(t_ready, 3 * AH * b + (3 * h + 1))
                    if h > 1:
                        act.wait_ge(a_ready, AH * b + (h - 1))
                    act.activation(probT[:, h % 2, 0, :], ps_t[0][:, :], ACT.Copy).then_inc(t_act, 1)
                    act.wait_ge(t_ready, 3 * AH * b + (3 * h + 3))
                    act.activation(probT[:, h % 2, 2, 0:2 * P], ps_t[2][:, 0:2 * P], ACT.Copy).then_inc(t_act, 1)

                with act.Fori(0, BATCH) as b:
                    layer_norm(b, 0)
                    act.wait_ge(proj_ready, 3 * b + 1)
                    act.activation(qT[:, :], ps_score[0][:, :], ACT.Copy, scale=float(AD) ** -0.5).then_inc(proj_taken, 1)
                    act.wait_ge(proj_ready, 3 * b + 2)
                    act.activation(kT[:, :], ps_score[1][:, :], ACT.Copy).then_inc(proj_taken, 1)
                    act.wait_ge(proj_ready, 3 * b + 3)
                    act.activation(v_pad[:, :, :, 0:AD].rearrange("p t h d -> p (t h) d"),
                                   ps_score[2][:, :].rearrange("p (a d) -> p a d", d=AD), ACT.Copy).then_inc(proj_taken, 1)
                    for h in range(AH):
                        for i in range(TILES):
                            k = h * TILES + i
                            act.wait_ge(max_ready, JOBS_BATCH * b + (k + 1))
                            if h > 1 and i == 0:
                                act.wait_ge(t_ready, 3 * AH * b + 3 * (h - 1))
                            act.activation(probs[:, h % 2, i, 0:(i + 1) * P], ps_score[k % SCORE_BANKS][:, 0:(i + 1) * P],
                                           ACT.Exp, bias=nmx[:, h % 2, i:i + 1],
                                           accum_out=den[:, h % 2, i:i + 1]).then_inc(exp_ready, 1)
                        if h:
                            take_transposed(b, h - 1)
                    take_transposed(b, AH - 1)
                    layer_norm(b, 1)

            @block.vector
            def _(dve):
                dve.memset(v_pad[:, :, :, :], 0.0).then_inc(zeroed, 1)
                dve.wait_ge(exp_c, 1)
                dve.tensor_scalar(silu[:, 0, :], silu[:, 0, :], 1.0, None, ALU.add).then_inc(zeroed, 1)
                dve.wait_ge(zeroed, 2)
                dve.reciprocal(silu[:, 0, :], silu[:, 0, :]).then_inc(zeroed, 1)
                dve.wait_ge(zeroed, 3)
                dve.tensor_tensor(silu[:, 1, :], cT[:, :], silu[:, 0, :], ALU.mult).then_inc(silu_ready, 1)
                dve.wait_ge(mod_ready, 1)
                dve.tensor_copy(mod[:, :, :].rearrange("p j b -> p (j b)"), ps_m[:, 0:6 * BATCH]).then_inc(mod_taken, 1)
                dve.wait_ge(mod_taken, 1)
                step = 0
                for j in (CA, CB):
                    dve.tensor_scalar(mod[:, j, :], mod[:, j, :], 1.0, None, ALU.add).then_inc(mod_done, 1)
                    step += 1
                for j in (GA, GB):
                    g = mod[:, j, :]
                    dve.wait_ge(mod_done, step)
                    dve.tensor_scalar(sign[:, :], g, 0.0, 2.0, ALU.is_ge, ALU.mult).then_inc(mod_done, 1)
                    dve.wait_ge(mod_done, step + 1)
                    dve.tensor_scalar(sign[:, :], sign[:, :], -1.0, None, ALU.add).then_inc(mod_done, 1)
                    dve.wait_ge(mod_done, step + 2)
                    dve.tensor_tensor(g, g, sign[:, :], ALU.mult).then_inc(mod_done, 1)
                    dve.wait_ge(mod_done, step + 3)
                    dve.scalar_tensor_tensor(g, g, 0.25, sign[:, :], ALU.max, ALU.mult).then_inc(mod_done, 1)
                    step += 4
                dve.wait_ge(mod_done, step)

                def modulation(b, j):
                    return mod[:, j, bass.ds(b, 1)]

                def layer_norm(b, k, src, shift, scale, dst):
                    dve.wait_ge(mean_ready, 2 * b + (k + 1))
                    dve.tensor_tensor(xc[:, :], src, ps_m[:, :], ALU.subtract).then_inc(centred, 1)
                    dve.wait_ge(var_ready, 2 * b + (k + 1))
                    dve.tensor_scalar(var[:, :], ps_m[:, :], LN_EPS, None, ALU.add).then_inc(var_taken, 1)
                    dve.wait_ge(root, 4 * b + (2 * k + 2))
                    chain = 10 * b + 5 * k
                    dve.tensor_tensor(sq[:, :], rstd[:, :], rstd[:, :], ALU.mult).then_inc(newton, 1)
                    dve.wait_ge(newton, chain + 1)
                    dve.tensor_tensor(sq[:, :], sq[:, :], var[:, :], ALU.mult).then_inc(newton, 1)
                    dve.scalar_tensor_tensor(xc[:, :], xc[:, :], modulation(b, scale), rstd[:, :], ALU.mult, ALU.mult)
                    dve.wait_ge(newton, chain + 2)
                    dve.tensor_scalar(sq[:, :], sq[:, :], -0.5, 1.5, ALU.mult, ALU.add).then_inc(newton, 1)
                    dve.wait_ge(newton, chain + 3)
                    dve.tensor_tensor(xc[:, :], xc[:, :], sq[:, :], ALU.mult).then_inc(newton, 1)
                    dve.wait_ge(newton, chain + 4)
                    dve.tensor_scalar(dst, xc[:, :], modulation(b, shift), None, ALU.add).then_inc(newton, 1)
                    dve.wait_ge(newton, chain + 5)

                def pick_head(b, h):
                    if h > 1:
                        dve.wait_ge(scores_ready, JOBS_BATCH * b + TILES * (h - 1))
                    dve.tensor_scalar(qm[:, h % 2, :], qT[:, :], head[:, h:h + 1], None, ALU.mult).then_inc(qm_ready, 1)

                def mask_and_max(b, h, i):
                    k = h * TILES + i
                    bank_k = ps_score[k % SCORE_BANKS]
                    dve.wait_ge(scores_ready, JOBS_BATCH * b + (k + 1))
                    diagonal = bank_k[:, i * P:(i + 1) * P]
                    dve.tensor_tensor(diagonal, diagonal, causal, ALU.add).then_inc(masked, 1)
                    dve.wait_ge(masked, JOBS_BATCH * b + (k + 1))
                    dve.tensor_reduce(nmx[:, h % 2, i:i + 1], bank_k[:, 0:(i + 1) * P], AX.X, ALU.max, negate=True)\
                       .then_inc(max_ready, 1)

                def normalise(b, h):
                    dve.wait_ge(exp_ready, JOBS_BATCH * b + TILES * (h + 1))
                    chain = 2 * AH * b + 2 * h
                    dve.tensor_scalar(rden[:, h % 2, 0, :], den[:, h % 2, :], ATT_EPS, None, ALU.add).then_inc(rden_own, 1)
                    dve.wait_ge(rden_own, chain + 1)
                    dve.reciprocal(rden[:, h % 2, 1, :], rden[:, h % 2, 0, :]).then_inc(rden_own, 1)
                    dve.wait_ge(rden_own, chain + 2)
                    for i in range(TILES):
                        row = probs[:, h % 2, i, 0:(i + 1) * P]
                        last = dve.tensor_scalar(row, row, rden[:, h % 2, 1, i:i + 1], None, ALU.mult)
                    last.then_inc(weights_ready, 1)

                def take_transposed(b, h):
                    dve.wait_ge(t_ready, 3 * AH * b + (3 * h + 2))
                    if h > 1:
                        dve.wait_ge(a_ready, AH * b + (h - 1))
                    dve.tensor_copy(probT[:, h % 2, 1, 0:3 * P], ps_t[1][:, 0:3 * P])
                    dve.tensor_copy(probT[:, h % 2, 3, 0:P], ps_t[1][:, 3 * P:4 * P]).then_inc(t_dve, 1)

                def take_round(b, r):
                    dve.wait_ge(a_ready, AH * b + HEADS_ROUND * (r + 1))
                    dve.tensor_copy(aT[:, r, :], ps_a[:, :]).then_inc(a_taken, 1)

                with dve.Fori(0, BATCH) as b:
                    dve.wait_ge(x_ready, b + 1)
                    dve.tensor_copy(xr[:, :], ps_m[:, :]).then_inc(xr_ready, 1)
                    dve.wait_ge(xr_ready, b + 1)
                    layer_norm(b, 0, xr[:, :], SA, CA, hT[:, :])
                    dve.sem_inc(h_ready, 1)
                    dve.wait_ge(proj_taken, 3 * b + 3)
                    pick_head(b, 0)
                    for h in range(AH):
                        if h + 1 < AH:
                            pick_head(b, h + 1)
                        mask_and_max(b, h, 0)
                        mask_and_max(b, h, 1)
                        if h:
                            normalise(b, h - 1)
                        mask_and_max(b, h, 2)
                        mask_and_max(b, h, 3)
                        if h:
                            take_transposed(b, h - 1)
                        if h and h % HEADS_ROUND == 0:
                            take_round(b, h // HEADS_ROUND - 1)
                    normalise(b, AH - 1)
                    take_transposed(b, AH - 1)
                    take_round(b, ROUNDS - 1)
                    dve.wait_ge(wo_ready, b + 1)
                    dve.wait_ge(x1_out, 16 * b + 16)
                    dve.scalar_tensor_tensor(x1[:, :], ps_m[:, :], modulation(b, GA), xr[:, :], ALU.mult, ALU.add)\
                       .then_inc(x1_ready, 1)
                    dve.wait_ge(x1_ready, b + 1)
                    layer_norm(b, 1, x1[:, :], SB, CB, xT[:, bass.ds(b * N, N)])
                    dve.sem_inc(h_ready, 1)
                    dve.sem_inc(x_done, 1)


def last_residual(nc, const_sb, mod, xT, x1_dram, out):
    ident = const_sb["ident"]
    GB = 5
    with ExitStack() as ctx:
        x1 = ctx.enter_context(nc.sbuf_tensor("lr_x1", [P, BATCH, N], F32))
        y = ctx.enter_context(nc.sbuf_tensor("lr_y", [P, BATCH, N], F32))
        y_tok = ctx.enter_context(nc.sbuf_tensor("lr_y_tok", [P, BATCH, N], F32))
        ps = [ctx.enter_context(nc.psum_tensor(f"lr_ps{i}", [P, N], F32)) for i in range(BATCH)]
        x1_in, y_ready, t_ready, t_taken, stored = (
            ctx.enter_context(nc.semaphore("lr_" + k)) for k in ("x1_in", "y_ready", "t_ready", "t_taken", "stored"))
        with nc.Block() as block:
            @block.sync
            def _(sp):
                sp.dma_start(x1[:, :, :].rearrange("p b n -> p (b n)"), x1_dram[:, :]).then_inc(x1_in, 16)
                for b in range(BATCH):
                    sp.wait_ge(t_taken, b + 1)
                    sp.dma_start(out[b, :, :].rearrange("(t p) d -> p t d", p=P),
                                 y_tok[:, b, :].rearrange("p (t d) -> p t d", d=DIM)).then_inc(stored, 16)
                sp.wait_ge(stored, 16 * BATCH)

            @block.vector
            def _(dve):
                dve.wait_ge(x1_in, 16)
                for b in range(BATCH):
                    dve.scalar_tensor_tensor(y[:, b, :], xT[:, b * N:(b + 1) * N], mod[:, GB, b:b + 1], x1[:, b, :],
                                             ALU.mult, ALU.add).then_inc(y_ready, 1)

            @block.tensor
            def _(pe):
                for b in range(BATCH):
                    pe.wait_ge(y_ready, b + 1)
                    for t in range(TILES):
                        last = pe.transpose(ps[b][:, t * P:(t + 1) * P], y[:, b, t * P:(t + 1) * P], ident)
                    last.then_inc(t_ready, 1)

            @block.scalar
            def _(act):
                for b in range(BATCH):
                    act.wait_ge(t_ready, b + 1)
                    act.activation(y_tok[:, b, :], ps[b][:, :], ACT.Copy).then_inc(t_taken, 1)


def adaln_block(nc, w, out):
    with ExitStack() as ctx:
        consts = ctx.enter_context(nc.sbuf_tensor("consts_sb", [P, C_END], F32))
        xT = ctx.enter_context(nc.sbuf_tensor("xT_sb", [P, BATCH * N], F32))
        mod = ctx.enter_context(nc.sbuf_tensor("mod_sb", [P, 6, BATCH], F32))
        x1_dram = nc.dram_tensor("x1_dims_first", [P, BATCH * N], F32, kind="Internal").ap()
        consts_in = ctx.enter_context(nc.semaphore("consts_in"))
        x_done = ctx.enter_context(nc.semaphore("x_done"))
        with nc.Block() as block:
            @block.sync
            def _(sp):
                sp.dma_start(consts[:, :], w["consts"]).then_inc(consts_in, 16)
                sp.wait_ge(consts_in, 16)
        const_sb = constant_views(consts)
        modulated_attention(nc, w, const_sb, mod, xT, x_done, x1_dram)
        local_stack(nc, w, DEPTH, const_sb, xT, x_done)
        last_residual(nc, const_sb, mod, xT, x1_dram, out)


def _layouts(inputs):
    a = {k: np.asarray(v) for k, v in inputs.items()}
    wkv = a["L0_attn_Wkv"]
    a_wo = np.zeros((P, ROUNDS, P), np.float32)
    rows = a["L0_attn_Wo"].T.reshape(ROUNDS, HEADS_ROUND, AD, DIM)
    for j in range(HEADS_ROUND):
        a_wo[j * 32:j * 32 + AD] = rows[:, j].transpose(1, 0, 2)
    b1 = np.zeros((P, DEPTH, 2 * HC), np.float32)
    for half in range(2):
        for j in range(HC):
            n = min(P, HID - j * P)
            b1[:n, :, half * HC + j] = a["L0_ffn_b1"][:, half * HID + j * P:half * HID + j * P + n].T
    q_scale, k_scale = a["L0_ffn_q_scale"], a["L0_ffn_k_scale"]
    swap = [np.concatenate([s[:, DH // 2:], s[:, :DH // 2]], 1) for s in (q_scale, k_scale)]
    qk_scale = np.stack([np.concatenate([q_scale, k_scale], 1), np.concatenate(swap, 1)]).reshape(-1)
    return {
        "consts": shape_constants(),
        "cT": a["L0_c"].T, "wmod": a["L0_wmod"], "x": a["L0_attn_x"],
        "wq": a["L0_attn_Wq"].T, "wk": wkv[:DIM].T, "wv": wkv[DIM:].T, "a_wo": a_wo,
        "wqkv": a["L0_ffn_Wqkv"], "wo": a["L0_ffn_Wo"], "w1": a["L0_ffn_W1"], "w2": a["L0_ffn_W2"],
        "ln_g": a["L0_ffn_ln_g"].T, "ln_b": a["L0_ffn_ln_b"].T, "b1": b1.reshape(P, -1), "b2": a["L0_ffn_b2"].T,
        "qk_scale": qk_scale,
    }


def kernel(**inputs):
    import concourse.bacc as bacc
    from concourse.bass_utils import run_bass_kernel_spmd

    nc = bacc.Bacc("TRN2", target_bir_lowering=False, num_devices=1)
    arrays, w = {}, {}
    for name, value in _layouts(inputs).items():
        value = np.ascontiguousarray(value)
        arrays["in_" + name] = value
        w[name] = nc.dram_tensor("in_" + name, value.shape, mybir.dt.from_np(value.dtype), kind="ExternalInput").ap()
    out = nc.dram_tensor("out_dram", (BATCH, N, DIM), F32, kind="ExternalOutput").ap()
    adaln_block(nc, w, out)
    result = run_bass_kernel_spmd(nc, [arrays], core_ids=[0])
    return np.asarray(result.results[0]["out_dram"])
```

```python
from contextlib import ExitStack

import numpy as np

import concourse.bass as bass
from concourse import mybir

ALU = mybir.AluOpType
ACT = mybir.ActivationFunctionType
AX = mybir.AxisListType
F32 = mybir.dt.float32

P = 128
BATCH, N, DIM = 8, 512, 128
TILES = N // P
DEPTH, HEADS, DH, WIN = 6, 16, 64, 32
INNER = HEADS * DH
IC = INNER // P
WPT = P // WIN
HID = int(DIM * 4 * 2 / 3)
HC = -(-HID // P)
NBANKS, BANK = 8, 512
H_BANKS = ((0, 1), (6, 7), (2, 3))
LN_EPS = 1e-5
NORM_FLOOR = 1e-24
SS_SCALE = 2.0 ** 24
RN_SHIFT = 12.0 * float(np.log(2.0))
EXP_LN_SET = "natural_log_exp_and_others"
MASKED = -3.0e38

C_IDENT, C_MEAN, C_MASK, C_CAUSAL = 0, P, 2 * P, 2 * P + 4 * WIN
C_ROT = C_CAUSAL + P
C_HEAD = C_ROT + TILES * 2 * 2 * DH
C_SHIFT = C_HEAD + HEADS
C_THREE = C_SHIFT + 1
C_END = C_THREE + 2 * HEADS


def shape_constants():
    c = np.zeros((P, C_END), np.float32)
    c[:, C_IDENT:C_IDENT + P] = np.eye(P, dtype=np.float32)
    c[:, C_MEAN:C_MEAN + P] = 1.0 / DIM
    i = np.arange(P)[:, None] % WIN
    j = np.arange(2 * WIN)[None, :]
    seen = np.where(j < WIN, j >= i, j - WIN <= i)
    first = seen & ((np.arange(P)[:, None] >= WIN) | (j >= WIN))
    c[:, C_MASK:C_MASK + 2 * WIN] = np.where(first, 0.0, MASKED)
    c[:, C_MASK + 2 * WIN:C_MASK + 4 * WIN] = np.where(seen, 0.0, MASKED)
    c[:, C_CAUSAL:C_CAUSAL + P] = np.where(np.arange(P)[None, :] <= np.arange(P)[:, None], 0.0, MASKED)
    half = np.arange(0, DH, 2, dtype=np.float32)
    inv_freq = (np.float32(1.0) / np.float32(10000.0) ** (half / np.float32(DH))).astype(np.float32)
    pos = np.arange(N, dtype=np.float32)
    freqs = (pos[:, None] * inv_freq[None, :]).astype(np.float64)
    base = ((half + np.float32(0.4 * DH)) / np.float32(1.4 * DH)).astype(np.float64)
    scale = base[None, :] ** ((pos.astype(np.float64)[:, None] - N // 2) / (WIN // 2))
    cos, sin = (np.concatenate([f(freqs)] * 2, -1) for f in (np.cos, np.sin))
    sin[:, :DH // 2] *= -1.0
    scale = np.concatenate([scale, scale], -1)
    tables = 0.5 * np.stack([np.concatenate([f * scale * 8.0, f / scale], -1) for f in (cos, sin)], 1)
    c[:, C_ROT:C_HEAD] = tables.reshape(TILES, P, 2 * 2 * DH).transpose(1, 0, 2).reshape(P, -1)
    c[:, C_SHIFT] = RN_SHIFT
    c[:, C_THREE:C_END] = 3.0
    c[:, C_HEAD:C_SHIFT] = np.arange(P)[:, None] // (P // HEADS) == np.arange(HEADS)[None, :]
    return c


def constant_views(consts):
    width = 2 * 2 * DH
    return {
        "ident": consts[:, C_IDENT:C_IDENT + P],
        "ones_mean": consts[:, C_MEAN:C_MEAN + P],
        "mask": [consts[:, C_MASK + i * 2 * WIN:C_MASK + (i + 1) * 2 * WIN] for i in range(2)],
        "causal": consts[:, C_CAUSAL:C_CAUSAL + P],
        "rot_base": [[consts[:, C_ROT + t * width + i * 2 * DH:C_ROT + t * width + (i + 1) * 2 * DH] for i in range(2)]
                     for t in range(TILES)],
        "head": consts[:, C_HEAD:C_SHIFT],
        "rn_shift": consts[:, C_SHIFT:C_SHIFT + 1],
        "three": consts[:, C_THREE:C_END],
    }


def local_stack(nc, w, LAYERS, const_sb, xT, x_done):
    NU = LAYERS * BATCH
    ident, ones_mean, mask, rot_base, rn_shift, three = (
        const_sb[k] for k in ("ident", "ones_mean", "mask", "rot_base", "rn_shift", "three"))

    def alive(u, d):
        return not isinstance(u, int) or 0 <= u + d < NU

    def tiles_done(u, d, t):
        return u * TILES + (TILES * d + t + 1)

    def units_done(u, d, per=1, index=0):
        return u * per + (per * d + index + 1)

    def batch_of(u, d):
        return (u + d) % BATCH if isinstance(u, int) else (u + (d % BATCH)) % BATCH

    def layer_of(u, d):
        return (u + d) // BATCH if isinstance(u, int) else (u + d) // BATCH

    def column(tensor, rows, layer, c=None):
        if isinstance(layer, int):
            return tensor[0:rows, layer:layer + 1] if c is None else tensor[0:rows, layer, c:c + 1]
        if c is None:
            return tensor[0:rows, bass.ds(layer, 1)]
        return tensor[0:rows, bass.ds(layer, 1), c:c + 1].rearrange("p a c -> p (a c)")

    def columns_of(b, t, shift=0, rows=slice(0, P), width=P):
        if isinstance(b, int):
            start = b * N + t * P - shift
            return xT[rows, start:start + width]
        return xT[rows, bass.ds(b * N + (t * P - shift), width)]

    def spread_count(u, d, t):
        per = 16 * (18 if t % 2 == 0 else 20)
        return u * per + (per * d + 16 * {0: 8, 1: 10, 2: 18, 3: 20}[t])

    def cols_of(a):
        return slice(a * INNER, (a + 1) * INNER)

    def heads_of(a):
        return slice(a * HEADS, (a + 1) * HEADS)

    with ExitStack() as ctx:
        def sb(name, shape):
            return ctx.enter_context(nc.sbuf_tensor("st_" + name, shape, F32))

        def sem(name):
            return ctx.enter_context(nc.semaphore("st_" + name))

        wqkv = sb("wqkv", [P, 2, 3 * INNER])
        wo = sb("wo", [P, IC, P])
        w1 = sb("w1", [P, 2 * HID])
        w2 = sb("w2", [P, HC, P])
        ln_g = sb("ln_g", [P, LAYERS])
        ln_b = sb("ln_b", [P, LAYERS])
        b1 = sb("b1", [P, LAYERS, 2 * HC])
        b2 = sb("b2", [P, LAYERS])
        qk_scale = sb("qk_scale", [P, 2, LAYERS, 2 * DH])
        rot = sb("rot", [P, TILES, 2, 2 * DH])
        xs = sb("xs", [P, N])
        qk_sq = sb("qk_sq", [P, 2 * INNER])
        qk_rot = sb("qk_rot", [P, 2 * INNER])
        ss = sb("ss", [P, 2, 2 * HEADS])
        rn = sb("rn", [P, 2, 2 * HEADS])
        nt = sb("nt", [P, 4, 2 * HEADS])
        v_tok = sb("v_tok", [P, 2, INNER])
        v_bd = sb("v_bd", [P, 2, WPT, 2, INNER // 2])
        qT = sb("qT", [P, 2, INNER])
        k_bd = sb("k_bd", [P, IC, 2, WIN + N])
        s = sb("s", [P, 2, INNER])
        mx = sb("mx", [P, 2, HEADS])
        den = sb("den", [P, 2, 2, HEADS])
        probT = sb("probT", [P, INNER])
        o = sb("o", [P, INNER])
        oT = sb("oT", [P, INNER])
        xs2 = sb("xs2", [P, N])
        xc = sb("xc", [P, N])
        xc2 = sb("xc2", [P, N])
        var = sb("var", [P, N])
        rstd = sb("rstd", [P, N])
        hid = sb("hid", [P, HC, N])

        ps = ctx.enter_context(nc.psum_tensor("st_ps", [P, NBANKS * BANK], F32))

        small_in, wqkv_in, wo_in, w12_in = sem("small_in"), sem("wqkv_in"), sem("wo_in"), sem("w12_in")
        vbd_in = [sem("vbd_in0"), sem("vbd_in1")]
        zeroed = sem("zeroed")
        KINDS = ("q", "k", "z", "v", "tq", "tk", "pt", "sim", "o", "m1", "m2", "h", "y", "ot")
        PER_UNIT = {k: {"m1": 1, "m2": 1, "h": HC, "y": 1}.get(k, TILES) for k in KINDS}
        ready = {k: sem(k + "_ready") for k in KINDS}
        qk_ready = [ready["q"], ready["k"]]
        taken = {k: sem(k + "_taken") for k in KINDS if k not in ("q", "k")}
        squared, rot_read, rot_done, ss_sum, ss_ready, rn_ready, rn_final, normed = (
            [sem(f"{k}_{a}") for a in "qk"] for k in
            ("squared", "rot_read", "rot_done", "ss_sum", "ss_ready", "rn_ready", "rn_final", "normed"))
        xs_ready = sem("xs_ready")
        rot_table = sem("rot_table")
        max_ready, shifted, exp_ready, den_ready = sem("max_ready"), sem("shifted"), sem("exp_ready"), sem("den_ready")
        ff_copied, ff_squared, ff_rstd, ff_xn = sem("ff_copied"), sem("ff_squared"), sem("ff_rstd"), sem("ff_xn")
        gelu_ready = sem("gelu_ready")
        dve_zero, newton, pool_own = sem("dve_zero"), sem("newton"), sem("pool_own")

        def jobs_of(t):
            def tile(kind, back, *banks):
                d, tt = divmod(t - back, TILES)
                return (kind, d, tt), banks

            feed = {3: [(("m1", -1, 0), (7,))], 0: [(("m2", -2, 0), (7,))], 1: [], 2: [(("y", -2, 0), (7,))]}[t]
            hidden = [(("h", -2, j), H_BANKS[j]) for j in range(HC)] if t == 1 else []
            return [tile("q", 0, 0, 1), tile("tq", 1, 2, 3), tile("k", 0, 4, 5), tile("tk", 1, 6, 7),
                    tile("v", 0, 2, 3), tile("ot", 3, 0, 1), tile("pt", 2, 6, 7), tile("sim", 1, 2, 3), *feed,
                    tile("z", 3, 6), tile("o", 2, 4, 5), *hidden]

        JOBS = [job for t in range(TILES) for job, _ in jobs_of(t)]
        BANKS = [banks for t in range(TILES) for _, banks in jobs_of(t)]
        STARTS = [sum(len(jobs_of(i)) for i in range(t)) for t in range(TILES)]
        FIRST_BANK = {job: banks[0] for job, banks in zip(JOBS, BANKS)}

        def slot_of(kind, d, index):
            first = FIRST_BANK[(kind, d, index)] * BANK
            return ps[:, first:min(first + INNER, NBANKS * BANK)]

        def slot_free(eng, u, at):
            held, back = set(BANKS[at]), at
            while held:
                back -= 1
                over, i = divmod(back, len(JOBS))
                if isinstance(u, int) and u + over < -1:
                    return
                kind, d, index = JOBS[i]
                if not held & set(BANKS[i]) or not alive(u, d + over):
                    continue
                held -= set(BANKS[i])
                count = units_done(u, d + over, PER_UNIT[kind], index)
                if kind in ("q", "k"):
                    eng.wait_ge(squared[kind == "k"], count)
                    eng.wait_ge(rot_read[kind == "k"], count)
                else:
                    eng.wait_ge(taken[kind], count)

        def loop(eng, unit):
            unit(0)
            unit(1)
            with eng.Fori(2, NU - 1) as u:
                unit(u)
            unit(NU - 1)
            unit(NU)
            unit(NU + 1)

        with nc.Block() as block:
            @block.sync
            def _(sp):
                for dst, src in ((ln_g, "ln_g"), (ln_b, "ln_b"), (b1[:, :, :].rearrange("p l c -> p (l c)"), "b1"), (b2, "b2")):
                    sp.dma_start(dst[:, :], w[src]).then_inc(small_in, 16)
                sp.dma_start(qk_scale[:, :, :, :].rearrange("p a l d -> p (a l d)"),
                             w["qk_scale"].partition_broadcast(P)).then_inc(small_in, 16)

                def load_wqkv(layer):
                    half = layer % 2
                    dst = wqkv[:, half, :] if isinstance(half, int) else wqkv[:, bass.ds(half, 1), :]
                    src = w["wqkv"][layer, :, :] if isinstance(layer, int) else w["wqkv"][bass.ds(layer, 1), :, :].rearrange("l p n -> p l n")
                    sp.dma_start(dst, src).then_inc(wqkv_in, 16)

                def one(name, layer):
                    return w[name][layer, :, :] if isinstance(layer, int) else w[name][bass.ds(layer, 1), :, :]

                def load_wo(layer):
                    src = one("wo", layer)
                    src = src.rearrange("(c p) n -> p c n", p=P) if isinstance(layer, int) else src.rearrange("l (c p) n -> p (l c) n", p=P)
                    sp.dma_start(wo[:, :, :], src).then_inc(wo_in, 16)

                def load_w12(layer):
                    a = one("w1", layer)
                    sp.dma_start(w1[:, :], a if isinstance(layer, int) else a.rearrange("l p n -> p (l n)")).then_inc(w12_in, 16)
                    b = one("w2", layer)
                    b = b if isinstance(layer, int) else b.rearrange("l p n -> (l p) n")
                    full = HID // P
                    sp.dma_start(w2[:, 0:full, :], b[0:full * P, :].rearrange("(c p) n -> p c n", p=P)).then_inc(w12_in, 16)
                    sp.dma_start(w2[0:HID - full * P, full, :], b[full * P:HID, :]).then_inc(w12_in, 16)

                def spread_v(u, t):
                    par = t % 2
                    sp.wait_ge(taken["v"], tiles_done(u, 0, t))
                    sp.wait_ge(ready["o"], tiles_done(u, 0, t))
                    for a in range(2):
                        rows = slice(a * 2 * WIN, (a + 1) * 2 * WIN)
                        cols = slice(a * INNER // 2, (a + 1) * INNER // 2)
                        for g in range(1, WPT):
                            sp.dma_start(v_bd[rows, par, g, a, :], v_tok[(g - 1) * WIN:(g + 1) * WIN, par, cols])\
                              .then_inc(vbd_in[par], 16)
                        sp.dma_start(v_bd[a * 2 * WIN + WIN:(a + 1) * 2 * WIN, par, 0, a, :], v_tok[0:WIN, par, cols])\
                          .then_inc(vbd_in[par], 16)
                        if t:
                            sp.dma_start(v_bd[a * 2 * WIN:a * 2 * WIN + WIN, par, 0, a, :],
                                         v_tok[P - WIN:P, 1 - par, cols]).then_inc(vbd_in[par], 16)

                def unit(u, layer=None, what=None):
                    for t in range(TILES):
                        if what == "wo" and t == 2:
                            sp.wait_ge(ready["z"], tiles_done(u, -1, TILES - 1))
                            sp.wait_ge(small_in, 80)
                            load_wo(layer)
                        if what == "w12" and t == 3:
                            sp.wait_ge(ready["y"], units_done(u, -2))
                            sp.wait_ge(small_in, 80)
                            load_w12(layer)
                        spread_v(u, t)

                def layer_loads(layer, first):
                    u0 = layer * BATCH
                    if not isinstance(layer, int) or layer + 1 < LAYERS:
                        if not first:
                            sp.wait_ge(ready["v"], u0 * TILES)
                        sp.wait_ge(wqkv_in, 16 * layer + 16)
                        sp.wait_ge(small_in, 80)
                        load_wqkv(layer + 1)
                    unit(u0, layer, None if first else "wo")
                    unit(u0 + 1, layer, None if first else "w12")
                    with sp.Fori(2, BATCH) as b:
                        unit(u0 + b)

                load_wqkv(0)
                load_wo(0)
                load_w12(0)
                layer_loads(0, True)
                if LAYERS > 2:
                    with sp.Fori(1, LAYERS - 1) as layer:
                        layer_loads(layer, False)
                layer_loads(LAYERS - 1, False)

            @block.tensor
            def _(pe):
                pe.wait_ge(zeroed, 2)
                pe.sem_inc(ready["o"], 2)

                def unit(u):
                    for t in range(TILES):
                        at = STARTS[t]

                        for i, ((kind, d, index), _) in enumerate(jobs_of(t)):
                            if not alive(u, d):
                                continue
                            slot_free(pe, u, at + i)
                            out = slot_of(kind, d, index)
                            par = index % 2
                            if kind in ("q", "k"):
                                if kind == "q":
                                    pe.wait_ge(xs_ready, tiles_done(u, 0, t))
                                    if t == 0:
                                        pe.wait_ge(wqkv_in, layer_of(u, 0) * 16 + 16)
                                half = layer_of(u, 0) % 2
                                for c in range(2):
                                    cols = slice((kind == "k") * INNER + c * 512, (kind == "k") * INNER + (c + 1) * 512)
                                    rhs = wqkv[:, half, cols] if isinstance(u, int) \
                                        else wqkv[:, bass.ds(half, 1), cols].rearrange("p a n -> p (a n)")
                                    last = pe.matmul(out[:, c * 512:(c + 1) * 512], xs[:, t * P:(t + 1) * P], rhs,
                                                     start=True, stop=True)
                            elif kind == "z":
                                pe.wait_ge(taken["ot"], tiles_done(u, d, index))
                                pe.wait_ge(wo_in, layer_of(u, d) * 16 + 16)
                                for c in range(IC):
                                    last = pe.matmul(out[:, 0:P], wo[:, c, :], oT[:, c * P:(c + 1) * P],
                                                     start=(c == 0), stop=(c == IC - 1))
                            elif kind == "v":
                                half = layer_of(u, 0) % 2
                                for a in range(2):
                                    cols = slice(2 * INNER, 3 * INNER)
                                    rhs = wqkv[:, half, cols] if isinstance(u, int) \
                                        else wqkv[:, bass.ds(half, 1), cols].rearrange("p a n -> p (a n)")
                                    rhs = rhs.rearrange("p (h a d) -> p a h d", a=2, d=DH)[:, a, :, :]
                                    last = pe.matmul(out[:, a * 512:(a + 1) * 512], xs[:, index * P:(index + 1) * P],
                                                     rhs, start=True, stop=True)
                            elif kind in ("tq", "tk"):
                                pe.wait_ge(normed[kind == "tk"], tiles_done(u, d, index))
                                src = qk_rot[:, (kind == "tk") * INNER:(1 + (kind == "tk")) * INNER]
                                for c in range(IC):
                                    last = pe.transpose(out[:, c * P:(c + 1) * P], src[:, c * P:(c + 1) * P], ident)
                            elif kind == "pt":
                                pe.wait_ge(exp_ready, tiles_done(u, d, index))
                                for c in range(IC):
                                    last = pe.transpose(out[:, c * P:(c + 1) * P], s[:, par, c * P:(c + 1) * P], ident)
                            elif kind == "sim":
                                pe.wait_ge(taken["tk"], tiles_done(u, d, index))
                                pe.wait_ge(taken["tq"], tiles_done(u, d, index))
                                for c in range(IC):
                                    for g in range(WPT):
                                        key = index * P + g * WIN
                                        last = pe.matmul(
                                            out[g * WIN:(g + 1) * WIN, c * P:(c + 1) * P],
                                            qT[:, par, c * P + g * WIN:c * P + (g + 1) * WIN],
                                            k_bd[:, c, :, key:key + 2 * WIN], start=True, stop=True)
                            elif kind == "o":
                                pe.wait_ge(taken["pt"], tiles_done(u, d, index))
                                pe.wait_ge(vbd_in[par], spread_count(u, d, index))
                                for c in range(IC):
                                    for g in range(WPT):
                                        last = pe.matmul(
                                            out[g * WIN:(g + 1) * WIN, c * P:(c + 1) * P],
                                            probT[:, c * P + g * WIN:c * P + (g + 1) * WIN],
                                            v_bd[:, par, g, :, c * DH:(c + 1) * DH], start=True, stop=True)
                            elif kind == "ot":
                                pe.wait_ge(taken["o"], tiles_done(u, d, index))
                                for c in range(IC):
                                    last = pe.transpose(out[:, c * P:(c + 1) * P], o[:, c * P:(c + 1) * P], ident)
                            elif kind == "m1":
                                pe.wait_ge(ff_copied, units_done(u, d))
                                last = pe.matmul(out[:, 0:N], ones_mean, xs2[:, :], start=True, stop=True)
                            elif kind == "m2":
                                pe.wait_ge(ff_squared, units_done(u, d))
                                last = pe.matmul(out[:, 0:N], ones_mean, xc2[:, :], start=True, stop=True)
                            elif kind == "h":
                                rows = min(P, HID - index * P)
                                if index == 0:
                                    pe.wait_ge(ff_xn, units_done(u, d))
                                    pe.wait_ge(w12_in, layer_of(u, d) * 48 + 48)
                                for a in range(2):
                                    last = pe.matmul(out[0:rows, a * 512:a * 512 + N],
                                                     w1[:, a * HID + index * P:a * HID + index * P + rows], xc[:, :],
                                                     start=True, stop=True)
                            elif kind == "y":
                                pe.wait_ge(taken["h"], units_done(u, d, HC, HC - 1))
                                for c in range(HC):
                                    rows = min(P, HID - c * P)
                                    last = pe.matmul(out[:, 0:N], w2[0:rows, c, :], hid[0:rows, c, :],
                                                     start=(c == 0), stop=(c == HC - 1))
                            last.then_inc(ready[kind], 1)

                loop(pe, unit)

            @block.scalar
            def _(act):
                act.preload_act_table_set(EXP_LN_SET)
                act.wait_ge(small_in, 80)
                act.wait_ge(zeroed, 2)

                def unit(u):
                    for t in range(TILES):
                        n = tiles_done(u, 0, t)
                        start = isinstance(u, int)
                        def square(a):
                            act.wait_ge(qk_ready[a], n)
                            if not (start and n < 2):
                                act.wait_ge(rot_done[a], n - 1)
                            act.activation(qk_sq[:, cols_of(a)], slot_of("qk"[a], 0, t), ACT.Square).then_inc(squared[a], 1)

                        def reciprocal_norm(a):
                            act.wait_ge(ss_ready[a], n)
                            if not (start and n < 3):
                                act.wait_ge(normed[a], n - 2)
                            r = rn[:, t % 2, heads_of(a)]
                            act.activation(r, ss[:, t % 2, heads_of(a)], ACT.Ln, scale=SS_SCALE).then_inc(rn_ready[a], 1)
                            act.wait_ge(rn_ready[a], 2 * n - 1)
                            act.activation(r, r, ACT.Exp, bias=rn_shift, scale=-0.5).then_inc(rn_ready[a], 1)

                        d1, t1 = divmod(t - 1, TILES)
                        d2, t2 = divmod(t - 2, TILES)
                        d3, t3 = divmod(t - 3, TILES)
                        if alive(u, 0):
                            square(0)
                        if alive(u, d1):
                            act.wait_ge(ready["tq"], n - 1)
                            if not (start and n < 4):
                                act.wait_ge(ready["sim"], n - 3)
                            act.activation(qT[:, t1 % 2, :], slot_of("tq", d1, t1), ACT.Copy).then_inc(taken["tq"], 1)
                        if alive(u, d2):
                            act.wait_ge(shifted, n - 2)
                            act.activation(s[:, t2 % 2, :], s[:, t2 % 2, :], ACT.Exp).then_inc(exp_ready, 1)
                        if alive(u, 0):
                            square(1)
                        if alive(u, d1):
                            act.wait_ge(ready["tk"], n - 1)
                            src = slot_of("tk", d1, t1).rearrange("p (c n) -> p c n", n=P)
                            for a in range(2):
                                rows = slice(a * DH, (a + 1) * DH)
                                last = act.activation(k_bd[rows, :, a, WIN + t1 * P:WIN + (t1 + 1) * P], src[rows, :, :], ACT.Copy)
                            last.then_inc(taken["tk"], 1)
                        if alive(u, 0):
                            reciprocal_norm(0)
                        if alive(u, 0):
                            par = t % 2
                            act.wait_ge(ready["v"], n)
                            if not (start and n < 2):
                                act.wait_ge(vbd_in[t1 % 2], spread_count(u, d1, t1))
                            if not (start and n < 3):
                                act.wait_ge(vbd_in[par], spread_count(u, d2, t2))
                            act.activation(v_tok[:, par, :], slot_of("v", 0, t), ACT.Copy).then_inc(taken["v"], 1)
                        if alive(u, d3):
                            act.wait_ge(ready["ot"], n - 3)
                            if not (start and n < 5):
                                act.wait_ge(ready["z"], n - 4)
                            act.activation(oT[:, :], slot_of("ot", d3, t3), ACT.Copy).then_inc(taken["ot"], 1)
                        if alive(u, d2):
                            act.wait_ge(ready["pt"], n - 2)
                            if not (start and n < 4):
                                act.wait_ge(ready["o"], n - 1)
                            act.activation(probT[:, :], slot_of("pt", d2, t2), ACT.Copy).then_inc(taken["pt"], 1)
                        if alive(u, 0):
                            reciprocal_norm(1)
                        if t == 3 and alive(u, -1):
                            act.wait_ge(taken["m1"], units_done(u, -1))
                            if alive(u, -2):
                                act.wait_ge(ready["m2"], units_done(u, -2))
                            act.activation(xc2[:, :], xc[:, :], ACT.Square).then_inc(ff_squared, 1)
                        if t == 0 and alive(u, -2):
                            act.wait_ge(taken["m2"], units_done(u, -2))
                            if alive(u, -3):
                                act.wait_ge(ff_xn, units_done(u, -3))
                            act.activation(rstd[:, :], var[:, :], ACT.Ln).then_inc(ff_rstd, 1)
                            act.wait_ge(ff_rstd, units_done(u, -2, 2, 0))
                            act.activation(rstd[:, :], rstd[:, :], ACT.Exp, scale=-0.5).then_inc(ff_rstd, 1)
                        if t == 1 and alive(u, -2):
                            for j in range(HC):
                                rows = min(P, HID - j * P)
                                act.wait_ge(ready["h"], units_done(u, -2, HC, j))
                                if j == 0 and alive(u, -3):
                                    act.wait_ge(ready["y"], units_done(u, -3))
                                gate = slot_of("h", -2, j)[0:rows, 512:512 + N]
                                act.activation(hid[0:rows, j, :], gate, ACT.Gelu,
                                               bias=column(b1, rows, layer_of(u, -2), HC + j)).then_inc(gelu_ready, 1)
                            act.preload_act_table_set(EXP_LN_SET)

                loop(act, unit)

            @block.vector
            def _(dve):
                dve.memset(k_bd[:, :, :, :], 0.0).then_inc(zeroed, 1)
                dve.memset(v_bd[:, :, :, :, :], 0.0).then_inc(zeroed, 1)
                dve.memset(xs[DH:P, 0:1], 0.0).then_inc(dve_zero, 1)
                dve.memset(xs2[DH:P, 0:1], 0.0).then_inc(dve_zero, 1)
                dve.wait_ge(small_in, 80)
                dve.wait_ge(dve_zero, 2)

                def shift_tile(u, d, t):
                    if t == 0:
                        dve.wait_ge(x_done, units_done(u, d))
                    if alive(u, d - 1):
                        dve.wait_ge(ready["v"], tiles_done(u, d - 1, t))
                    b = batch_of(u, d)
                    dve.tensor_copy(xs[0:DH, t * P:(t + 1) * P], columns_of(b, t, 0, slice(0, DH)))
                    if t:
                        dve.tensor_copy(xs[DH:P, t * P:(t + 1) * P], columns_of(b, t, 1, slice(DH, P))).then_inc(xs_ready, 1)
                    else:
                        dve.tensor_copy(xs[DH:P, 1:P], columns_of(b, 0, 0, slice(DH, P), P - 1)).then_inc(xs_ready, 1)

                shift_tile(0, 0, 0)

                def unit(u):
                    start = isinstance(u, int)
                    for t in range(TILES):
                        n = tiles_done(u, 0, t)
                        d2, t2 = divmod(t - 2, TILES)
                        if t == 1 and alive(u, -2):
                            dve.wait_ge(ff_rstd, units_done(u, -2, 2, 1))
                            chain = units_done(u, -2, 4, 0)
                            dve.tensor_tensor(xc2[:, :], rstd[:, :], rstd[:, :], ALU.mult).then_inc(newton, 1)
                            dve.wait_ge(newton, chain)
                            dve.tensor_tensor(xc2[:, :], xc2[:, :], var[:, :], ALU.mult).then_inc(newton, 1)
                            dve.scalar_tensor_tensor(xc[:, :], xc[:, :], column(ln_g, P, layer_of(u, -2)), rstd[:, :],
                                                     ALU.mult, ALU.mult)
                            dve.wait_ge(newton, chain + 1)
                            dve.tensor_scalar(xc2[:, :], xc2[:, :], -0.5, 1.5, ALU.mult, ALU.add).then_inc(newton, 1)
                            dve.wait_ge(newton, chain + 2)
                            dve.tensor_tensor(xc[:, :], xc[:, :], xc2[:, :], ALU.mult).then_inc(newton, 1)
                            dve.wait_ge(newton, chain + 3)
                            dve.tensor_scalar(xc[:, :], xc[:, :], column(ln_b, P, layer_of(u, -2)), None,
                                              ALU.add).then_inc(ff_xn, 1)
                        dn, tn = divmod(t + 1, TILES)
                        if alive(u, dn):
                            shift_tile(u, dn, tn)
                        def rotate(a):
                            par, cols, heads = t % 2, cols_of(a), heads_of(a)
                            dve.wait_ge(squared[a], n)
                            if a == 0:
                                dve.wait_ge(rot_table, n)
                            if not (start and n < 2):
                                dve.wait_ge(ready[("tq", "tk")[a]], n - 1)
                            dve.tensor_tensor(
                                qk_rot[:, cols].rearrange("p (h d) -> p h d", d=DH),
                                slot_of("qk"[a], 0, t).rearrange("p (h d) -> p h d", d=DH),
                                rot[:, t, 0, a * DH:(a + 1) * DH].unsqueeze(1).to_broadcast([P, HEADS, DH]), ALU.mult)
                            if not (start and n < 3):
                                dve.wait_ge(normed[a], n - 2)
                            dve.tensor_reduce(nt[:, 2 + par, heads], qk_sq[:, cols].rearrange("p (h d) -> p h d", d=DH),
                                              AX.X, ALU.add).then_inc(ss_sum[a], 1)
                            dve.wait_ge(ss_sum[a], n)
                            dve.tensor_scalar(ss[:, par, heads], nt[:, 2 + par, heads], NORM_FLOOR, None, ALU.max)\
                               .then_inc(ss_ready[a], 1)
                            src = slot_of("qk"[a], 0, t).rearrange("p (h g d) -> p h g d", h=HEADS, g=2)
                            dst = qk_sq[:, cols].rearrange("p (h g d) -> p h g d", h=HEADS, g=2)
                            for g in range(2):
                                table = rot[:, t, 1, a * DH + g * (DH // 2):a * DH + (g + 1) * (DH // 2)]
                                last = dve.tensor_tensor(dst[:, :, g, :], src[:, :, 1 - g, :],
                                                         table.unsqueeze(1).to_broadcast([P, HEADS, DH // 2]), ALU.mult)
                            last.then_inc(rot_read[a], 1)

                        if alive(u, 0):
                            rotate(0)
                            rotate(1)
                        if alive(u, d2):
                            dve.wait_ge(exp_ready, n - 2)
                            dve.tensor_reduce(den[:, t2 % 2, 0, :], s[:, t2 % 2, :].rearrange("p (h k) -> p h k", h=HEADS),
                                              AX.X, ALU.add).then_inc(den_ready, 1)
                            dve.wait_ge(den_ready, 2 * (n - 2) - 1)
                            dve.reciprocal(den[:, t2 % 2, 1, :], den[:, t2 % 2, 0, :]).then_inc(den_ready, 1)
                        d1, t1 = divmod(t - 1, TILES)
                        if alive(u, d1):
                            par = t1 % 2
                            dve.wait_ge(ready["sim"], n - 1)
                            if not (start and n < 4):
                                dve.wait_ge(ready["pt"], n - 3)
                            scores = s[:, par, :].rearrange("p (h k) -> p h k", h=HEADS)
                            dve.tensor_tensor(scores, slot_of("sim", d1, t1).rearrange("p (h k) -> p h k", h=HEADS),
                                              mask[0 if t1 == 0 else 1].unsqueeze(1).to_broadcast([P, HEADS, 2 * WIN]),
                                              ALU.add).then_inc(taken["sim"], 1)
                            dve.wait_ge(taken["sim"], n - 1)
                            dve.tensor_reduce(mx[:, par, :], scores, AX.X, ALU.max).then_inc(max_ready, 1)
                        if t == 3 and alive(u, -1):
                            dve.wait_ge(ready["m1"], units_done(u, -1))
                            if alive(u, -2):
                                dve.wait_ge(ready["h"], units_done(u, -2, HC, HC - 1))
                            dve.tensor_tensor(xc[:, :], xs2[:, :], slot_of("m1", -1, 0)[:, 0:N],
                                              ALU.subtract).then_inc(taken["m1"], 1)
                        if t == 0 and alive(u, -2):
                            dve.wait_ge(ready["m2"], units_done(u, -2))
                            dve.tensor_scalar(var[:, :], slot_of("m2", -2, 0)[:, 0:N], LN_EPS, None,
                                              ALU.add).then_inc(taken["m2"], 1)
                        if t == 2 and alive(u, -2):
                            dve.wait_ge(ready["y"], units_done(u, -2))
                            x = columns_of(batch_of(u, -2), 0, 0, slice(0, P), N)
                            dve.scalar_tensor_tensor(x, slot_of("y", -2, 0)[:, 0:N], column(b2, P, layer_of(u, -2)), x,
                                                     ALU.add, ALU.add).then_inc(taken["y"], 1)
                            dve.wait_ge(taken["y"], units_done(u, -2))
                            dve.sem_inc(x_done, 1)
                        d3, t3 = divmod(t - 3, TILES)
                        if alive(u, d3):
                            dve.wait_ge(ready["z"], n - 3)
                            x = columns_of(batch_of(u, d3), t3)
                            dve.tensor_tensor(x, slot_of("z", d3, t3)[:, 0:P], x, ALU.add).then_inc(taken["z"], 1)
                        if t == 2 and alive(u, -1):
                            dve.wait_ge(taken["z"], tiles_done(u, -1, TILES - 1))
                            if alive(u, -2):
                                dve.wait_ge(ready["m1"], units_done(u, -2))
                            b = batch_of(u, -1)
                            dve.tensor_copy(xs2[0:DH, :], columns_of(b, 0, 0, slice(0, DH), N))
                            dve.tensor_copy(xs2[DH:P, 1:N], columns_of(b, 0, 0, slice(DH, P), N - 1)).then_inc(ff_copied, 1)
                        if alive(u, d2):
                            dve.wait_ge(ready["o"], n)
                            dve.wait_ge(den_ready, 2 * (n - 2))
                            if not (start and n < 4):
                                dve.wait_ge(ready["ot"], n - 3)
                            dve.tensor_tensor(
                                o[:, :].rearrange("p (h d) -> p h d", h=HEADS),
                                slot_of("o", d2, t2).rearrange("p (h d) -> p h d", h=HEADS),
                                den[:, t2 % 2, 1, :].unsqueeze(2).to_broadcast([P, HEADS, DH]),
                                ALU.mult).then_inc(taken["o"], 1)
                        if t == 1 and alive(u, -2):
                            for j in range(HC):
                                rows = min(P, HID - j * P)
                                dve.wait_ge(gelu_ready, units_done(u, -2, HC, j))
                                dve.scalar_tensor_tensor(hid[0:rows, j, :], slot_of("h", -2, j)[0:rows, 0:N],
                                                         column(b1, rows, layer_of(u, -2), j), hid[0:rows, j, :],
                                                         ALU.add, ALU.mult).then_inc(taken["h"], 1)

                loop(dve, unit)

            @block.gpsimd
            def _(pool):
                pool.wait_ge(small_in, 80)

                def rot_tables(u, d, t):
                    layer = layer_of(u, d)
                    for part in range(2):
                        scale = qk_scale[:, part, layer, :] if isinstance(layer, int) \
                            else qk_scale[:, part, bass.ds(layer, 1), :].rearrange("p l d -> p (l d)")
                        last = pool.tensor_tensor(rot[:, t, part, :], rot_base[t][part], scale, ALU.mult)
                    last.then_inc(rot_table, 1)

                rot_tables(0, 0, 0)

                def unit(u):
                    start = isinstance(u, int)
                    for t in range(TILES):
                        n = tiles_done(u, 0, t)
                        def normalise(a):
                            par, cols = t % 2, cols_of(a)
                            pool.wait_ge(rot_read[a], n)
                            pool.tensor_tensor(qk_rot[:, cols], qk_rot[:, cols], qk_sq[:, cols], ALU.add).then_inc(rot_done[a], 1)
                            pool.wait_ge(rn_ready[a], 2 * n)
                            r, q, w_ = (x[:, par, heads_of(a)] for x in (rn, ss, nt))
                            chain = 6 * n - 6 + 3 * a
                            pool.tensor_tensor(w_, r, r, ALU.mult).then_inc(pool_own, 1)
                            pool.wait_ge(pool_own, chain + 1)
                            pool.tensor_tensor(w_, w_, q, ALU.mult).then_inc(pool_own, 1)
                            pool.wait_ge(pool_own, chain + 2)
                            pool.tensor_tensor(w_, three[:, 0:HEADS], w_, ALU.subtract).then_inc(pool_own, 1)
                            pool.wait_ge(pool_own, chain + 3)
                            pool.tensor_tensor(r, r, w_, ALU.mult).then_inc(rn_final[a], 1)
                            pool.wait_ge(rn_final[a], n)
                            view = qk_rot[:, cols].rearrange("p (h d) -> p h d", d=DH)
                            pool.tensor_tensor(view, view, r.unsqueeze(2).to_broadcast([P, HEADS, DH]),
                                               ALU.mult).then_inc(normed[a], 1)

                        if alive(u, 0):
                            normalise(0)
                            normalise(1)
                        dn, tn = divmod(t + 1, TILES)
                        if alive(u, dn):
                            rot_tables(u, dn, tn)
                        d, tt = divmod(t - 1, TILES)
                        if alive(u, d):
                            pool.wait_ge(max_ready, n - 1)
                            scores = s[:, tt % 2, :].rearrange("p (h k) -> p h k", h=HEADS)
                            pool.tensor_tensor(scores, scores, mx[:, tt % 2, :].unsqueeze(2).to_broadcast([P, HEADS, 2 * WIN]),
                                               ALU.subtract).then_inc(shifted, 1)

                loop(pool, unit)
AH = 16
AD = DIM // AH
ATT_EPS = 1e-8
JOBS_HEAD = TILES
JOBS_BATCH = AH * TILES
HEADS_ROUND = 4
ROUNDS = AH // HEADS_ROUND
SCORE_BANKS = 3


def modulated_attention(nc, w, const_sb, mod, xT, x_done, x1_dram):
    ident, ones_mean, causal, head = (const_sb[k] for k in ("ident", "ones_mean", "causal", "head"))
    SA, CA, GA, SB, CB, GB = range(6)

    with ExitStack() as ctx:
        def sb(name, shape):
            return ctx.enter_context(nc.sbuf_tensor("at_" + name, shape, F32))

        def sem(name):
            return ctx.enter_context(nc.semaphore("at_" + name))

        def bank(name):
            return ctx.enter_context(nc.psum_tensor("at_" + name, [P, 512], F32))

        cT = sb("cT", [P, BATCH])
        silu = sb("silu", [P, 2, BATCH])
        sign = sb("sign", [P, BATCH])
        wmod = sb("wmod", [P, 6 * DIM])
        wq, wk, wv = sb("wq", [P, P]), sb("wk", [P, P]), sb("wv", [P, P])
        wo = sb("wo", [P, ROUNDS, P])
        x_tok = sb("x_tok", [P, TILES, P])
        xr = sb("xr", [P, N])
        x1 = sb("x1", [P, N])
        xc, sq, var, rstd, hT = (sb(k, [P, N]) for k in ("xc", "sq", "var", "rstd", "hT"))
        qT, kT = sb("qT", [P, N]), sb("kT", [P, N])
        qm = sb("qm", [P, 2, N])
        v_pad = sb("v_pad", [P, TILES, AH, 32])
        probs = sb("probs", [P, 2, TILES, N])
        probT = sb("probT", [P, 2, TILES, N])
        nmx = sb("nmx", [P, 2, TILES])
        den = sb("den", [P, 2, TILES])
        rden = sb("rden", [P, 2, 2, TILES])
        aT = sb("aT", [P, ROUNDS, N])

        ps_score = [bank(f"score{i}") for i in range(SCORE_BANKS)]
        ps_t = [bank(f"t{i}") for i in range(3)]
        ps_a = bank("a")
        ps_m = bank("m")
        PLACE = [(0, 0), (1, 0), (2, 0), (1, 384)]

        w_in, x_in, x1_out = sem("w_in"), sem("x_in"), sem("x1_out")
        exp_c, silu_ready, mod_ready, mod_taken, mod_done = (
            sem(k) for k in ("exp_c", "silu_ready", "mod_ready", "mod_taken", "mod_done"))
        zeroed, x_ready, xr_ready = sem("zeroed"), sem("x_ready"), sem("xr_ready")
        mean_ready, centred, squared, var_ready, var_taken, root, newton, h_ready = (
            sem(k) for k in ("mean_ready", "centred", "squared", "var_ready", "var_taken", "root", "newton", "h_ready"))
        proj_ready, proj_taken = sem("proj_ready"), sem("proj_taken")
        qm_ready, scores_ready, masked, max_ready, exp_ready = (
            sem(k) for k in ("qm_ready", "scores_ready", "masked", "max_ready", "exp_ready"))
        rden_own, weights_ready, t_ready, t_act, t_dve = (
            sem(k) for k in ("rden_own", "weights_ready", "t_ready", "t_act", "t_dve"))
        a_ready, a_taken, wo_ready, x1_ready = (sem(k) for k in ("a_ready", "a_taken", "wo_ready", "x1_ready"))

        with nc.Block() as block:
            @block.sync
            def _(sp):
                for dst, src in ((cT[:, :], w["cT"]), (wmod[:, :], w["wmod"]), (wq[:, :], w["wq"]), (wk[:, :], w["wk"]),
                                 (wv[:, :], w["wv"]), (wo[:, :, :], w["a_wo"])):
                    sp.dma_start(dst, src).then_inc(w_in, 16)
                sp.dma_start(x_tok[:, :, :], w["x"][0, :, :].rearrange("(t p) d -> p t d", p=P)).then_inc(x_in, 16)

                sp.sem_inc(x1_out, 16)

                def store(b):
                    sp.wait_ge(x1_ready, b + 1)
                    dst = x1_dram[:, b * N:(b + 1) * N] if isinstance(b, int) else x1_dram[:, bass.ds(b * N, N)]
                    sp.dma_start(dst, x1[:, :]).then_inc(x1_out, 16)

                with sp.Fori(0, BATCH - 1) as b:
                    sp.wait_ge(x_ready, b + 1)
                    sp.dma_start(x_tok[:, :, :], w["x"][bass.ds(b + 1, 1), :, :].rearrange("b (t p) d -> p (b t) d", p=P))\
                      .then_inc(x_in, 16)
                    store(b)
                store(BATCH - 1)
                sp.wait_ge(x1_out, 16 * BATCH + 16)

            @block.tensor
            def _(pe):
                pe.wait_ge(w_in, 96)
                pe.wait_ge(silu_ready, 1)
                for j in range(6):
                    last = pe.matmul(ps_m[:, j * BATCH:(j + 1) * BATCH], wmod[:, j * DIM:(j + 1) * DIM], silu[:, 1, :],
                                     start=True, stop=True)
                last.then_inc(mod_ready, 1)
                pe.wait_ge(mod_taken, 1)

                def layer_norm(b, k):
                    pe.matmul(ps_m[:, :], ones_mean, (xr if k == 0 else x1)[:, :], start=True, stop=True)\
                      .then_inc(mean_ready, 1)
                    pe.wait_ge(squared, 2 * b + (k + 1))
                    pe.matmul(ps_m[:, :], ones_mean, sq[:, :], start=True, stop=True).then_inc(var_ready, 1)

                def weigh(b, h):
                    pe.wait_ge(weights_ready, AH * b + (h + 1))
                    if h:
                        pe.wait_ge(t_act, AH * 2 * b + 2 * h)
                        pe.wait_ge(t_dve, AH * b + h)
                    for j in (0, 1, 3, 2):
                        at, col = PLACE[j]
                        for i in range(j, TILES):
                            last = pe.transpose(ps_t[at][:, col + (i - j) * P:col + (i - j + 1) * P],
                                                probs[:, h % 2, i, j * P:(j + 1) * P], ident)
                        if j in (0, 3, 2):
                            last.then_inc(t_ready, 1)
                    if h % HEADS_ROUND == 0 and h:
                        pe.wait_ge(a_taken, ROUNDS * b + h // HEADS_ROUND)
                    pe.wait_ge(t_act, AH * 2 * b + (2 * h + 2))
                    pe.wait_ge(t_dve, AH * b + (h + 1))
                    g = h % HEADS_ROUND
                    for j in range(TILES):
                        last = pe.matmul(ps_a[g * 32:(g + 1) * 32, j * P:N], v_pad[:, j, h, :],
                                         probT[:, h % 2, j, 0:N - j * P], start=(j == 0), stop=(j == TILES - 1))
                    last.then_inc(a_ready, 1)

                with pe.Fori(0, BATCH) as b:
                    pe.wait_ge(x_in, 16 * b + 16)
                    for t in range(TILES):
                        last = pe.transpose(ps_m[:, t * P:(t + 1) * P], x_tok[:, t, :], ident)
                    last.then_inc(x_ready, 1)
                    pe.wait_ge(xr_ready, b + 1)
                    layer_norm(b, 0)
                    pe.wait_ge(h_ready, 2 * b + 1)
                    pe.matmul(ps_score[0][:, :], wq[:, :], hT[:, :], start=True, stop=True).then_inc(proj_ready, 1)
                    pe.matmul(ps_score[1][:, :], wk[:, :], hT[:, :], start=True, stop=True).then_inc(proj_ready, 1)
                    for t in range(TILES):
                        last = pe.matmul(ps_score[2][:, t * P:(t + 1) * P], hT[:, t * P:(t + 1) * P], wv[:, :],
                                         start=True, stop=True)
                    last.then_inc(proj_ready, 1)
                    pe.wait_ge(proj_taken, 3 * b + 3)
                    for h in range(AH):
                        pe.wait_ge(qm_ready, AH * b + (h + 1))
                        for i in range(TILES):
                            k = h * TILES + i
                            if k >= SCORE_BANKS:
                                pe.wait_ge(exp_ready, JOBS_BATCH * b + (k - SCORE_BANKS + 1))
                            pe.matmul(ps_score[k % SCORE_BANKS][:, 0:(i + 1) * P], qm[:, h % 2, i * P:(i + 1) * P],
                                      kT[:, 0:(i + 1) * P], start=True, stop=True).then_inc(scores_ready, 1)
                        if h:
                            weigh(b, h - 1)
                    weigh(b, AH - 1)
                    pe.wait_ge(a_taken, ROUNDS * b + ROUNDS)
                    for r in range(ROUNDS):
                        last = pe.matmul(ps_m[:, :], wo[:, r, :], aT[:, r, :], start=(r == 0), stop=(r == ROUNDS - 1))
                    last.then_inc(wo_ready, 1)
                    pe.wait_ge(x1_ready, b + 1)
                    layer_norm(b, 1)
                    pe.wait_ge(var_taken, 2 * b + 2)

            @block.scalar
            def _(act):
                act.preload_act_table_set(EXP_LN_SET)
                act.wait_ge(w_in, 96)
                act.activation(silu[:, 0, :], cT[:, :], ACT.Exp, scale=-1.0).then_inc(exp_c, 1)

                def layer_norm(b, k):
                    act.wait_ge(centred, 2 * b + (k + 1))
                    act.activation(sq[:, :], xc[:, :], ACT.Square).then_inc(squared, 1)
                    act.wait_ge(var_taken, 2 * b + (k + 1))
                    act.activation(rstd[:, :], var[:, :], ACT.Ln).then_inc(root, 1)
                    act.wait_ge(root, 4 * b + (2 * k + 1))
                    act.activation(rstd[:, :], rstd[:, :], ACT.Exp, scale=-0.5).then_inc(root, 1)

                def take_transposed(b, h):
                    act.wait_ge(t_ready, 3 * AH * b + (3 * h + 1))
                    if h > 1:
                        act.wait_ge(a_ready, AH * b + (h - 1))
                    act.activation(probT[:, h % 2, 0, :], ps_t[0][:, :], ACT.Copy).then_inc(t_act, 1)
                    act.wait_ge(t_ready, 3 * AH * b + (3 * h + 3))
                    act.activation(probT[:, h % 2, 2, 0:2 * P], ps_t[2][:, 0:2 * P], ACT.Copy).then_inc(t_act, 1)

                with act.Fori(0, BATCH) as b:
                    layer_norm(b, 0)
                    act.wait_ge(proj_ready, 3 * b + 1)
                    act.activation(qT[:, :], ps_score[0][:, :], ACT.Copy, scale=float(AD) ** -0.5).then_inc(proj_taken, 1)
                    act.wait_ge(proj_ready, 3 * b + 2)
                    act.activation(kT[:, :], ps_score[1][:, :], ACT.Copy).then_inc(proj_taken, 1)
                    act.wait_ge(proj_ready, 3 * b + 3)
                    act.activation(v_pad[:, :, :, 0:AD].rearrange("p t h d -> p (t h) d"),
                                   ps_score[2][:, :].rearrange("p (a d) -> p a d", d=AD), ACT.Copy).then_inc(proj_taken, 1)
                    for h in range(AH):
                        for i in range(TILES):
                            k = h * TILES + i
                            act.wait_ge(max_ready, JOBS_BATCH * b + (k + 1))
                            if h > 1 and i == 0:
                                act.wait_ge(t_ready, 3 * AH * b + 3 * (h - 1))
                            act.activation(probs[:, h % 2, i, 0:(i + 1) * P], ps_score[k % SCORE_BANKS][:, 0:(i + 1) * P],
                                           ACT.Exp, bias=nmx[:, h % 2, i:i + 1],
                                           accum_out=den[:, h % 2, i:i + 1]).then_inc(exp_ready, 1)
                        if h:
                            take_transposed(b, h - 1)
                    take_transposed(b, AH - 1)
                    layer_norm(b, 1)

            @block.vector
            def _(dve):
                dve.memset(v_pad[:, :, :, :], 0.0).then_inc(zeroed, 1)
                dve.wait_ge(exp_c, 1)
                dve.tensor_scalar(silu[:, 0, :], silu[:, 0, :], 1.0, None, ALU.add).then_inc(zeroed, 1)
                dve.wait_ge(zeroed, 2)
                dve.reciprocal(silu[:, 0, :], silu[:, 0, :]).then_inc(zeroed, 1)
                dve.wait_ge(zeroed, 3)
                dve.tensor_tensor(silu[:, 1, :], cT[:, :], silu[:, 0, :], ALU.mult).then_inc(silu_ready, 1)
                dve.wait_ge(mod_ready, 1)
                dve.tensor_copy(mod[:, :, :].rearrange("p j b -> p (j b)"), ps_m[:, 0:6 * BATCH]).then_inc(mod_taken, 1)
                dve.wait_ge(mod_taken, 1)
                step = 0
                for j in (CA, CB):
                    dve.tensor_scalar(mod[:, j, :], mod[:, j, :], 1.0, None, ALU.add).then_inc(mod_done, 1)
                    step += 1
                for j in (GA, GB):
                    g = mod[:, j, :]
                    dve.wait_ge(mod_done, step)
                    dve.tensor_scalar(sign[:, :], g, 0.0, 2.0, ALU.is_ge, ALU.mult).then_inc(mod_done, 1)
                    dve.wait_ge(mod_done, step + 1)
                    dve.tensor_scalar(sign[:, :], sign[:, :], -1.0, None, ALU.add).then_inc(mod_done, 1)
                    dve.wait_ge(mod_done, step + 2)
                    dve.tensor_tensor(g, g, sign[:, :], ALU.mult).then_inc(mod_done, 1)
                    dve.wait_ge(mod_done, step + 3)
                    dve.scalar_tensor_tensor(g, g, 0.25, sign[:, :], ALU.max, ALU.mult).then_inc(mod_done, 1)
                    step += 4
                dve.wait_ge(mod_done, step)

                def modulation(b, j):
                    return mod[:, j, bass.ds(b, 1)]

                def layer_norm(b, k, src, shift, scale, dst):
                    dve.wait_ge(mean_ready, 2 * b + (k + 1))
                    dve.tensor_tensor(xc[:, :], src, ps_m[:, :], ALU.subtract).then_inc(centred, 1)
                    dve.wait_ge(var_ready, 2 * b + (k + 1))
                    dve.tensor_scalar(var[:, :], ps_m[:, :], LN_EPS, None, ALU.add).then_inc(var_taken, 1)
                    dve.wait_ge(root, 4 * b + (2 * k + 2))
                    chain = 10 * b + 5 * k
                    dve.tensor_tensor(sq[:, :], rstd[:, :], rstd[:, :], ALU.mult).then_inc(newton, 1)
                    dve.wait_ge(newton, chain + 1)
                    dve.tensor_tensor(sq[:, :], sq[:, :], var[:, :], ALU.mult).then_inc(newton, 1)
                    dve.scalar_tensor_tensor(xc[:, :], xc[:, :], modulation(b, scale), rstd[:, :], ALU.mult, ALU.mult)
                    dve.wait_ge(newton, chain + 2)
                    dve.tensor_scalar(sq[:, :], sq[:, :], -0.5, 1.5, ALU.mult, ALU.add).then_inc(newton, 1)
                    dve.wait_ge(newton, chain + 3)
                    dve.tensor_tensor(xc[:, :], xc[:, :], sq[:, :], ALU.mult).then_inc(newton, 1)
                    dve.wait_ge(newton, chain + 4)
                    dve.tensor_scalar(dst, xc[:, :], modulation(b, shift), None, ALU.add).then_inc(newton, 1)
                    dve.wait_ge(newton, chain + 5)

                def pick_head(b, h):
                    if h > 1:
                        dve.wait_ge(scores_ready, JOBS_BATCH * b + TILES * (h - 1))
                    dve.tensor_scalar(qm[:, h % 2, :], qT[:, :], head[:, h:h + 1], None, ALU.mult).then_inc(qm_ready, 1)

                def mask_and_max(b, h, i):
                    k = h * TILES + i
                    bank_k = ps_score[k % SCORE_BANKS]
                    dve.wait_ge(scores_ready, JOBS_BATCH * b + (k + 1))
                    diagonal = bank_k[:, i * P:(i + 1) * P]
                    dve.tensor_tensor(diagonal, diagonal, causal, ALU.add).then_inc(masked, 1)
                    dve.wait_ge(masked, JOBS_BATCH * b + (k + 1))
                    dve.tensor_reduce(nmx[:, h % 2, i:i + 1], bank_k[:, 0:(i + 1) * P], AX.X, ALU.max, negate=True)\
                       .then_inc(max_ready, 1)

                def normalise(b, h):
                    dve.wait_ge(exp_ready, JOBS_BATCH * b + TILES * (h + 1))
                    chain = 2 * AH * b + 2 * h
                    dve.tensor_scalar(rden[:, h % 2, 0, :], den[:, h % 2, :], ATT_EPS, None, ALU.add).then_inc(rden_own, 1)
                    dve.wait_ge(rden_own, chain + 1)
                    dve.reciprocal(rden[:, h % 2, 1, :], rden[:, h % 2, 0, :]).then_inc(rden_own, 1)
                    dve.wait_ge(rden_own, chain + 2)
                    for i in range(TILES):
                        row = probs[:, h % 2, i, 0:(i + 1) * P]
                        last = dve.tensor_scalar(row, row, rden[:, h % 2, 1, i:i + 1], None, ALU.mult)
                    last.then_inc(weights_ready, 1)

                def take_transposed(b, h):
                    dve.wait_ge(t_ready, 3 * AH * b + (3 * h + 2))
                    if h > 1:
                        dve.wait_ge(a_ready, AH * b + (h - 1))
                    dve.tensor_copy(probT[:, h % 2, 1, 0:3 * P], ps_t[1][:, 0:3 * P])
                    dve.tensor_copy(probT[:, h % 2, 3, 0:P], ps_t[1][:, 3 * P:4 * P]).then_inc(t_dve, 1)

                def take_round(b, r):
                    dve.wait_ge(a_ready, AH * b + HEADS_ROUND * (r + 1))
                    dve.tensor_copy(aT[:, r, :], ps_a[:, :]).then_inc(a_taken, 1)

                with dve.Fori(0, BATCH) as b:
                    dve.wait_ge(x_ready, b + 1)
                    dve.tensor_copy(xr[:, :], ps_m[:, :]).then_inc(xr_ready, 1)
                    dve.wait_ge(xr_ready, b + 1)
                    layer_norm(b, 0, xr[:, :], SA, CA, hT[:, :])
                    dve.sem_inc(h_ready, 1)
                    dve.wait_ge(proj_taken, 3 * b + 3)
                    pick_head(b, 0)
                    for h in range(AH):
                        if h + 1 < AH:
                            pick_head(b, h + 1)
                        mask_and_max(b, h, 0)
                        mask_and_max(b, h, 1)
                        if h:
                            normalise(b, h - 1)
                        mask_and_max(b, h, 2)
                        mask_and_max(b, h, 3)
                        if h:
                            take_transposed(b, h - 1)
                        if h and h % HEADS_ROUND == 0:
                            take_round(b, h // HEADS_ROUND - 1)
                    normalise(b, AH - 1)
                    take_transposed(b, AH - 1)
                    take_round(b, ROUNDS - 1)
                    dve.wait_ge(wo_ready, b + 1)
                    dve.wait_ge(x1_out, 16 * b + 16)
                    dve.scalar_tensor_tensor(x1[:, :], ps_m[:, :], modulation(b, GA), xr[:, :], ALU.mult, ALU.add)\
                       .then_inc(x1_ready, 1)
                    dve.wait_ge(x1_ready, b + 1)
                    layer_norm(b, 1, x1[:, :], SB, CB, xT[:, bass.ds(b * N, N)])
                    dve.sem_inc(h_ready, 1)
                    dve.sem_inc(x_done, 1)


def last_residual(nc, const_sb, mod, xT, x1_dram, out):
    ident = const_sb["ident"]
    GB = 5
    with ExitStack() as ctx:
        x1 = ctx.enter_context(nc.sbuf_tensor("lr_x1", [P, BATCH, N], F32))
        y = ctx.enter_context(nc.sbuf_tensor("lr_y", [P, BATCH, N], F32))
        y_tok = ctx.enter_context(nc.sbuf_tensor("lr_y_tok", [P, BATCH, N], F32))
        ps = [ctx.enter_context(nc.psum_tensor(f"lr_ps{i}", [P, N], F32)) for i in range(BATCH)]
        x1_in, y_ready, t_ready, t_taken, stored = (
            ctx.enter_context(nc.semaphore("lr_" + k)) for k in ("x1_in", "y_ready", "t_ready", "t_taken", "stored"))
        with nc.Block() as block:
            @block.sync
            def _(sp):
                sp.dma_start(x1[:, :, :].rearrange("p b n -> p (b n)"), x1_dram[:, :]).then_inc(x1_in, 16)
                for b in range(BATCH):
                    sp.wait_ge(t_taken, b + 1)
                    sp.dma_start(out[b, :, :].rearrange("(t p) d -> p t d", p=P),
                                 y_tok[:, b, :].rearrange("p (t d) -> p t d", d=DIM)).then_inc(stored, 16)
                sp.wait_ge(stored, 16 * BATCH)

            @block.vector
            def _(dve):
                dve.wait_ge(x1_in, 16)
                for b in range(BATCH):
                    dve.scalar_tensor_tensor(y[:, b, :], xT[:, b * N:(b + 1) * N], mod[:, GB, b:b + 1], x1[:, b, :],
                                             ALU.mult, ALU.add).then_inc(y_ready, 1)

            @block.tensor
            def _(pe):
                for b in range(BATCH):
                    pe.wait_ge(y_ready, b + 1)
                    for t in range(TILES):
                        last = pe.transpose(ps[b][:, t * P:(t + 1) * P], y[:, b, t * P:(t + 1) * P], ident)
                    last.then_inc(t_ready, 1)

            @block.scalar
            def _(act):
                for b in range(BATCH):
                    act.wait_ge(t_ready, b + 1)
                    act.activation(y_tok[:, b, :], ps[b][:, :], ACT.Copy).then_inc(t_taken, 1)


def adaln_block(nc, w, out):
    with ExitStack() as ctx:
        consts = ctx.enter_context(nc.sbuf_tensor("consts_sb", [P, C_END], F32))
        xT = ctx.enter_context(nc.sbuf_tensor("xT_sb", [P, BATCH * N], F32))
        mod = ctx.enter_context(nc.sbuf_tensor("mod_sb", [P, 6, BATCH], F32))
        x1_dram = nc.dram_tensor("x1_dims_first", [P, BATCH * N], F32, kind="Internal").ap()
        consts_in = ctx.enter_context(nc.semaphore("consts_in"))
        x_done = ctx.enter_context(nc.semaphore("x_done"))
        with nc.Block() as block:
            @block.sync
            def _(sp):
                sp.dma_start(consts[:, :], w["consts"]).then_inc(consts_in, 16)
                sp.wait_ge(consts_in, 16)
        const_sb = constant_views(consts)
        modulated_attention(nc, w, const_sb, mod, xT, x_done, x1_dram)
        local_stack(nc, w, DEPTH, const_sb, xT, x_done)
        last_residual(nc, const_sb, mod, xT, x1_dram, out)


def _layouts(inputs):
    a = {k: np.asarray(v) for k, v in inputs.items()}
    wkv = a["L0_attn_Wkv"]
    a_wo = np.zeros((P, ROUNDS, P), np.float32)
    rows = a["L0_attn_Wo"].T.reshape(ROUNDS, HEADS_ROUND, AD, DIM)
    for j in range(HEADS_ROUND):
        a_wo[j * 32:j * 32 + AD] = rows[:, j].transpose(1, 0, 2)
    b1 = np.zeros((P, DEPTH, 2 * HC), np.float32)
    for half in range(2):
        for j in range(HC):
            n = min(P, HID - j * P)
            b1[:n, :, half * HC + j] = a["L0_ffn_b1"][:, half * HID + j * P:half * HID + j * P + n].T
    q_scale, k_scale = a["L0_ffn_q_scale"], a["L0_ffn_k_scale"]
    swap = [np.concatenate([s[:, DH // 2:], s[:, :DH // 2]], 1) for s in (q_scale, k_scale)]
    qk_scale = np.stack([np.concatenate([q_scale, k_scale], 1), np.concatenate(swap, 1)]).reshape(-1)
    return {
        "consts": shape_constants(),
        "cT": a["L0_c"].T, "wmod": a["L0_wmod"], "x": a["L0_attn_x"],
        "wq": a["L0_attn_Wq"].T, "wk": wkv[:DIM].T, "wv": wkv[DIM:].T, "a_wo": a_wo,
        "wqkv": a["L0_ffn_Wqkv"], "wo": a["L0_ffn_Wo"], "w1": a["L0_ffn_W1"], "w2": a["L0_ffn_W2"],
        "ln_g": a["L0_ffn_ln_g"].T, "ln_b": a["L0_ffn_ln_b"].T, "b1": b1.reshape(P, -1), "b2": a["L0_ffn_b2"].T,
        "qk_scale": qk_scale,
    }


def kernel(**inputs):
    import concourse.bacc as bacc
    from concourse.bass_utils import run_bass_kernel_spmd

    nc = bacc.Bacc("TRN2", target_bir_lowering=False, num_devices=1)
    arrays, w = {}, {}
    for name, value in _layouts(inputs).items():
        value = np.ascontiguousarray(value)
        arrays["in_" + name] = value
        w[name] = nc.dram_tensor("in_" + name, value.shape, mybir.dt.from_np(value.dtype), kind="ExternalInput").ap()
    out = nc.dram_tensor("out_dram", (BATCH, N, DIM), F32, kind="ExternalOutput").ap()
    adaln_block(nc, w, out)
    result = run_bass_kernel_spmd(nc, [arrays], core_ids=[0])
    return np.asarray(result.results[0]["out_dram"])
```

```python
from contextlib import ExitStack

import numpy as np

import concourse.bass as bass
from concourse import mybir

ALU = mybir.AluOpType
ACT = mybir.ActivationFunctionType
AX = mybir.AxisListType
F32 = mybir.dt.float32
F32R = mybir.dt.float32r

P = 128
BATCH, N, DIM = 8, 512, 128
TILES = N // P
DEPTH, HEADS, DH, WIN = 6, 16, 64, 32
INNER = HEADS * DH
IC = INNER // P
WPT = P // WIN
HID = int(DIM * 4 * 2 / 3)
HC = -(-HID // P)
NBANKS, BANK = 8, 512
H_BANKS = ((0, 1), (6, 7), (2, 3))
PASSES = ((0, 0), (0, 1), (1, 0))
LN_EPS = 1e-5
NORM_FLOOR = 1e-24
SS_SCALE = 2.0 ** 24
RN_SHIFT = 12.0 * float(np.log(2.0))
EXP_LN_SET = "natural_log_exp_and_others"
MASKED = -3.0e38

C_IDENT, C_MEAN, C_MASK, C_CAUSAL = 0, P, 2 * P, 2 * P + 4 * WIN
C_ROT = C_CAUSAL + P
C_HEAD = C_ROT + TILES * 2 * 2 * DH
C_LOW = C_HEAD + 4
C_SHIFT = C_LOW + 2
C_THREE = C_SHIFT + 1
C_ONE = C_THREE + 2 * HEADS
C_END = C_ONE + 1


def shape_constants():
    c = np.zeros((P, C_END), np.float32)
    c[:, C_IDENT:C_IDENT + P] = np.eye(P, dtype=np.float32)
    c[:, C_MEAN:C_MEAN + P] = 1.0 / DIM
    i = np.arange(P)[:, None] % WIN
    j = np.arange(2 * WIN)[None, :]
    seen = np.where(j < WIN, j >= i, j - WIN <= i)
    first = seen & ((np.arange(P)[:, None] >= WIN) | (j >= WIN))
    c[:, C_MASK:C_MASK + 2 * WIN] = np.where(first, 0.0, MASKED)
    c[:, C_MASK + 2 * WIN:C_MASK + 4 * WIN] = np.where(seen, 0.0, MASKED)
    c[:, C_CAUSAL:C_CAUSAL + P] = np.where(np.arange(P)[None, :] <= np.arange(P)[:, None], 0.0, MASKED)
    half = np.arange(0, DH, 2, dtype=np.float32)
    inv_freq = (np.float32(1.0) / np.float32(10000.0) ** (half / np.float32(DH))).astype(np.float32)
    pos = np.arange(N, dtype=np.float32)
    freqs = (pos[:, None] * inv_freq[None, :]).astype(np.float64)
    base = ((half + np.float32(0.4 * DH)) / np.float32(1.4 * DH)).astype(np.float64)
    scale = base[None, :] ** ((pos.astype(np.float64)[:, None] - N // 2) / (WIN // 2))
    cos, sin = (np.concatenate([f(freqs)] * 2, -1) for f in (np.cos, np.sin))
    sin[:, :DH // 2] *= -1.0
    scale = np.concatenate([scale, scale], -1)
    tables = 0.5 * np.stack([np.concatenate([f * scale * 8.0, f / scale], -1) for f in (cos, sin)], 1)
    c[:, C_ROT:C_HEAD] = tables.reshape(TILES, P, 2 * 2 * DH).transpose(1, 0, 2).reshape(P, -1)
    c[:, C_SHIFT] = RN_SHIFT
    c[:, C_THREE:C_ONE] = 3.0
    c[:, C_ONE] = 1.0
    row = np.arange(P)
    c[:, C_HEAD:C_LOW] = row[:, None] % 32 // 8 == np.arange(4)[None, :]
    c[:, C_LOW] = -1.0 * (row // 64 == 1)
    c[:, C_LOW + 1] = -1.0 * (row // 32 % 2 == 1)
    return c


def constant_views(consts):
    width = 2 * 2 * DH
    return {
        "ident": consts[:, C_IDENT:C_IDENT + P],
        "ones_mean": consts[:, C_MEAN:C_MEAN + P],
        "mask": [consts[:, C_MASK + i * 2 * WIN:C_MASK + (i + 1) * 2 * WIN] for i in range(2)],
        "causal": consts[:, C_CAUSAL:C_CAUSAL + P],
        "rot_base": [[consts[:, C_ROT + t * width + i * 2 * DH:C_ROT + t * width + (i + 1) * 2 * DH] for i in range(2)]
                     for t in range(TILES)],
        "head": consts[:, C_HEAD:C_LOW],
        "low_q": consts[:, C_LOW:C_LOW + 1],
        "low_k": consts[:, C_LOW + 1:C_LOW + 2],
        "rn_shift": consts[:, C_SHIFT:C_SHIFT + 1],
        "three": consts[:, C_THREE:C_ONE],
        "one": consts[:, C_ONE:C_END],
    }


def local_stack(nc, w, LAYERS, const_sb, xT, x_done, w_split):
    NU = LAYERS * BATCH
    ident, ones_mean, mask, rot_base, rn_shift, three = (
        const_sb[k] for k in ("ident", "ones_mean", "mask", "rot_base", "rn_shift", "three"))

    def alive(u, d):
        return not isinstance(u, int) or 0 <= u + d < NU

    def tiles_done(u, d, t):
        return u * TILES + (TILES * d + t + 1)

    def units_done(u, d, per=1, index=0):
        return u * per + (per * d + index + 1)

    def batch_of(u, d):
        return (u + d) % BATCH if isinstance(u, int) else (u + (d % BATCH)) % BATCH

    def layer_of(u, d):
        return (u + d) // BATCH if isinstance(u, int) else (u + d) // BATCH

    def column(tensor, rows, layer, c=None):
        if isinstance(layer, int):
            return tensor[0:rows, layer:layer + 1] if c is None else tensor[0:rows, layer, c:c + 1]
        if c is None:
            return tensor[0:rows, bass.ds(layer, 1)]
        return tensor[0:rows, bass.ds(layer, 1), c:c + 1].rearrange("p a c -> p (a c)")

    def columns_of(b, t, shift=0, rows=slice(0, P), width=P):
        if isinstance(b, int):
            start = b * N + t * P - shift
            return xT[rows, start:start + width]
        return xT[rows, bass.ds(b * N + (t * P - shift), width)]

    def spread_count(u, d, t):
        return u * 256 + (256 * d + 128 * (t // 2 + 1))

    def carry_count(u, d, t):
        per = 64 if t % 2 else 32
        return u * per + (per * d + 32 * ((t + 1) // 2))

    def cols_of(a):
        return slice(a * INNER, (a + 1) * INNER)

    def heads_of(a):
        return slice(a * HEADS, (a + 1) * HEADS)

    with ExitStack() as ctx:
        def sb(name, shape, dtype=F32):
            return ctx.enter_context(nc.sbuf_tensor("st_" + name, shape, dtype))

        def sem(name):
            return ctx.enter_context(nc.semaphore("st_" + name))

        wqkv = sb("wqkv", [P, 3, 2, INNER], F32R)
        wo = sb("wo", [P, IC, P])
        w1 = sb("w1", [P, 2 * HID])
        w2 = sb("w2", [P, HC, P])
        ln_g = sb("ln_g", [P, LAYERS])
        ln_b = sb("ln_b", [P, LAYERS])
        b1 = sb("b1", [P, LAYERS, 2 * HC])
        b2 = sb("b2", [P, LAYERS])
        qk_scale = sb("qk_scale", [P, 2, LAYERS, 2 * DH])
        rot = sb("rot", [P, TILES, 2, 2 * DH])
        xs = sb("xs", [P, 2, N], F32R)
        qk_sq = sb("qk_sq", [P, 2 * INNER])
        qk_rot = sb("qk_rot", [P, 2 * INNER])
        ss = sb("ss", [P, 2, 2 * HEADS])
        rn = sb("rn", [P, 2, 2 * HEADS])
        nt = sb("nt", [P, 4, 2 * HEADS])
        v_tok = sb("v_tok", [P, 2, INNER])
        v_bd = sb("v_bd", [P, 2, WPT, 2, INNER // 2])
        qT = sb("qT", [P, 2, INNER])
        k_bd = sb("k_bd", [P, IC, 2, WIN + N])
        s = sb("s", [P, 2, INNER])
        mx = sb("mx", [P, 2, HEADS])
        den = sb("den", [P, 2, 2, HEADS])
        probT = sb("probT", [P, INNER])
        o = sb("o", [P, INNER])
        oT = sb("oT", [P, INNER])
        xs2 = sb("xs2", [P, N])
        xc = sb("xc", [P, N])
        xc2 = sb("xc2", [P, N])
        var = sb("var", [P, N])
        rstd = sb("rstd", [P, N])
        hid = sb("hid", [P, HC, N])

        ps = ctx.enter_context(nc.psum_tensor("st_ps", [P, NBANKS * BANK], F32))

        small_in, wo_in, w12_in = sem("small_in"), sem("wo_in"), sem("w12_in")
        wqkv_in = {k: sem(f"w{k}_in") for k in "qkv"}
        vbd_in = [sem("vbd_in0"), sem("vbd_in1")]
        carry_in = [sem("carry_in0"), sem("carry_in1")]
        zeroed = sem("zeroed")
        KINDS = ("q", "k", "z", "v", "tq", "tk", "pt", "sim", "o", "m1", "m2", "h", "y", "ot")
        PER_UNIT = {k: {"m1": 1, "m2": 1, "h": HC, "y": 1}.get(k, TILES) for k in KINDS}
        ready = {k: sem(k + "_ready") for k in KINDS}
        qk_ready = [ready["q"], ready["k"]]
        taken = {k: sem(k + "_taken") for k in KINDS if k not in ("q", "k")}
        squared, rot_read, rot_done, ss_sum, ss_ready, rn_ready, rn_final, normed = (
            [sem(f"{k}_{a}") for a in "qk"] for k in
            ("squared", "rot_read", "rot_done", "ss_sum", "ss_ready", "rn_ready", "rn_final", "normed"))
        xs_high, xs_ready = sem("xs_high"), sem("xs_ready")
        rot_table = sem("rot_table")
        max_ready, shifted, exp_ready, den_ready = sem("max_ready"), sem("shifted"), sem("exp_ready"), sem("den_ready")
        ff_copied, ff_squared, ff_rstd, ff_xn = sem("ff_copied"), sem("ff_squared"), sem("ff_rstd"), sem("ff_xn")
        gelu_ready = sem("gelu_ready")
        dve_zero, ff_gain, ff_newton, pool_own = sem("dve_zero"), sem("ff_gain"), sem("ff_newton"), sem("pool_own")

        def jobs_of(t):
            def tile(kind, back, *banks):
                d, tt = divmod(t - back, TILES)
                return (kind, d, tt), banks

            feed = {3: [(("m1", -1, 0), (7,))], 0: [(("m2", -2, 0), (7,))], 1: [], 2: [(("y", -2, 0), (7,))]}[t]
            hidden = [(("h", -2, j), H_BANKS[j]) for j in range(HC)] if t == 1 else []
            return [tile("q", 0, 0, 1), tile("tq", 1, 2, 3), tile("k", 0, 4, 5), tile("tk", 1, 6, 7),
                    tile("v", 0, 2, 3), tile("ot", 3, 0, 1), tile("pt", 2, 6, 7), tile("sim", 1, 2, 3), *feed,
                    tile("z", 3, 6), tile("o", 2, 4, 5), *hidden]

        JOBS = [job for t in range(TILES) for job, _ in jobs_of(t)]
        BANKS = [banks for t in range(TILES) for _, banks in jobs_of(t)]
        STARTS = [sum(len(jobs_of(i)) for i in range(t)) for t in range(TILES)]
        FIRST_BANK = {job: banks[0] for job, banks in zip(JOBS, BANKS)}

        def slot_of(kind, d, index):
            first = FIRST_BANK[(kind, d, index)] * BANK
            return ps[:, first:min(first + INNER, NBANKS * BANK)]

        def slot_free(eng, u, at):
            held, back = set(BANKS[at]), at
            while held:
                back -= 1
                over, i = divmod(back, len(JOBS))
                if isinstance(u, int) and u + over < -1:
                    return
                kind, d, index = JOBS[i]
                if not held & set(BANKS[i]) or not alive(u, d + over):
                    continue
                held -= set(BANKS[i])
                count = units_done(u, d + over, PER_UNIT[kind], index)
                if kind in ("q", "k"):
                    eng.wait_ge(squared[kind == "k"], count)
                    eng.wait_ge(rot_read[kind == "k"], count)
                else:
                    eng.wait_ge(taken[kind], count)

        def loop(eng, unit):
            unit(0)
            unit(1)
            with eng.Fori(2, NU - 1) as u:
                unit(u)
            unit(NU - 1)
            unit(NU)
            unit(NU + 1)

        with nc.Block() as block:
            @block.sync
            def _(sp):
                for dst, src in ((ln_g, "ln_g"), (ln_b, "ln_b"), (b1[:, :, :].rearrange("p l c -> p (l c)"), "b1"), (b2, "b2")):
                    sp.dma_start(dst[:, :], w[src]).then_inc(small_in, 16)
                sp.dma_start(qk_scale[:, :, :, :].rearrange("p a l d -> p (a l d)"),
                             w["qk_scale"].partition_broadcast(P)).then_inc(small_in, 16)

                def load_wqkv(layer, kind):
                    a = "qkv".index(kind)
                    src = w_split[layer * 3 + a, :, :] if isinstance(layer, int) \
                        else w_split[bass.ds(layer * 3 + a, 1), :, :].rearrange("l p n -> p (l n)")
                    sp.dma_start(wqkv[:, a, :, :].bitcast(F32).rearrange("p a n -> p (a n)"), src)\
                      .then_inc(wqkv_in[kind], 16)

                def one(name, layer):
                    return w[name][layer, :, :] if isinstance(layer, int) else w[name][bass.ds(layer, 1), :, :]

                def load_wo(layer):
                    src = one("wo", layer)
                    src = src.rearrange("(c p) n -> p c n", p=P) if isinstance(layer, int) else src.rearrange("l (c p) n -> p (l c) n", p=P)
                    sp.dma_start(wo[:, :, :], src).then_inc(wo_in, 16)

                def load_w12(layer):
                    a = one("w1", layer)
                    sp.dma_start(w1[:, :], a if isinstance(layer, int) else a.rearrange("l p n -> p (l n)")).then_inc(w12_in, 16)
                    b = one("w2", layer)
                    b = b if isinstance(layer, int) else b.rearrange("l p n -> (l p) n")
                    full = HID // P
                    sp.dma_start(w2[:, 0:full, :], b[0:full * P, :].rearrange("(c p) n -> p c n", p=P)).then_inc(w12_in, 16)
                    sp.dma_start(w2[0:HID - full * P, full, :], b[full * P:HID, :]).then_inc(w12_in, 16)

                def spread_v(u, t):
                    par = t % 2
                    sp.wait_ge(taken["v"], tiles_done(u, 0, t))
                    sp.wait_ge(ready["o"], tiles_done(u, 0, t))
                    for a in range(2) if t else ():
                        cols = slice(a * INNER // 2, (a + 1) * INNER // 2)
                        sp.dma_start(v_bd[a * 2 * WIN:a * 2 * WIN + WIN, par, 0, a, :],
                                     v_tok[P - WIN:P, 1 - par, cols]).then_inc(carry_in[par], 16)
                    for a in range(2):
                        rows = slice(a * 2 * WIN, (a + 1) * 2 * WIN)
                        cols = slice(a * INNER // 2, (a + 1) * INNER // 2)
                        for g in range(1, WPT):
                            sp.dma_start(v_bd[rows, par, g, a, :], v_tok[(g - 1) * WIN:(g + 1) * WIN, par, cols])\
                              .then_inc(vbd_in[par], 16)
                        sp.dma_start(v_bd[a * 2 * WIN + WIN:(a + 1) * 2 * WIN, par, 0, a, :], v_tok[0:WIN, par, cols])\
                          .then_inc(vbd_in[par], 16)

                def unit(u, layer=None, what=None):
                    for t in range(TILES):
                        if what == "wo" and t == 2:
                            sp.wait_ge(ready["z"], tiles_done(u, -1, TILES - 1))
                            sp.wait_ge(small_in, 80)
                            load_wo(layer)
                        if what == "w12" and t == 3:
                            sp.wait_ge(ready["y"], units_done(u, -2))
                            sp.wait_ge(small_in, 80)
                            load_w12(layer)
                        if what == "wqkv" and t == TILES - 1:
                            for kind in "qk":
                                sp.wait_ge(ready[kind], tiles_done(u, 0, t))
                                load_wqkv(layer + 1, kind)
                        spread_v(u, t)
                    if what == "wqkv":
                        load_wqkv(layer + 1, "v")

                def layer_loads(layer, first, last):
                    u0 = layer * BATCH
                    unit(u0, layer, None if first else "wo")
                    unit(u0 + 1, layer, None if first else "w12")
                    with sp.Fori(2, BATCH - 1) as b:
                        unit(u0 + b)
                    unit(u0 + (BATCH - 1), layer, None if last else "wqkv")

                for kind in "qkv":
                    load_wqkv(0, kind)
                load_wo(0)
                load_w12(0)
                layer_loads(0, True, False)
                if LAYERS > 2:
                    with sp.Fori(1, LAYERS - 1) as layer:
                        layer_loads(layer, False, False)
                layer_loads(LAYERS - 1, False, True)

            @block.tensor
            def _(pe):
                pe.wait_ge(zeroed, 2)
                pe.sem_inc(ready["o"], 2)

                def unit(u):
                    for t in range(TILES):
                        at = STARTS[t]

                        for i, ((kind, d, index), _) in enumerate(jobs_of(t)):
                            if not alive(u, d):
                                continue
                            slot_free(pe, u, at + i)
                            out = slot_of(kind, d, index)
                            par = index % 2
                            if kind in ("q", "k", "v"):
                                if kind == "q":
                                    pe.wait_ge(xs_ready, tiles_done(u, 0, t))
                                if t == 0:
                                    pe.wait_ge(wqkv_in[kind], layer_of(u, 0) * 16 + 16)
                                for c in range(2):
                                    for n, (x_part, w_part) in enumerate(PASSES):
                                        rhs = wqkv[:, "qkv".index(kind), w_part, :]
                                        if kind == "v":
                                            rhs = rhs.rearrange("p (h a d) -> p a h d", a=2, d=DH)[:, c, :, :]
                                        else:
                                            rhs = rhs[:, c * 512:(c + 1) * 512]
                                        last = pe.matmul(out[:, c * 512:(c + 1) * 512],
                                                         xs[:, x_part, t * P:(t + 1) * P], rhs,
                                                         start=(n == 0), stop=(n == len(PASSES) - 1))
                            elif kind == "z":
                                pe.wait_ge(taken["ot"], tiles_done(u, d, index))
                                pe.wait_ge(wo_in, layer_of(u, d) * 16 + 16)
                                for c in range(IC):
                                    last = pe.matmul(out[:, 0:P], wo[:, c, :], oT[:, c * P:(c + 1) * P],
                                                     start=(c == 0), stop=(c == IC - 1))
                            elif kind in ("tq", "tk"):
                                pe.wait_ge(normed[kind == "tk"], tiles_done(u, d, index))
                                src = qk_rot[:, (kind == "tk") * INNER:(1 + (kind == "tk")) * INNER]
                                for c in range(IC):
                                    last = pe.transpose(out[:, c * P:(c + 1) * P], src[:, c * P:(c + 1) * P], ident)
                            elif kind == "pt":
                                pe.wait_ge(exp_ready, tiles_done(u, d, index))
                                for c in range(IC):
                                    last = pe.transpose(out[:, c * P:(c + 1) * P], s[:, par, c * P:(c + 1) * P], ident)
                            elif kind == "sim":
                                pe.wait_ge(taken["tk"], tiles_done(u, d, index))
                                pe.wait_ge(taken["tq"], tiles_done(u, d, index))
                                for c in range(IC):
                                    for g in range(WPT):
                                        key = index * P + g * WIN
                                        last = pe.matmul(
                                            out[g * WIN:(g + 1) * WIN, c * P:(c + 1) * P],
                                            qT[:, par, c * P + g * WIN:c * P + (g + 1) * WIN],
                                            k_bd[:, c, :, key:key + 2 * WIN], start=True, stop=True)
                            elif kind == "o":
                                pe.wait_ge(taken["pt"], tiles_done(u, d, index))
                                pe.wait_ge(vbd_in[par], spread_count(u, d, index))
                                if index:
                                    pe.wait_ge(carry_in[par], carry_count(u, d, index))
                                for c in range(IC):
                                    for g in range(WPT):
                                        last = pe.matmul(
                                            out[g * WIN:(g + 1) * WIN, c * P:(c + 1) * P],
                                            probT[:, c * P + g * WIN:c * P + (g + 1) * WIN],
                                            v_bd[:, par, g, :, c * DH:(c + 1) * DH], start=True, stop=True)
                            elif kind == "ot":
                                pe.wait_ge(taken["o"], tiles_done(u, d, index))
                                for c in range(IC):
                                    last = pe.transpose(out[:, c * P:(c + 1) * P], o[:, c * P:(c + 1) * P], ident)
                            elif kind == "m1":
                                pe.wait_ge(ff_copied, units_done(u, d))
                                last = pe.matmul(out[:, 0:N], ones_mean, xs2[:, :], start=True, stop=True)
                            elif kind == "m2":
                                pe.wait_ge(ff_squared, units_done(u, d))
                                last = pe.matmul(out[:, 0:N], ones_mean, xc2[:, :], start=True, stop=True)
                            elif kind == "h":
                                rows = min(P, HID - index * P)
                                if index == 0:
                                    pe.wait_ge(ff_xn, units_done(u, d))
                                    pe.wait_ge(w12_in, layer_of(u, d) * 48 + 48)
                                for a in range(2):
                                    last = pe.matmul(out[0:rows, a * 512:a * 512 + N],
                                                     w1[:, a * HID + index * P:a * HID + index * P + rows], xc[:, :],
                                                     start=True, stop=True)
                            elif kind == "y":
                                pe.wait_ge(taken["h"], units_done(u, d, HC, HC - 1))
                                for c in range(HC):
                                    rows = min(P, HID - c * P)
                                    last = pe.matmul(out[:, 0:N], w2[0:rows, c, :], hid[0:rows, c, :],
                                                     start=(c == 0), stop=(c == HC - 1))
                            last.then_inc(ready[kind], 1)

                loop(pe, unit)

            @block.scalar
            def _(act):
                act.preload_act_table_set(EXP_LN_SET)
                act.wait_ge(small_in, 80)
                act.wait_ge(zeroed, 2)

                def unit(u):
                    for t in range(TILES):
                        n = tiles_done(u, 0, t)
                        start = isinstance(u, int)
                        def square(a):
                            act.wait_ge(qk_ready[a], n)
                            if not (start and n < 2):
                                act.wait_ge(rot_done[a], n - 1)
                            act.activation(qk_sq[:, cols_of(a)], slot_of("qk"[a], 0, t), ACT.Square).then_inc(squared[a], 1)

                        def reciprocal_norm(a):
                            act.wait_ge(ss_ready[a], n)
                            if not (start and n < 3):
                                act.wait_ge(normed[a], n - 2)
                            r = rn[:, t % 2, heads_of(a)]
                            act.activation(r, ss[:, t % 2, heads_of(a)], ACT.Ln, scale=SS_SCALE).then_inc(rn_ready[a], 1)
                            act.wait_ge(rn_ready[a], 2 * n - 1)
                            act.activation(r, r, ACT.Exp, bias=rn_shift, scale=-0.5).then_inc(rn_ready[a], 1)

                        d1, t1 = divmod(t - 1, TILES)
                        d2, t2 = divmod(t - 2, TILES)
                        d3, t3 = divmod(t - 3, TILES)
                        if alive(u, 0):
                            square(0)
                        if alive(u, d1):
                            act.wait_ge(ready["tq"], n - 1)
                            if not (start and n < 4):
                                act.wait_ge(ready["sim"], n - 3)
                            act.activation(qT[:, t1 % 2, :], slot_of("tq", d1, t1), ACT.Copy).then_inc(taken["tq"], 1)
                        if alive(u, 0):
                            square(1)
                        if alive(u, d1):
                            act.wait_ge(ready["tk"], n - 1)
                            src = slot_of("tk", d1, t1).rearrange("p (c n) -> p c n", n=P)
                            for a in range(2):
                                rows = slice(a * DH, (a + 1) * DH)
                                last = act.activation(k_bd[rows, :, a, WIN + t1 * P:WIN + (t1 + 1) * P], src[rows, :, :], ACT.Copy)
                            last.then_inc(taken["tk"], 1)
                        if alive(u, d2):
                            act.wait_ge(shifted, n - 2)
                            act.activation(s[:, t2 % 2, :], s[:, t2 % 2, :], ACT.Exp).then_inc(exp_ready, 1)
                        if alive(u, 0):
                            par = t % 2
                            act.wait_ge(ready["v"], n)
                            if t1 and not (start and n < 2):
                                act.wait_ge(carry_in[t1 % 2], carry_count(u, d1, t1))
                            if not (start and n < 3):
                                act.wait_ge(vbd_in[par], spread_count(u, d2, t2))
                            act.activation(v_tok[:, par, :], slot_of("v", 0, t), ACT.Copy).then_inc(taken["v"], 1)
                        if alive(u, 0):
                            reciprocal_norm(0)
                        if alive(u, d3):
                            act.wait_ge(ready["ot"], n - 3)
                            if not (start and n < 5):
                                act.wait_ge(ready["z"], n - 4)
                            act.activation(oT[:, :], slot_of("ot", d3, t3), ACT.Copy).then_inc(taken["ot"], 1)
                        if alive(u, d2):
                            act.wait_ge(ready["pt"], n - 2)
                            if not (start and n < 4):
                                act.wait_ge(ready["o"], n - 1)
                            act.activation(probT[:, :], slot_of("pt", d2, t2), ACT.Copy).then_inc(taken["pt"], 1)
                        if alive(u, 0):
                            reciprocal_norm(1)
                        if t == 3 and alive(u, -1):
                            act.wait_ge(taken["m1"], units_done(u, -1))
                            if alive(u, -2):
                                act.wait_ge(ready["m2"], units_done(u, -2))
                            act.activation(xc2[:, :], xc[:, :], ACT.Square).then_inc(ff_squared, 1)
                        if t == 0 and alive(u, -2):
                            act.wait_ge(taken["m2"], units_done(u, -2))
                            if alive(u, -3):
                                act.wait_ge(ff_xn, units_done(u, -3))
                            act.activation(rstd[:, :], var[:, :], ACT.Ln).then_inc(ff_rstd, 1)
                            act.wait_ge(ff_rstd, units_done(u, -2, 2, 0))
                            act.activation(rstd[:, :], rstd[:, :], ACT.Exp, scale=-0.5).then_inc(ff_rstd, 1)
                        if t == 1 and alive(u, -2):
                            for j in range(HC):
                                rows = min(P, HID - j * P)
                                act.wait_ge(ready["h"], units_done(u, -2, HC, j))
                                if j == 0 and alive(u, -3):
                                    act.wait_ge(ready["y"], units_done(u, -3))
                                gate = slot_of("h", -2, j)[0:rows, 512:512 + N]
                                act.activation(hid[0:rows, j, :], gate, ACT.Gelu,
                                               bias=column(b1, rows, layer_of(u, -2), HC + j)).then_inc(gelu_ready, 1)
                            act.preload_act_table_set(EXP_LN_SET)

                loop(act, unit)

            @block.vector
            def _(dve):
                dve.memset(k_bd[:, :, :, :], 0.0).then_inc(zeroed, 1)
                dve.memset(v_bd[:, :, :, :, :], 0.0).then_inc(zeroed, 1)
                dve.memset(xs[DH:P, :, 0:1].bitcast(F32), 0.0).then_inc(dve_zero, 1)
                dve.memset(xs2[DH:P, 0:1], 0.0).then_inc(dve_zero, 1)
                dve.wait_ge(small_in, 80)
                dve.wait_ge(dve_zero, 2)

                def shift_tile(u, d, t):
                    if t == 0:
                        dve.wait_ge(x_done, units_done(u, d))
                    if alive(u, d - 1):
                        dve.wait_ge(ready["v"], tiles_done(u, d - 1, t))
                    b = batch_of(u, d)
                    low, high = slice(0, DH), slice(DH, P)
                    skip = 0 if t else 1
                    parts = ((low, columns_of(b, t, 0, low), t * P),
                             (high, columns_of(b, t, 1 - skip, high, P - skip), t * P + skip))
                    for rows, x, first in parts:
                        dve.tensor_copy(xs[rows, 0, first:(t + 1) * P], x).then_inc(xs_high, 1)
                    dve.wait_ge(xs_high, units_done(u, d, 2 * TILES, 2 * t + 1))
                    for rows, x, first in parts:
                        last = dve.tensor_tensor(xs[rows, 1, first:(t + 1) * P], x,
                                                 xs[rows, 0, first:(t + 1) * P].bitcast(F32), ALU.subtract)
                    last.then_inc(xs_ready, 1)

                shift_tile(0, 0, 0)

                def unit(u):
                    start = isinstance(u, int)
                    for t in range(TILES):
                        n = tiles_done(u, 0, t)
                        d2, t2 = divmod(t - 2, TILES)
                        if t == 1 and alive(u, -2):
                            dve.wait_ge(ff_rstd, units_done(u, -2, 2, 1))
                            dve.scalar_tensor_tensor(xc[:, :], xc[:, :], column(ln_g, P, layer_of(u, -2)), rstd[:, :],
                                                     ALU.mult, ALU.mult).then_inc(ff_gain, 1)
                        def rotate(a):
                            par, cols, heads = t % 2, cols_of(a), heads_of(a)
                            dve.wait_ge(squared[a], n)
                            if a == 0:
                                dve.wait_ge(rot_table, n)
                            if not (start and n < 2):
                                dve.wait_ge(ready[("tq", "tk")[a]], n - 1)
                            dve.tensor_tensor(
                                qk_rot[:, cols].rearrange("p (h d) -> p h d", d=DH),
                                slot_of("qk"[a], 0, t).rearrange("p (h d) -> p h d", d=DH),
                                rot[:, t, 0, a * DH:(a + 1) * DH].unsqueeze(1).to_broadcast([P, HEADS, DH]), ALU.mult)
                            if not (start and n < 3):
                                dve.wait_ge(normed[a], n - 2)
                            dve.tensor_reduce(nt[:, 2 + par, heads], qk_sq[:, cols].rearrange("p (h d) -> p h d", d=DH),
                                              AX.X, ALU.add).then_inc(ss_sum[a], 1)
                            dve.wait_ge(ss_sum[a], n)
                            dve.tensor_scalar(ss[:, par, heads], nt[:, 2 + par, heads], NORM_FLOOR, None, ALU.max)\
                               .then_inc(ss_ready[a], 1)
                            src = slot_of("qk"[a], 0, t).rearrange("p (h g d) -> p h g d", h=HEADS, g=2)
                            dst = qk_sq[:, cols].rearrange("p (h g d) -> p h g d", h=HEADS, g=2)
                            for g in range(2):
                                table = rot[:, t, 1, a * DH + g * (DH // 2):a * DH + (g + 1) * (DH // 2)]
                                last = dve.tensor_tensor(dst[:, :, g, :], src[:, :, 1 - g, :],
                                                         table.unsqueeze(1).to_broadcast([P, HEADS, DH // 2]), ALU.mult)
                            last.then_inc(rot_read[a], 1)

                        if alive(u, 0):
                            rotate(0)
                            rotate(1)
                        dn, tn = divmod(t + 1, TILES)
                        if alive(u, dn):
                            shift_tile(u, dn, tn)
                        d1, t1 = divmod(t - 1, TILES)
                        if alive(u, d1):
                            par = t1 % 2
                            dve.wait_ge(ready["sim"], n - 1)
                            if not (start and n < 4):
                                dve.wait_ge(ready["pt"], n - 3)
                            scores = s[:, par, :].rearrange("p (h k) -> p h k", h=HEADS)
                            dve.tensor_tensor(scores, slot_of("sim", d1, t1).rearrange("p (h k) -> p h k", h=HEADS),
                                              mask[0 if t1 == 0 else 1].unsqueeze(1).to_broadcast([P, HEADS, 2 * WIN]),
                                              ALU.add).then_inc(taken["sim"], 1)
                            dve.wait_ge(taken["sim"], n - 1)
                            dve.tensor_reduce(mx[:, par, :], scores, AX.X, ALU.max).then_inc(max_ready, 1)
                        if t == 3 and alive(u, -1):
                            dve.wait_ge(ready["m1"], units_done(u, -1))
                            if alive(u, -2):
                                dve.wait_ge(ready["h"], units_done(u, -2, HC, HC - 1))
                            dve.tensor_tensor(xc[:, :], xs2[:, :], slot_of("m1", -1, 0)[:, 0:N],
                                              ALU.subtract).then_inc(taken["m1"], 1)
                        if t == 0 and alive(u, -2):
                            dve.wait_ge(ready["m2"], units_done(u, -2))
                            dve.tensor_scalar(var[:, :], slot_of("m2", -2, 0)[:, 0:N], LN_EPS, None,
                                              ALU.add).then_inc(taken["m2"], 1)
                        if t == 2 and alive(u, -2):
                            dve.wait_ge(ready["y"], units_done(u, -2))
                            x = columns_of(batch_of(u, -2), 0, 0, slice(0, P), N)
                            dve.scalar_tensor_tensor(x, slot_of("y", -2, 0)[:, 0:N], column(b2, P, layer_of(u, -2)), x,
                                                     ALU.add, ALU.add).then_inc(taken["y"], 1)
                            dve.wait_ge(taken["y"], units_done(u, -2))
                            dve.sem_inc(x_done, 1)
                        if t == 1 and alive(u, -2):
                            dve.wait_ge(ff_newton, units_done(u, -2, 4, 3))
                            dve.tensor_scalar(xc[:, :], xc[:, :], 0.5, column(ln_b, P, layer_of(u, -2)), ALU.mult,
                                              ALU.add).then_inc(ff_xn, 1)
                        d3, t3 = divmod(t - 3, TILES)
                        if alive(u, d3):
                            dve.wait_ge(ready["z"], n - 3)
                            x = columns_of(batch_of(u, d3), t3)
                            dve.tensor_tensor(x, slot_of("z", d3, t3)[:, 0:P], x, ALU.add).then_inc(taken["z"], 1)
                        if t == 2 and alive(u, -1):
                            dve.wait_ge(taken["z"], tiles_done(u, -1, TILES - 1))
                            if alive(u, -2):
                                dve.wait_ge(ready["m1"], units_done(u, -2))
                            b = batch_of(u, -1)
                            dve.tensor_copy(xs2[0:DH, :], columns_of(b, 0, 0, slice(0, DH), N))
                            dve.tensor_copy(xs2[DH:P, 1:N], columns_of(b, 0, 0, slice(DH, P), N - 1)).then_inc(ff_copied, 1)
                        if alive(u, d2):
                            dve.wait_ge(exp_ready, n - 2)
                            dve.tensor_reduce(den[:, t2 % 2, 0, :], s[:, t2 % 2, :].rearrange("p (h k) -> p h k", h=HEADS),
                                              AX.X, ALU.add).then_inc(den_ready, 1)
                            dve.wait_ge(den_ready, 2 * (n - 2) - 1)
                            dve.reciprocal(den[:, t2 % 2, 1, :], den[:, t2 % 2, 0, :]).then_inc(den_ready, 1)
                        if alive(u, d2):
                            dve.wait_ge(ready["o"], n)
                            dve.wait_ge(den_ready, 2 * (n - 2))
                            if not (start and n < 4):
                                dve.wait_ge(ready["ot"], n - 3)
                            dve.tensor_tensor(
                                o[:, :].rearrange("p (h d) -> p h d", h=HEADS),
                                slot_of("o", d2, t2).rearrange("p (h d) -> p h d", h=HEADS),
                                den[:, t2 % 2, 1, :].unsqueeze(2).to_broadcast([P, HEADS, DH]),
                                ALU.mult).then_inc(taken["o"], 1)
                        if t == 1 and alive(u, -2):
                            for j in range(HC):
                                rows = min(P, HID - j * P)
                                dve.wait_ge(gelu_ready, units_done(u, -2, HC, j))
                                dve.scalar_tensor_tensor(hid[0:rows, j, :], slot_of("h", -2, j)[0:rows, 0:N],
                                                         column(b1, rows, layer_of(u, -2), j), hid[0:rows, j, :],
                                                         ALU.add, ALU.mult).then_inc(taken["h"], 1)

                loop(dve, unit)

            @block.gpsimd
            def _(pool):
                pool.wait_ge(small_in, 80)

                def rot_tables(u, d, t):
                    layer = layer_of(u, d)
                    for part in range(2):
                        scale = qk_scale[:, part, layer, :] if isinstance(layer, int) \
                            else qk_scale[:, part, bass.ds(layer, 1), :].rearrange("p l d -> p (l d)")
                        last = pool.tensor_tensor(rot[:, t, part, :], rot_base[t][part], scale, ALU.mult)
                    last.then_inc(rot_table, 1)

                rot_tables(0, 0, 0)

                def unit(u):
                    start = isinstance(u, int)
                    for t in range(TILES):
                        n = tiles_done(u, 0, t)
                        def normalise(a):
                            par, cols = t % 2, cols_of(a)
                            pool.wait_ge(rot_read[a], n)
                            pool.tensor_tensor(qk_rot[:, cols], qk_rot[:, cols], qk_sq[:, cols], ALU.add).then_inc(rot_done[a], 1)
                            pool.wait_ge(rn_ready[a], 2 * n)
                            r, q, w_ = (x[:, par, heads_of(a)] for x in (rn, ss, nt))
                            chain = 6 * n - 6 + 3 * a
                            pool.tensor_tensor(w_, r, r, ALU.mult).then_inc(pool_own, 1)
                            pool.wait_ge(pool_own, chain + 1)
                            pool.tensor_tensor(w_, w_, q, ALU.mult).then_inc(pool_own, 1)
                            pool.wait_ge(pool_own, chain + 2)
                            pool.tensor_tensor(w_, three[:, 0:HEADS], w_, ALU.subtract).then_inc(pool_own, 1)
                            pool.wait_ge(pool_own, chain + 3)
                            pool.tensor_tensor(r, r, w_, ALU.mult).then_inc(rn_final[a], 1)
                            pool.wait_ge(rn_final[a], n)
                            view = qk_rot[:, cols].rearrange("p (h d) -> p h d", d=DH)
                            pool.tensor_tensor(view, view, r.unsqueeze(2).to_broadcast([P, HEADS, DH]),
                                               ALU.mult).then_inc(normed[a], 1)

                        if t == 1 and alive(u, -2):
                            chain = units_done(u, -2, 4, 0)
                            pool.wait_ge(ff_rstd, units_done(u, -2, 2, 1))
                            pool.tensor_tensor(xc2[:, :], rstd[:, :], rstd[:, :], ALU.mult).then_inc(ff_newton, 1)
                            pool.wait_ge(ff_newton, chain)
                            pool.tensor_tensor(xc2[:, :], xc2[:, :], var[:, :], ALU.mult).then_inc(ff_newton, 1)
                            pool.wait_ge(ff_newton, chain + 1)
                            pool.tensor_tensor(xc2[:, :], three[:, 0:1].to_broadcast([P, N]), xc2[:, :], ALU.subtract)\
                                .then_inc(ff_newton, 1)
                            pool.wait_ge(ff_newton, chain + 2)
                            pool.wait_ge(ff_gain, units_done(u, -2))
                            pool.tensor_tensor(xc[:, :], xc[:, :], xc2[:, :], ALU.mult).then_inc(ff_newton, 1)
                        if alive(u, 0):
                            normalise(0)
                            normalise(1)
                        dn, tn = divmod(t + 1, TILES)
                        if alive(u, dn):
                            rot_tables(u, dn, tn)
                        d, tt = divmod(t - 1, TILES)
                        if alive(u, d):
                            pool.wait_ge(max_ready, n - 1)
                            scores = s[:, tt % 2, :].rearrange("p (h k) -> p h k", h=HEADS)
                            pool.tensor_tensor(scores, scores, mx[:, tt % 2, :].unsqueeze(2).to_broadcast([P, HEADS, 2 * WIN]),
                                               ALU.subtract).then_inc(shifted, 1)

                loop(pool, unit)
AH = 16
AD = DIM // AH
ATT_EPS = 1e-8
GROUP = 4
GROUPS = AH // GROUP
GP = P // GROUP
SCORE_BANKS = 4
ROW_AT = [i * (i + 1) // 2 * P for i in range(TILES)]
ROWS_END = TILES * (TILES + 1) // 2 * P
KEY_AT = {0: 0, 1: 512, 3: 896, 2: 1024}
PROB_BUFS, PROBT_BUFS = 4, 8
SPLIT_STEPS = (2, 9, 13)


def modulated_attention(nc, w, const_sb, mod, xT, x_done, x1_dram, w_split):
    ident, ones_mean, causal, head, low_q, low_k, one = (
        const_sb[k] for k in ("ident", "ones_mean", "causal", "head", "low_q", "low_k", "one"))
    SA, CA, GA, SB, CB, GB = range(6)

    def alive(b, d):
        return not isinstance(b, int) or 0 <= b + d < BATCH

    def head_of(s, back):
        return divmod(s - back, AH)

    def count(b, d, per, index):
        return b * per + (per * d + index + 1)

    with ExitStack() as ctx:
        def sb(name, shape, dtype=F32):
            return ctx.enter_context(nc.sbuf_tensor("at_" + name, shape, dtype))

        def sem(name):
            return ctx.enter_context(nc.semaphore("at_" + name))

        def bank(name, n=1):
            return ctx.enter_context(nc.psum_tensor("at_" + name, [P, n * 512], F32))

        cT = sb("cT", [P, BATCH])
        silu = sb("silu", [P, 2, BATCH])
        sign = sb("sign", [P, BATCH])
        wmod = sb("wmod", [P, 6 * DIM])
        wqk = sb("wqk", [P, 2, GROUPS, P])
        wv = sb("wv", [P, P])
        wo = sb("wo", [P, GROUPS, P])
        x_tok = sb("x_tok", [P, TILES, P])
        xr = sb("xr", [P, N])
        x1 = sb("x1", [P, N])
        xc, sq, var, rstd = (sb(k, [P, 2, N]) for k in ("xc", "sq", "var", "rstd"))
        hT = sb("hT", [P, N])
        q_full = sb("q_full", [P, N])
        high = sb("high", [P, N], F32R)
        q4, k4 = sb("q4", [P, 2, N], F32R), sb("k4", [P, 2, N], F32R)
        qm = sb("qm", [P, 2, N], F32R)
        v_pad = sb("v_pad", [P, TILES, AH, GP])
        probs = sb("probs", [P, PROB_BUFS, ROWS_END])
        probT = sb("probT", [P, PROBT_BUFS, ROWS_END])
        nmx = sb("nmx", [P, 2, TILES])
        den = sb("den", [P, 2, TILES])
        rden = sb("rden", [P, 2, 2, TILES])
        aT = sb("aT", [P, GROUPS, N])
        w_raw = sb("w_raw", [P, INNER])
        w_parts = sb("w_parts", [P, 2, INNER], F32R)

        ps_score = [bank(f"score{i}") for i in range(SCORE_BANKS)]
        ps_t = bank("t", 3)
        ps_m = bank("m")

        w_in, x_in, x1_out = sem("w_in"), sem("x_in"), sem("x1_out")
        raw_in, high_done, split_done, parts_out = (
            sem(k) for k in ("raw_in", "high_done", "split_done", "parts_out"))
        exp_c, silu_ready, mod_ready, mod_taken, mod_done = (
            sem(k) for k in ("exp_c", "silu_ready", "mod_ready", "mod_taken", "mod_done"))
        zeroed = sem("zeroed")
        squared, root, newton = ([sem(f"{k}_{i}") for i in range(2)] for k in ("squared", "root", "newton"))
        q_scaled, high_ready = sem("q_scaled"), sem("high_ready")
        qm_ready, scores_ready, masked, max_ready, exp_ready = (
            sem(k) for k in ("qm_ready", "scores_ready", "masked", "max_ready", "exp_ready"))
        rden_own, weights_ready = (
            sem(k) for k in ("rden_own", "weights_ready"))
        t_ready, t_copied = [sem("t_ready_0"), sem("t_ready_1")], [sem("t_copied_0"), sem("t_copied_1")]

        M_JOBS = [(0, 0, "round", -1, 2), (1, 0, "q", 0, 1), (2, 0, "k", 0, 1), (3, 0, "x", 1, 0),
                  (4, 0, "round", -1, 3), (5, 0, "q", 0, 2), (5, 1, "v", 0, 0), (6, 0, "wo", -1, 0),
                  (6, 1, "mean0", 1, 0), (7, 0, "k", 0, 2), (8, 0, "round", 0, 0), (8, 1, "mean1", -1, 0),
                  (9, 0, "q", 0, 3), (10, 0, "k", 0, 3), (11, 0, "var0", 1, 0), (12, 0, "round", 0, 1),
                  (13, 0, "var1", -1, 0), (14, 0, "q", 1, 0), (15, 0, "k", 1, 0)]
        PER = {"q": GROUPS, "k": GROUPS, "round": GROUPS, "v": 1, "wo": 1, "mean0": 1, "var0": 1, "mean1": 1, "var1": 1, "x": 1}
        ready, taken = ({k: sem(f"{k}_{what}") for k in PER} for what in ("ready", "taken"))
        h_ready, x1_ready = sem("h_ready"), taken["wo"]

        def jobs_at(s, part, *kinds):
            return [(kind, d + s // AH, g) for step, p, kind, d, g in M_JOBS
                    if (step, p) == (s % AH, part) and (not kinds or kind in kinds)]

        def loop(eng, batch):
            batch(-1)
            batch(0)
            with eng.Fori(1, BATCH - 1) as b:
                batch(b)
            batch(BATCH - 1)
            batch(BATCH)

        with nc.Block() as block:
            @block.sync
            def _(sp):
                for dst, src in ((cT[:, :], w["cT"]), (wmod[:, :], w["wmod"]),
                                 (wqk[:, :, :, :].rearrange("p a g n -> p (a g n)"), w["wqk"]),
                                 (wv[:, :], w["wv"]), (wo[:, :, :], w["a_wo"])):
                    sp.dma_start(dst, src).then_inc(w_in, 16)
                sp.dma_start(x_tok[:, :, :], w["x"][0, :, :].rearrange("(t p) d -> p t d", p=P)).then_inc(x_in, 16)

                sp.sem_inc(x1_out, 16)
                sp.sem_inc(parts_out, 16)

                def store(b):
                    sp.wait_ge(x1_ready, b + 1)
                    dst = x1_dram[:, b * N:(b + 1) * N] if isinstance(b, int) else x1_dram[:, bass.ds(b * N, N)]
                    sp.dma_start(dst, x1[:, :]).then_inc(x1_out, 16)

                def load(b):
                    sp.wait_ge(ready["x"], b)
                    src = w["x"][b, :, :].rearrange("(t p) d -> p t d", p=P) if isinstance(b, int) \
                        else w["x"][bass.ds(b, 1), :, :].rearrange("b (t p) d -> p (b t) d", p=P)
                    sp.dma_start(x_tok[:, :, :], src).then_inc(x_in, 16)

                def split_weights(layer, a):
                    sp.wait_ge(split_done, layer * 3 + (a + 1))
                    sp.dma_start(w_raw[:, :], w["wqkv"][bass.ds(layer, 1), :, a * INNER:(a + 1) * INNER]
                                 .rearrange("l p n -> p (l n)")).then_inc(raw_in, 16)
                    sp.wait_ge(split_done, layer * 3 + (a + 2))
                    sp.dma_start(w_split[bass.ds(layer * 3 + a, 1), :, :].rearrange("l p n -> p (l n)"),
                                 w_parts[:, :, :].bitcast(F32).rearrange("p a n -> p (a n)")).then_inc(parts_out, 16)

                load(1)
                with sp.Fori(2, BATCH) as b:
                    load(b)
                    split_weights(b - 2, 0)
                    store(b - 2)
                    split_weights(b - 2, 1)
                    split_weights(b - 2, 2)
                store(BATCH - 2)
                store(BATCH - 1)
                sp.wait_ge(x1_out, 16 * BATCH + 16)
                sp.wait_ge(parts_out, 16 * 3 * DEPTH + 16)

            @block.tensor
            def _(pe):
                pe.wait_ge(w_in, 80)
                pe.wait_ge(silu_ready, 1)
                for j in range(6):
                    last = pe.matmul(ps_m[:, j * BATCH:(j + 1) * BATCH], wmod[:, j * DIM:(j + 1) * DIM], silu[:, 1, :],
                                     start=True, stop=True)
                last.then_inc(mod_ready, 1)
                pe.wait_ge(mod_taken, 1)

                def score(b, h, i):
                    k = h * TILES + i
                    if i == 0:
                        pe.wait_ge(qm_ready, count(b, 0, AH, h))
                        if h % GROUP == 0:
                            pe.wait_ge(taken["k"], count(b, 0, GROUPS, h // GROUP))
                    if not (isinstance(b, int) and b == 0 and h == 0):
                        pe.wait_ge(exp_ready, count(b, 0, AH * TILES, k - SCORE_BANKS))
                    pe.matmul(ps_score[i][:, 0:(i + 1) * P], qm[:, h % 2, i * P:(i + 1) * P],
                              k4[:, h // GROUP % 2, 0:(i + 1) * P], start=True, stop=True).then_inc(scores_ready, 1)

                def transpose(b, d, h, part):
                    if part == 0:
                        pe.wait_ge(weights_ready, count(b, d, AH, h))
                    if not (isinstance(b, int) and b + d == 0 and h == 0):
                        pe.wait_ge(t_copied[part], count(b, d, AH, h - 1))
                    for j in ((0,), (1, 3, 2))[part]:
                        for i in range(j, TILES):
                            at = KEY_AT[j] + (i - j) * P
                            last = pe.transpose(ps_t[:, at:at + P],
                                                probs[:, h % PROB_BUFS, ROW_AT[i] + j * P:ROW_AT[i] + (j + 1) * P], ident)
                    last.then_inc(t_ready[part], 1)

                def m_product(b, job):
                    kind, d, g = job
                    back = [m[2:] for m in M_JOBS].index(job)
                    while True:
                        back -= 1
                        over, i = divmod(back, len(M_JOBS))
                        if isinstance(b, int) and b + over < -1:
                            break
                        kind0, d0, g0 = M_JOBS[i][2:]
                        if alive(b, d0 + over):
                            pe.wait_ge(taken[kind0], count(b, d0 + over, PER[kind0], g0))
                            break
                    if kind == "round":
                        pe.wait_ge(t_copied[1], count(b, d, AH, GROUP * g + GROUP - 1))
                        if g == 0:
                            pe.wait_ge(taken["v"], count(b, d, 1, 0))
                        for j in range(TILES):
                            for c in range(GROUP):
                                h = GROUP * g + c
                                last = pe.matmul(ps_m[c * GP:(c + 1) * GP, j * P:N], v_pad[:, j, h, :],
                                                 probT[:, h % PROBT_BUFS, KEY_AT[j]:KEY_AT[j] + N - j * P],
                                                 start=(j == 0), stop=(j == TILES - 1))
                    elif kind in ("q", "k"):
                        if g == 0 and kind == "q":
                            pe.wait_ge(h_ready, count(b, d, 1, 0))
                        last = pe.matmul(ps_m[:, :], wqk[:, kind == "k", g, :], hT[:, :], start=True, stop=True)
                    elif kind == "v":
                        for t in range(TILES):
                            last = pe.matmul(ps_m[:, t * P:(t + 1) * P], hT[:, t * P:(t + 1) * P], wv[:, :],
                                             start=True, stop=True)
                    elif kind == "wo":
                        pe.wait_ge(taken["round"], count(b, d, GROUPS, GROUPS - 1))
                        for r in range(GROUPS):
                            last = pe.matmul(ps_m[:, :], wo[:, r, :], aT[:, r, :], start=(r == 0), stop=(r == GROUPS - 1))
                    elif kind == "x":
                        pe.wait_ge(x_in, count(b, d, 1, 0) * 16)
                        for t in range(TILES):
                            last = pe.transpose(ps_m[:, t * P:(t + 1) * P], x_tok[:, t, :], ident)
                    elif kind in ("mean0", "mean1"):
                        last = pe.matmul(ps_m[:, :], ones_mean, (xr if kind == "mean0" else x1)[:, :],
                                         start=True, stop=True)
                    else:
                        second = kind == "var1"
                        pe.wait_ge(squared[second], count(b, d, 1, 0))
                        last = pe.matmul(ps_m[:, :], ones_mean, sq[:, second, :], start=True, stop=True)
                    last.then_inc(ready[kind], 1)

                def m_products(b, s, part):
                    for job in jobs_at(s, part):
                        if alive(b, job[1]):
                            m_product(b, job)

                def batch(b):
                    for s in range(AH):
                        dt, ht = head_of(s, 3)
                        for i in range(TILES):
                            if alive(b, 0):
                                score(b, s, i)
                            if i in (1, 2) and alive(b, dt):
                                transpose(b, dt, ht, i - 1)
                            if i == 1:
                                m_products(b, s, 0)
                        m_products(b, s, 1)

                loop(pe, batch)

            @block.scalar
            def _(act):
                act.preload_act_table_set(EXP_LN_SET)
                act.wait_ge(w_in, 80)
                act.activation(silu[:, 0, :], cT[:, :], ACT.Exp, scale=-1.0).then_inc(exp_c, 1)

                def take(b, job):
                    kind, d, g = job
                    if kind in ("q", "k"):
                        act.wait_ge(ready[kind], count(b, d, GROUPS, g))
                        if not (isinstance(b, int) and b + d == 0 and g == 0 and kind == "q"):
                            if kind == "q":
                                act.wait_ge(taken["k"], count(b, d, GROUPS, g - 1))
                            else:
                                act.wait_ge(taken["q"], count(b, d, GROUPS, g))
                        if kind == "q":
                            act.activation(q_full[:, :], ps_m[:, :], ACT.Copy, scale=float(AD) ** -0.5).then_inc(q_scaled, 1)
                            act.wait_ge(q_scaled, count(b, d, GROUPS, g))
                            act.activation(high[:, :], q_full[:, :], ACT.Copy).then_inc(high_ready, 1)
                        else:
                            act.activation(high[:, :], ps_m[:, :], ACT.Copy).then_inc(high_ready, 1)
                    elif kind == "v":
                        act.wait_ge(ready["v"], count(b, d, 1, 0))
                        act.wait_ge(zeroed, 3)
                        if not (isinstance(b, int) and b + d == 0):
                            act.wait_ge(ready["round"], count(b, d, GROUPS, -1))
                        act.activation(v_pad[:, :, :, 0:AD].rearrange("p t h d -> p (t h) d"),
                                       ps_m[:, :].rearrange("p (a d) -> p a d", d=AD), ACT.Copy).then_inc(taken["v"], 1)
                    elif kind in ("mean0", "mean1"):
                        act.wait_ge(taken[kind], count(b, d, 1, 0))
                        second = kind == "mean1"
                        act.activation(sq[:, second, :], xc[:, second, :], ACT.Square).then_inc(squared[second], 1)
                    elif kind in ("var0", "var1"):
                        second = kind == "var1"
                        act.wait_ge(taken[kind], count(b, d, 1, 0))
                        act.activation(rstd[:, second, :], var[:, second, :], ACT.Ln).then_inc(root[second], 1)
                        act.wait_ge(root[second], count(b, d, 2, 0))
                        act.activation(rstd[:, second, :], rstd[:, second, :], ACT.Exp, scale=-0.5).then_inc(root[second], 1)

                def exponentials(b, h, i):
                    act.wait_ge(max_ready, count(b, 0, AH * TILES, h * TILES + i))
                    if i == 0 and not (isinstance(b, int) and b == 0 and h < PROB_BUFS):
                        act.wait_ge(t_ready[1], count(b, 0, AH, h - PROB_BUFS))
                    act.activation(probs[:, h % PROB_BUFS, ROW_AT[i]:ROW_AT[i] + (i + 1) * P],
                                   ps_score[i][:, 0:(i + 1) * P], ACT.Exp, bias=nmx[:, h % 2, i:i + 1],
                                   accum_out=den[:, h % 2, i:i + 1]).then_inc(exp_ready, 1)

                def copy_transposed(b, d, h, part):
                    act.wait_ge(t_ready[part], count(b, d, AH, h))
                    if part == 0 and not (isinstance(b, int) and b + d == 0 and h < PROBT_BUFS):
                        act.wait_ge(ready["round"], count(b, d, GROUPS, (h - PROBT_BUFS) // GROUP))
                    cols = (slice(0, KEY_AT[1]), slice(KEY_AT[1], ROWS_END))[part]
                    act.activation(probT[:, h % PROBT_BUFS, cols], ps_t[:, cols], ACT.Copy).then_inc(t_copied[part], 1)

                def batch(b):
                    for s in range(AH):
                        dt, ht = head_of(s, 3)
                        for i in range(TILES):
                            if alive(b, 0):
                                exponentials(b, s, i)
                            if i in (1, 2) and alive(b, dt):
                                copy_transposed(b, dt, ht, i - 1)
                            took = {0: jobs_at(s - 1, 1, "v") + jobs_at(s, 0, "q", "k"), 1: (),
                                    2: jobs_at(s - 1, 1, "mean0", "mean1"), 3: jobs_at(s, 0, "var0", "var1")}[i]
                            for job in took:
                                if alive(b, job[1]):
                                    take(b, job)

                loop(act, batch)

            @block.vector
            def _(dve):
                dve.memset(v_pad[:, :, :, :], 0.0).then_inc(zeroed, 1)
                dve.wait_ge(exp_c, 1)
                dve.tensor_scalar(silu[:, 0, :], silu[:, 0, :], 1.0, None, ALU.add).then_inc(zeroed, 1)
                dve.wait_ge(zeroed, 2)
                dve.reciprocal(silu[:, 0, :], silu[:, 0, :]).then_inc(zeroed, 1)
                dve.wait_ge(zeroed, 3)
                dve.tensor_tensor(silu[:, 1, :], cT[:, :], silu[:, 0, :], ALU.mult).then_inc(silu_ready, 1)
                dve.wait_ge(mod_ready, 1)
                dve.tensor_copy(mod[:, :, :].rearrange("p j b -> p (j b)"), ps_m[:, 0:6 * BATCH]).then_inc(mod_taken, 1)
                dve.wait_ge(mod_taken, 1)
                step = 0
                for j in (CA, CB):
                    dve.tensor_scalar(mod[:, j, :], mod[:, j, :], 1.0, None, ALU.add).then_inc(mod_done, 1)
                    step += 1
                for j in (GA, GB):
                    g = mod[:, j, :]
                    dve.wait_ge(mod_done, step)
                    dve.tensor_scalar(sign[:, :], g, 0.0, 2.0, ALU.is_ge, ALU.mult).then_inc(mod_done, 1)
                    dve.wait_ge(mod_done, step + 1)
                    dve.tensor_scalar(sign[:, :], sign[:, :], -1.0, None, ALU.add).then_inc(mod_done, 1)
                    dve.wait_ge(mod_done, step + 2)
                    dve.tensor_tensor(g, g, sign[:, :], ALU.mult).then_inc(mod_done, 1)
                    dve.wait_ge(mod_done, step + 3)
                    dve.scalar_tensor_tensor(g, g, 0.25, sign[:, :], ALU.max, ALU.mult).then_inc(mod_done, 1)
                    step += 4
                dve.wait_ge(mod_done, step)

                def modulation(b, d, j):
                    return mod[:, j, b + d:b + d + 1] if isinstance(b, int) else mod[:, j, bass.ds(b + d, 1)]

                def columns_of(b, d):
                    return xT[:, (b + d) * N:(b + d + 1) * N] if isinstance(b, int) else xT[:, bass.ds((b + d) * N, N)]

                def finish_norm(b, d, second):
                    centred, root_, square, variance = (x[:, second, :] for x in (xc, rstd, sq, var))
                    chain = count(b, d, 5, -1)
                    dve.wait_ge(root[second], count(b, d, 2, 1))
                    dve.tensor_tensor(square, root_, root_, ALU.mult).then_inc(newton[second], 1)
                    dve.wait_ge(newton[second], chain + 1)
                    dve.tensor_tensor(square, square, variance, ALU.mult).then_inc(newton[second], 1)
                    dve.scalar_tensor_tensor(centred, centred, modulation(b, d, CB if second else CA), root_,
                                             ALU.mult, ALU.mult)
                    dve.wait_ge(newton[second], chain + 2)
                    dve.tensor_scalar(square, square, -0.5, 1.5, ALU.mult, ALU.add).then_inc(newton[second], 1)
                    dve.wait_ge(newton[second], chain + 3)
                    dve.tensor_tensor(centred, centred, square, ALU.mult).then_inc(newton[second], 1)
                    dve.wait_ge(newton[second], chain + 4)
                    if not second and alive(b, 0):
                        dve.wait_ge(ready["k"], count(b, 0, GROUPS, GROUPS - 1))
                        dve.wait_ge(ready["v"], count(b, 0, 1, 0))
                    dst = columns_of(b, d) if second else hT[:, :]
                    dve.tensor_scalar(dst, centred, modulation(b, d, SB if second else SA), None, ALU.add)\
                       .then_inc(newton[second], 1)
                    dve.wait_ge(newton[second], chain + 5)
                    dve.sem_inc(x_done if second else h_ready, 1)

                def take(b, job):
                    kind, d, g = job
                    if kind == "q":
                        dve.wait_ge(high_ready, count(b, d, 2 * GROUPS, 2 * g))
                        dve.scalar_tensor_tensor(q4[:, g % 2, :], high[:, :].bitcast(F32), low_q, q_full[:, :],
                                                 ALU.mult, ALU.add).then_inc(taken["q"], 1)
                    elif kind == "k":
                        dve.wait_ge(high_ready, count(b, d, 2 * GROUPS, 2 * g + 1))
                        if not (isinstance(b, int) and b + d == 0 and g < 2):
                            dve.wait_ge(scores_ready, count(b, d, AH * TILES, (g - 1) * GROUP * TILES - 1))
                        dve.scalar_tensor_tensor(k4[:, g % 2, :], high[:, :].bitcast(F32), low_k, ps_m[:, :],
                                                 ALU.mult, ALU.add).then_inc(taken["k"], 1)
                    elif kind == "wo":
                        dve.wait_ge(ready["wo"], count(b, d, 1, 0))
                        dve.wait_ge(x1_out, count(b, d, 1, 0) * 16)
                        dve.scalar_tensor_tensor(x1[:, :], ps_m[:, :], modulation(b, d, GA), columns_of(b, d),
                                                 ALU.mult, ALU.add).then_inc(taken["wo"], 1)
                    elif kind == "round":
                        dve.wait_ge(ready["round"], count(b, d, GROUPS, g))
                        if g == 0 and alive(b, d - 1):
                            dve.wait_ge(ready["wo"], count(b, d - 1, 1, 0))
                        dve.tensor_copy(aT[:, g, :], ps_m[:, :]).then_inc(taken["round"], 1)
                    elif kind == "x":
                        dve.wait_ge(ready["x"], count(b, d, 1, 0))
                        dve.tensor_copy(xr[:, :], ps_m[:, :]).then_inc(taken["x"], 1)
                        dve.wait_ge(taken["x"], count(b, d, 1, 0))
                        dve.tensor_copy(columns_of(b, d), xr[:, :])
                    elif kind in ("mean0", "mean1"):
                        if kind == "mean1":
                            dve.wait_ge(taken["wo"], count(b, d, 1, 0))
                        dve.wait_ge(ready[kind], count(b, d, 1, 0))
                        dve.tensor_tensor(xc[:, kind == "mean1", :], (xr if kind == "mean0" else x1)[:, :], ps_m[:, :],
                                          ALU.subtract)\
                           .then_inc(taken[kind], 1)
                    elif kind in ("var0", "var1"):
                        dve.wait_ge(ready[kind], count(b, d, 1, 0))
                        dve.tensor_scalar(var[:, kind == "var1", :], ps_m[:, :], LN_EPS, None, ALU.add).then_inc(taken[kind], 1)

                def pick_head(b, d, h):
                    if h % GROUP == 0:
                        dve.wait_ge(taken["q"], count(b, d, GROUPS, h // GROUP))
                    if not (isinstance(b, int) and b + d == 0 and h < 2):
                        dve.wait_ge(scores_ready, count(b, d, AH * TILES, TILES * (h - 1) - 1))
                    dve.tensor_scalar(qm[:, h % 2, :], q4[:, h // GROUP % 2, :].bitcast(F32),
                                      head[:, h % GROUP:h % GROUP + 1], None, ALU.mult).then_inc(qm_ready, 1)

                def mask(b, d, h, i):
                    dve.wait_ge(scores_ready, count(b, d, AH * TILES, h * TILES + i))
                    diagonal = ps_score[i][:, i * P:(i + 1) * P]
                    dve.tensor_tensor(diagonal, diagonal, causal, ALU.add).then_inc(masked, 1)

                def maximum(b, h, i):
                    dve.wait_ge(masked, count(b, 0, AH * TILES, h * TILES + i))
                    dve.tensor_reduce(nmx[:, h % 2, i:i + 1], ps_score[i][:, 0:(i + 1) * P],
                                      AX.X, ALU.max, negate=True).then_inc(max_ready, 1)

                def reciprocals(b, d, h):
                    dve.wait_ge(exp_ready, count(b, d, AH * TILES, TILES * (h + 1) - 1))
                    if not (isinstance(b, int) and b + d == 0 and h < 2):
                        dve.wait_ge(weights_ready, count(b, d, AH, h - 2))
                    dve.tensor_scalar(rden[:, h % 2, 0, :], den[:, h % 2, :], ATT_EPS, None, ALU.add).then_inc(rden_own, 1)
                    dve.wait_ge(rden_own, count(b, d, 2 * AH, 2 * h))
                    dve.reciprocal(rden[:, h % 2, 1, :], rden[:, h % 2, 0, :]).then_inc(rden_own, 1)

                def batch(b):
                    for s in range(AH):
                        dn, hn = head_of(s, -1)
                        if alive(b, dn):
                            pick_head(b, dn, hn)
                        dr, hr = head_of(s, 1)
                        for i in range(TILES):
                            dm, hm = (0, s) if i < TILES - 1 else (dn, hn)
                            if alive(b, dm):
                                mask(b, dm, hm, (i + 1) % TILES)
                            if alive(b, 0):
                                maximum(b, s, i)
                            if i == 0 and alive(b, dr):
                                reciprocals(b, dr, hr)
                            took = {0: jobs_at(s - 1, 1, "mean0", "mean1"), 1: jobs_at(s, 0, "round", "x", "wo", "var0", "var1"),
                                    2: jobs_at(s, 0, "q", "k")}.get(i, ())
                            for job in took:
                                if alive(b, job[1]):
                                    take(b, job)
                        if s == 12 and alive(b, 1):
                            finish_norm(b, 1, False)
                        if s == 14 and alive(b, -1):
                            finish_norm(b, -1, True)

                loop(dve, batch)

            @block.gpsimd
            def _(pool):
                pool.sem_inc(split_done, 1)
                assert DEPTH == BATCH - 2

                def split(layer, a):
                    pool.wait_ge(raw_in, layer * 48 + (16 * a + 16))
                    pool.wait_ge(parts_out, layer * 48 + (16 * a + 16))
                    pool.tensor_tensor(w_parts[:, 0, :], w_raw[:, :], one.to_broadcast([P, INNER]), ALU.mult).then_inc(high_done, 1)
                    pool.wait_ge(high_done, layer * 3 + (a + 1))
                    pool.tensor_tensor(w_parts[:, 1, :], w_raw[:, :], w_parts[:, 0, :].bitcast(F32), ALU.subtract)\
                        .then_inc(split_done, 1)

                def batch(b):
                    for s in range(AH):
                        if s in SPLIT_STEPS and not isinstance(b, int):
                            split(b - 1, SPLIT_STEPS.index(s))
                        d, h = head_of(s, 1)
                        if not alive(b, d):
                            continue
                        pool.wait_ge(rden_own, count(b, d, 2 * AH, 2 * h + 1))
                        for i in range(TILES):
                            row = probs[:, h % PROB_BUFS, ROW_AT[i]:ROW_AT[i] + (i + 1) * P]
                            last = pool.tensor_tensor(row, row, rden[:, h % 2, 1, i:i + 1].to_broadcast([P, (i + 1) * P]),
                                                      ALU.mult)
                        last.then_inc(weights_ready, 1)

                loop(pool, batch)


def last_residual(nc, const_sb, mod, xT, x1_dram, out):
    ident = const_sb["ident"]
    GB = 5
    with ExitStack() as ctx:
        x1 = ctx.enter_context(nc.sbuf_tensor("lr_x1", [P, BATCH, N], F32))
        y = ctx.enter_context(nc.sbuf_tensor("lr_y", [P, BATCH, N], F32))
        y_tok = ctx.enter_context(nc.sbuf_tensor("lr_y_tok", [P, BATCH, N], F32))
        ps = [ctx.enter_context(nc.psum_tensor(f"lr_ps{i}", [P, N], F32)) for i in range(BATCH)]
        x1_in, y_ready, t_ready, t_taken, stored = (
            ctx.enter_context(nc.semaphore("lr_" + k)) for k in ("x1_in", "y_ready", "t_ready", "t_taken", "stored"))
        with nc.Block() as block:
            @block.sync
            def _(sp):
                sp.dma_start(x1[:, :, :].rearrange("p b n -> p (b n)"), x1_dram[:, :]).then_inc(x1_in, 16)
                for b in range(BATCH):
                    sp.wait_ge(t_taken, b + 1)
                    sp.dma_start(out[b, :, :].rearrange("(t p) d -> p t d", p=P),
                                 y_tok[:, b, :].rearrange("p (t d) -> p t d", d=DIM)).then_inc(stored, 16)
                sp.wait_ge(stored, 16 * BATCH)

            @block.vector
            def _(dve):
                dve.wait_ge(x1_in, 16)
                for b in range(BATCH):
                    dve.scalar_tensor_tensor(y[:, b, :], xT[:, b * N:(b + 1) * N], mod[:, GB, b:b + 1], x1[:, b, :],
                                             ALU.mult, ALU.add).then_inc(y_ready, 1)

            @block.tensor
            def _(pe):
                for b in range(BATCH):
                    pe.wait_ge(y_ready, b + 1)
                    for t in range(TILES):
                        last = pe.transpose(ps[b][:, t * P:(t + 1) * P], y[:, b, t * P:(t + 1) * P], ident)
                    last.then_inc(t_ready, 1)

            @block.scalar
            def _(act):
                for b in range(BATCH):
                    act.wait_ge(t_ready, b + 1)
                    act.activation(y_tok[:, b, :], ps[b][:, :], ACT.Copy).then_inc(t_taken, 1)


def adaln_block(nc, w, out):
    with ExitStack() as ctx:
        consts = ctx.enter_context(nc.sbuf_tensor("consts_sb", [P, C_END], F32))
        xT = ctx.enter_context(nc.sbuf_tensor("xT_sb", [P, BATCH * N], F32))
        mod = ctx.enter_context(nc.sbuf_tensor("mod_sb", [P, 6, BATCH], F32))
        w_split = nc.dram_tensor("wqkv_parts", [DEPTH * 3, P, 2 * INNER], F32, kind="Internal").ap()
        x1_dram = nc.dram_tensor("x1_dims_first", [P, BATCH * N], F32, kind="Internal").ap()
        consts_in = ctx.enter_context(nc.semaphore("consts_in"))
        x_done = ctx.enter_context(nc.semaphore("x_done"))
        with nc.Block() as block:
            @block.sync
            def _(sp):
                sp.dma_start(consts[:, :], w["consts"]).then_inc(consts_in, 16)
                sp.wait_ge(consts_in, 16)
        const_sb = constant_views(consts)
        modulated_attention(nc, w, const_sb, mod, xT, x_done, x1_dram, w_split)
        local_stack(nc, w, DEPTH, const_sb, xT, x_done, w_split)
        last_residual(nc, const_sb, mod, xT, x1_dram, out)


def _layouts(inputs):
    a = {k: np.asarray(v) for k, v in inputs.items()}
    wkv = a["L0_attn_Wkv"]
    a_wo = np.zeros((P, GROUPS, P), np.float32)
    rows = a["L0_attn_Wo"].T.reshape(GROUPS, GROUP, AD, DIM)
    for j in range(GROUP):
        a_wo[j * GP:j * GP + AD] = rows[:, j].transpose(1, 0, 2)
    wqk = np.stack([m.T.reshape(DIM, GROUPS, 1, GP).repeat(GROUP, 2).reshape(DIM, -1) for m in (a["L0_attn_Wq"], wkv[:DIM])], 1)
    b1 = np.zeros((P, DEPTH, 2 * HC), np.float32)
    for half in range(2):
        for j in range(HC):
            n = min(P, HID - j * P)
            b1[:n, :, half * HC + j] = a["L0_ffn_b1"][:, half * HID + j * P:half * HID + j * P + n].T
    q_scale, k_scale = a["L0_ffn_q_scale"], a["L0_ffn_k_scale"]
    swap = [np.concatenate([s[:, DH // 2:], s[:, :DH // 2]], 1) for s in (q_scale, k_scale)]
    qk_scale = np.stack([np.concatenate([q_scale, k_scale], 1), np.concatenate(swap, 1)]).reshape(-1)
    return {
        "consts": shape_constants(),
        "cT": a["L0_c"].T, "wmod": a["L0_wmod"], "x": a["L0_attn_x"],
        "wqk": wqk.reshape(DIM, -1), "wv": wkv[DIM:].T, "a_wo": a_wo,
        "wqkv": a["L0_ffn_Wqkv"], "wo": a["L0_ffn_Wo"], "w1": a["L0_ffn_W1"], "w2": a["L0_ffn_W2"],
        "ln_g": a["L0_ffn_ln_g"].T, "ln_b": a["L0_ffn_ln_b"].T, "b1": b1.reshape(P, -1), "b2": a["L0_ffn_b2"].T,
        "qk_scale": qk_scale,
    }


def kernel(**inputs):
    import concourse.bacc as bacc
    from concourse.bass_utils import run_bass_kernel_spmd

    nc = bacc.Bacc("TRN2", target_bir_lowering=False, num_devices=1)
    arrays, w = {}, {}
    for name, value in _layouts(inputs).items():
        value = np.ascontiguousarray(value)
        arrays["in_" + name] = value
        w[name] = nc.dram_tensor("in_" + name, value.shape, mybir.dt.from_np(value.dtype), kind="ExternalInput").ap()
    out = nc.dram_tensor("out_dram", (BATCH, N, DIM), F32, kind="ExternalOutput").ap()
    adaln_block(nc, w, out)
    result = run_bass_kernel_spmd(nc, [arrays], core_ids=[0])
    return np.asarray(result.results[0]["out_dram"])
```
